# Optimizing a Trainium2 kernel written in Bass

```python
import numpy as np
import jax
import jax.numpy as jnp

def _softmax(x, axis=-1):
    return jax.nn.softmax(x, axis=axis)

def _gelu(x):
    return jax.nn.gelu(x, approximate=True)

def _silu(x):
    return jax.nn.silu(x)

def _sigmoid(x):
    return jax.nn.sigmoid(x)

def _layernorm(x, axis=-1, eps=1e-05):
    m = jnp.mean(x, axis=axis, keepdims=True)
    v = jnp.var(x, axis=axis, keepdims=True)
    return (x - m) / jnp.sqrt(v + eps)

def _scatter_add(tgt, idx, src, axis=0):
    return tgt.at[idx].add(src)

def _segment_sum(src, seg, n):
    return jax.ops.segment_sum(src, seg, n)
kernel_name = 'mk_gnn_preln_d4_gnn_r32_bd4dec'

def setup_inputs(seed: int=0):
    np.random.seed(seed)
    _w = jnp.asarray

    def _rec_inputs():
        import jax
        import jax.numpy as jnp
        _gk = jax.random.key(seed)
        x = -0.000202 + 1 * jax.random.normal(jax.random.fold_in(_gk, 1), (50000, 128), jnp.float32)
        src = jax.random.randint(jax.random.fold_in(_gk, 2), (50000,), 0, 50000, jnp.int32)
        dst = jnp.minimum((50000 * jax.random.uniform(jax.random.fold_in(_gk, 3), (50000,)) ** 2.0).astype(jnp.int32), 49999)
        _o = jnp.argsort(dst, stable=True)
        src = src[_o]
        dst = dst[_o]
        return (x, src, dst)
    x, src, dst = _rec_inputs()

    def _L0_gnn_setup():
        import jax, jax.numpy as jnp
        import numpy as np
        N = 50000
        E = 50000
        D_IN = 128
        D_OUT = 128
        key = jax.random.key(seed)
        k1, k2, k3, k4, k5 = jax.random.split(key, 5)
        x = jax.random.normal(k1, (N, D_IN), dtype=jnp.float32)
        edge_index = jax.random.randint(k2, (2, E), 0, N, dtype=jnp.int64)
        Wl = jax.random.normal(k3, (D_OUT, D_IN), dtype=jnp.float32) / np.sqrt(D_IN)
        bl = jax.random.normal(k4, (D_OUT,), dtype=jnp.float32) * 0.01
        Wr = jax.random.normal(k5, (D_OUT, D_IN), dtype=jnp.float32) / np.sqrt(D_IN)
        return {'x': x, 'edge_index': edge_index, 'Wl': Wl, 'bl': bl, 'Wr': Wr}
    _L0_gnn_all = _L0_gnn_setup()
    _L0_gnn_in = {k: v for k, v in _L0_gnn_all.items() if k in ('Wl', 'bl', 'Wr')}
    del _L0_gnn_all

    def _L1_gnn_setup():
        import jax, jax.numpy as jnp
        import numpy as np
        N_NODES, N_EDGES, N_INC = (50000, 10000, 25000)
        IN_C, HID_C, OUT_C = (128, 128, 128)
        EPS = 1e-05

        def _hconv(x, W, b, node_idx, edge_idx, hw):
            x = x @ W.T
            D = jax.ops.segment_sum(hw[edge_idx], node_idx, num_segments=N_NODES)
            Dinv = jnp.where(D > 0, 1.0 / D, 0.0)
            Bdeg = jax.ops.segment_sum(jnp.ones_like(edge_idx, dtype=x.dtype), edge_idx, num_segments=N_EDGES)
            Binv = jnp.where(Bdeg > 0, 1.0 / Bdeg, 0.0)
            e = jax.ops.segment_sum(Binv[edge_idx][:, None] * x[node_idx], edge_idx, num_segments=N_EDGES)
            out = jax.ops.segment_sum(Dinv[node_idx][:, None] * e[edge_idx], node_idx, num_segments=N_NODES)
            return out + b
        key = jax.random.key(seed)
        ks = jax.random.split(key, 6)
        x = jax.random.normal(ks[0], (N_NODES, IN_C), jnp.float32)
        node_idx = jax.random.randint(ks[1], (N_INC,), 0, N_NODES)
        edge_idx = jax.random.randint(ks[2], (N_INC,), 0, N_EDGES)
        hyperedge_index = jnp.stack([node_idx, edge_idx])
        hyperedge_weight = jnp.ones((N_EDGES,), jnp.float32)
        s1 = 1.0 / np.sqrt(IN_C)
        s2 = 1.0 / np.sqrt(HID_C)
        W1 = jax.random.uniform(ks[3], (HID_C, IN_C), jnp.float32, -s1, s1)
        b1 = jnp.zeros((HID_C,), jnp.float32)
        gamma = jnp.ones((HID_C,), jnp.float32)
        beta = jnp.zeros((HID_C,), jnp.float32)
        W2 = jax.random.uniform(ks[4], (OUT_C, HID_C), jnp.float32, -s2, s2)
        b2 = jnp.zeros((OUT_C,), jnp.float32)
        return dict(x=x, hyperedge_index=hyperedge_index, hyperedge_weight=hyperedge_weight, W1=W1, b1=b1, gamma=gamma, beta=beta, W2=W2, b2=b2)
    _L1_gnn_all = _L1_gnn_setup()
    _L1_gnn_in = {k: v for k, v in _L1_gnn_all.items() if k in ('hyperedge_weight', 'W1', 'b1', 'gamma', 'beta', 'W2', 'b2')}
    del _L1_gnn_all

    def _L2_gnn_setup():
        import jax, jax.numpy as jnp
        import numpy as np
        N = 50000
        E = 50000
        IN = 128
        HID = 128
        OUT = 128
        HEADS = 4
        ALPHA = 0.2
        EPS = 1e-06

        def _head_attention(h, a_h, row, col, scale):
            s_src = h @ a_h[:HID]
            s_dst = h @ a_h[HID:]
            e = s_src[row] + s_dst[col]
            e = jnp.where(e > 0, e, ALPHA * e) / scale
            ee = jnp.exp(e)
            rowsum = jax.ops.segment_sum(ee, row, num_segments=N)
            agg = jax.ops.segment_sum(ee[:, None] * h[col], row, num_segments=N)
            zero = rowsum == 0
            agg = jnp.where(zero[:, None], h, agg)
            denom = jnp.where(zero, 1.0, rowsum)
            return agg / denom[:, None]
        key = jax.random.key(seed)
        ks = jax.random.split(key, 8)
        edge = jax.random.randint(ks[0], (2, E), 0, N, dtype=jnp.int32)
        data = jax.random.normal(ks[1], (N, IN), dtype=jnp.float32)
        W_w = jax.random.normal(ks[2], (HEADS, HID, IN), dtype=jnp.float32) * 0.05
        W_b = jax.random.normal(ks[3], (HEADS, HID), dtype=jnp.float32) * 0.05
        a = jax.random.normal(ks[4], (HEADS, 2 * HID), dtype=jnp.float32) * 0.05
        V_w = jax.random.normal(ks[5], (OUT, HID), dtype=jnp.float32) * 0.05
        V_b = jnp.zeros((OUT,), dtype=jnp.float32)
        ln_g = jnp.ones((HID,), dtype=jnp.float32)
        ln_b = jnp.zeros((HID,), dtype=jnp.float32)
        return {'edge': edge, 'data': data, 'W_w': W_w, 'W_b': W_b, 'a': a, 'V_w': V_w, 'V_b': V_b, 'ln_g': ln_g, 'ln_b': ln_b}
    _L2_gnn_all = _L2_gnn_setup()
    _L2_gnn_in = {k: v for k, v in _L2_gnn_all.items() if k in ('W_w', 'W_b', 'a', 'V_w', 'V_b', 'ln_g', 'ln_b')}
    del _L2_gnn_all

    def _L3_gnn_setup():
        import jax, jax.numpy as jnp
        import numpy as np
        N_AGT = 50000
        N_CTX = 3125
        N_EDGE = 18750
        D = 128
        N_BLK = 2
        EPS_GN = 1e-05

        def group_norm(x, w, b):
            mu = jnp.mean(x, axis=1, keepdims=True)
            var = jnp.var(x, axis=1, keepdims=True)
            return (x - mu) * jax.lax.rsqrt(var + EPS_GN) * w + b

        def _graph_att(agt, ctx, u, v, Wq, Wk, Wctx, gnc_w, gnc_b, Wagt, gna_w, gna_b, norm_w, norm_b, Wlin, gnl_w, gnl_b):
            res = agt
            q = (agt @ Wq.T)[v]
            k = (ctx @ Wk.T)[u]
            c = jnp.sum(q * k, axis=1)
            c = jnp.where(c >= 0, c, 0.1 * c)
            c = jnp.exp(c - jnp.max(c))
            c_sum = jax.ops.segment_sum(c, v, num_segments=agt.shape[0])
            c = c / (c_sum[v] + 1e-16)
            ctx_p = group_norm(ctx @ Wctx.T, gnc_w, gnc_b)
            msg = ctx_p[u] * c[:, None]
            agg = jax.ops.segment_sum(msg, v, num_segments=agt.shape[0])
            x = group_norm(jnp.concatenate([agt, agg], axis=1) @ Wagt.T, gna_w, gna_b)
            x = group_norm(x, norm_w, norm_b)
            x = jax.nn.relu(x)
            x = group_norm(x @ Wlin.T, gnl_w, gnl_b)
            return jax.nn.relu(x + res)
        key = jax.random.key(seed)
        ks = jax.random.split(key, 20)
        s = 1.0 / np.sqrt(D)
        inp = {'agt': jax.random.normal(ks[0], (N_AGT, D), jnp.float32), 'ctx': jax.random.normal(ks[1], (N_CTX, D), jnp.float32), 'u': jax.random.randint(ks[2], (N_EDGE,), 0, N_CTX), 'v': jax.random.randint(ks[3], (N_EDGE,), 0, N_AGT), 'Wq': jax.random.normal(ks[4], (N_BLK, D, D), jnp.float32) * s, 'Wk': jax.random.normal(ks[5], (N_BLK, D, D), jnp.float32) * s, 'Wctx': jax.random.normal(ks[6], (N_BLK, D, D), jnp.float32) * s, 'gnc_w': jnp.ones((N_BLK, D), jnp.float32), 'gnc_b': jnp.zeros((N_BLK, D), jnp.float32), 'Wagt': jax.random.normal(ks[7], (N_BLK, D, 2 * D), jnp.float32) * (1.0 / np.sqrt(2 * D)), 'gna_w': jnp.ones((N_BLK, D), jnp.float32), 'gna_b': jnp.zeros((N_BLK, D), jnp.float32), 'norm_w': jnp.ones((N_BLK, D), jnp.float32), 'norm_b': jnp.zeros((N_BLK, D), jnp.float32), 'Wlin': jax.random.normal(ks[8], (N_BLK, D, D), jnp.float32) * s, 'gnl_w': jnp.ones((N_BLK, D), jnp.float32), 'gnl_b': jnp.zeros((N_BLK, D), jnp.float32)}
        return inp
    _L3_gnn_all = _L3_gnn_setup()
    _L3_gnn_in = {k: v for k, v in _L3_gnn_all.items() if k in ('ctx', 'Wq', 'Wk', 'Wctx', 'gnc_w', 'gnc_b', 'Wagt', 'gna_w', 'gna_b', 'norm_w', 'norm_b', 'Wlin', 'gnl_w', 'gnl_b')}
    del _L3_gnn_all
    return {'x': x, 'src': src, 'dst': dst, 'L0_gnn_Wl': _L0_gnn_in['Wl'], 'L0_gnn_bl': _L0_gnn_in['bl'], 'L0_gnn_Wr': _L0_gnn_in['Wr'], 'L1_gnn_hyperedge_weight': _L1_gnn_in['hyperedge_weight'], 'L1_gnn_W1': _L1_gnn_in['W1'], 'L1_gnn_b1': _L1_gnn_in['b1'], 'L1_gnn_gamma': _L1_gnn_in['gamma'], 'L1_gnn_beta': _L1_gnn_in['beta'], 'L1_gnn_W2': _L1_gnn_in['W2'], 'L1_gnn_b2': _L1_gnn_in['b2'], 'L2_gnn_W_w': _L2_gnn_in['W_w'], 'L2_gnn_W_b': _L2_gnn_in['W_b'], 'L2_gnn_a': _L2_gnn_in['a'], 'L2_gnn_V_w': _L2_gnn_in['V_w'], 'L2_gnn_V_b': _L2_gnn_in['V_b'], 'L2_gnn_ln_g': _L2_gnn_in['ln_g'], 'L2_gnn_ln_b': _L2_gnn_in['ln_b'], 'L3_gnn_ctx': _L3_gnn_in['ctx'], 'L3_gnn_Wq': _L3_gnn_in['Wq'], 'L3_gnn_Wk': _L3_gnn_in['Wk'], 'L3_gnn_Wctx': _L3_gnn_in['Wctx'], 'L3_gnn_gnc_w': _L3_gnn_in['gnc_w'], 'L3_gnn_gnc_b': _L3_gnn_in['gnc_b'], 'L3_gnn_Wagt': _L3_gnn_in['Wagt'], 'L3_gnn_gna_w': _L3_gnn_in['gna_w'], 'L3_gnn_gna_b': _L3_gnn_in['gna_b'], 'L3_gnn_norm_w': _L3_gnn_in['norm_w'], 'L3_gnn_norm_b': _L3_gnn_in['norm_b'], 'L3_gnn_Wlin': _L3_gnn_in['Wlin'], 'L3_gnn_gnl_w': _L3_gnn_in['gnl_w'], 'L3_gnn_gnl_b': _L3_gnn_in['gnl_b']}

def reference(x, src, dst, L0_gnn_Wl, L0_gnn_bl, L0_gnn_Wr, L1_gnn_hyperedge_weight, L1_gnn_W1, L1_gnn_b1, L1_gnn_gamma, L1_gnn_beta, L1_gnn_W2, L1_gnn_b2, L2_gnn_W_w, L2_gnn_W_b, L2_gnn_a, L2_gnn_V_w, L2_gnn_V_b, L2_gnn_ln_g, L2_gnn_ln_b, L3_gnn_ctx, L3_gnn_Wq, L3_gnn_Wk, L3_gnn_Wctx, L3_gnn_gnc_w, L3_gnn_gnc_b, L3_gnn_Wagt, L3_gnn_gna_w, L3_gnn_gna_b, L3_gnn_norm_w, L3_gnn_norm_b, L3_gnn_Wlin, L3_gnn_gnl_w, L3_gnn_gnl_b):
    import jax
    import jax.numpy as jnp

    def _L0_gnn_ref(x, edge_index, Wl, bl, Wr):
        import jax, jax.numpy as jnp
        import numpy as np
        N = 50000
        E = 50000
        D_IN = 128
        D_OUT = 128
        src = edge_index[0]
        dst = edge_index[1]
        msg = x[src] - x[dst]
        agg_sum = jax.ops.segment_sum(msg, dst, num_segments=N)
        cnt = jax.ops.segment_sum(jnp.ones((msg.shape[0],), dtype=x.dtype), dst, num_segments=N)
        agg = agg_sum / jnp.maximum(cnt, 1.0)[:, None]
        out = jnp.einsum('nd,od->no', agg, Wl) + bl + jnp.einsum('nd,od->no', x, Wr)
        return out

    def _L1_gnn_ref(x, hyperedge_index, hyperedge_weight, W1, b1, gamma, beta, W2, b2):
        import jax, jax.numpy as jnp
        import numpy as np
        N_NODES, N_EDGES, N_INC = (50000, 10000, 25000)
        IN_C, HID_C, OUT_C = (128, 128, 128)
        EPS = 1e-05

        def _hconv(x, W, b, node_idx, edge_idx, hw):
            x = x @ W.T
            D = jax.ops.segment_sum(hw[edge_idx], node_idx, num_segments=N_NODES)
            Dinv = jnp.where(D > 0, 1.0 / D, 0.0)
            Bdeg = jax.ops.segment_sum(jnp.ones_like(edge_idx, dtype=x.dtype), edge_idx, num_segments=N_EDGES)
            Binv = jnp.where(Bdeg > 0, 1.0 / Bdeg, 0.0)
            e = jax.ops.segment_sum(Binv[edge_idx][:, None] * x[node_idx], edge_idx, num_segments=N_EDGES)
            out = jax.ops.segment_sum(Dinv[node_idx][:, None] * e[edge_idx], node_idx, num_segments=N_NODES)
            return out + b
        node_idx, edge_idx = (hyperedge_index[0], hyperedge_index[1])
        h = _hconv(x, W1, b1, node_idx, edge_idx, hyperedge_weight)
        mu = h.mean(axis=0)
        var = h.var(axis=0)
        h = gamma * (h - mu) * jax.lax.rsqrt(var + EPS) + beta
        return _hconv(h, W2, b2, node_idx, edge_idx, hyperedge_weight)

    def _L2_gnn_ref(edge, data, W_w, W_b, a, V_w, V_b, ln_g, ln_b):
        import jax, jax.numpy as jnp
        import numpy as np
        N = 50000
        E = 50000
        IN = 128
        HID = 128
        OUT = 128
        HEADS = 4
        ALPHA = 0.2
        EPS = 1e-06

        def _head_attention(h, a_h, row, col, scale):
            s_src = h @ a_h[:HID]
            s_dst = h @ a_h[HID:]
            e = s_src[row] + s_dst[col]
            e = jnp.where(e > 0, e, ALPHA * e) / scale
            ee = jnp.exp(e)
            rowsum = jax.ops.segment_sum(ee, row, num_segments=N)
            agg = jax.ops.segment_sum(ee[:, None] * h[col], row, num_segments=N)
            zero = rowsum == 0
            agg = jnp.where(zero[:, None], h, agg)
            denom = jnp.where(zero, 1.0, rowsum)
            return agg / denom[:, None]
        row, col = (edge[0], edge[1])
        scale = jnp.sqrt(jnp.float32(HID * HEADS))
        heads = []
        for hd in range(HEADS):
            h = data @ W_w[hd].T + W_b[hd]
            heads.append(_head_attention(h, a[hd], row, col, scale))
        h_prime = jnp.stack(heads, axis=0).mean(axis=0)
        mean = h_prime.mean(-1, keepdims=True)
        std = h_prime.std(-1, keepdims=True, ddof=1)
        x = ln_g * (h_prime - mean) / (std + EPS) + ln_b
        return jax.nn.relu(x) @ V_w.T + V_b

    def _L3_gnn_ref(agt, ctx, u, v, Wq, Wk, Wctx, gnc_w, gnc_b, Wagt, gna_w, gna_b, norm_w, norm_b, Wlin, gnl_w, gnl_b):
        import jax, jax.numpy as jnp
        import numpy as np
        N_AGT = 50000
        N_CTX = 3125
        N_EDGE = 18750
        D = 128
        N_BLK = 2
        EPS_GN = 1e-05

        def group_norm(x, w, b):
            mu = jnp.mean(x, axis=1, keepdims=True)
            var = jnp.var(x, axis=1, keepdims=True)
            return (x - mu) * jax.lax.rsqrt(var + EPS_GN) * w + b

        def _graph_att(agt, ctx, u, v, Wq, Wk, Wctx, gnc_w, gnc_b, Wagt, gna_w, gna_b, norm_w, norm_b, Wlin, gnl_w, gnl_b):
            res = agt
            q = (agt @ Wq.T)[v]
            k = (ctx @ Wk.T)[u]
            c = jnp.sum(q * k, axis=1)
            c = jnp.where(c >= 0, c, 0.1 * c)
            c = jnp.exp(c - jnp.max(c))
            c_sum = jax.ops.segment_sum(c, v, num_segments=agt.shape[0])
            c = c / (c_sum[v] + 1e-16)
            ctx_p = group_norm(ctx @ Wctx.T, gnc_w, gnc_b)
            msg = ctx_p[u] * c[:, None]
            agg = jax.ops.segment_sum(msg, v, num_segments=agt.shape[0])
            x = group_norm(jnp.concatenate([agt, agg], axis=1) @ Wagt.T, gna_w, gna_b)
            x = group_norm(x, norm_w, norm_b)
            x = jax.nn.relu(x)
            x = group_norm(x @ Wlin.T, gnl_w, gnl_b)
            return jax.nn.relu(x + res)
        for i in range(N_BLK):
            agt = _graph_att(agt, ctx, u, v, Wq[i], Wk[i], Wctx[i], gnc_w[i], gnc_b[i], Wagt[i], gna_w[i], gna_b[i], norm_w[i], norm_b[i], Wlin[i], gnl_w[i], gnl_b[i])
        return agt
    edge_index = jnp.stack([src, dst])
    h = jnp.maximum(_layernorm(x, axis=-1), 0.0)
    x = x + _L0_gnn_ref(h, edge_index, L0_gnn_Wl, L0_gnn_bl, L0_gnn_Wr)
    h = jnp.maximum(_layernorm(x, axis=-1), 0.0)
    x = x + _L1_gnn_ref(h, edge_index, L1_gnn_hyperedge_weight, L1_gnn_W1, L1_gnn_b1, L1_gnn_gamma, L1_gnn_beta, L1_gnn_W2, L1_gnn_b2)
    h = jnp.maximum(_layernorm(x, axis=-1), 0.0)
    x = x + _L2_gnn_ref(edge_index, h, L2_gnn_W_w, L2_gnn_W_b, L2_gnn_a, L2_gnn_V_w, L2_gnn_V_b, L2_gnn_ln_g, L2_gnn_ln_b)
    h = jnp.maximum(_layernorm(x, axis=-1), 0.0)
    x = x + _L3_gnn_ref(h, L3_gnn_ctx, src, dst, L3_gnn_Wq, L3_gnn_Wk, L3_gnn_Wctx, L3_gnn_gnc_w, L3_gnn_gnc_b, L3_gnn_Wagt, L3_gnn_gna_w, L3_gnn_gna_b, L3_gnn_norm_w, L3_gnn_norm_b, L3_gnn_Wlin, L3_gnn_gnl_w, L3_gnn_gnl_b)
    return x

_drawn_inputs = setup_inputs


def setup_inputs(seed=0):
    import zlib

    import numpy as np

    out = dict(_drawn_inputs(seed))
    spreads = {'L1_gnn_hyperedge_weight': (1.0, 0.2),
     'L1_gnn_b1': (0.0, 2.0),
     'L1_gnn_gamma': (1.0, 0.2),
     'L1_gnn_beta': (0.0, 0.474),
     'L1_gnn_b2': (0.0, 0.1),
     'L2_gnn_V_b': (0.0, 0.1),
     'L2_gnn_ln_g': (1.0, 0.2),
     'L2_gnn_ln_b': (0.0, 0.331),
     'L3_gnn_gnc_w': (1.0, 0.2),
     'L3_gnn_gnc_b': (0.0, 0.28),
     'L3_gnn_gna_w': (1.0, 0.2),
     'L3_gnn_gna_b': (0.0, 0.1),
     'L3_gnn_norm_w': (1.0, 0.2),
     'L3_gnn_norm_b': (0.0, 0.1),
     'L3_gnn_gnl_w': (1.0, 0.2),
     'L3_gnn_gnl_b': (0.0, 0.1)}
    factors = {'L0_gnn_bl': 8.0, 'L2_gnn_a': 183.993}
    for name, (base, spread) in spreads.items():
        noise = np.random.default_rng([zlib.crc32(name.encode()), seed]).standard_normal(out[name].shape)
        drawn = base * np.exp(spread * noise) if base else spread * noise
        out[name] = jnp.asarray(drawn.astype(out[name].dtype))
    for name, factor in factors.items():
        out[name] = (out[name] * factor).astype(out[name].dtype)
    return out
```

```python
import concourse.bass as bass
from concourse import mybir
from contextlib import ExitStack, contextmanager

FP32 = mybir.dt.float32
BF16 = mybir.dt.bfloat16
I32 = mybir.dt.int32
ALU = mybir.AluOpType
ACT = mybir.ActivationFunctionType
AX = mybir.AxisListType
ds = bass.ds

P = 128
N = 50000
GT = 4
ROWS = GT * P
GROUPS = -(-N // (2 * ROWS)) * 2
STEPS = GROUPS // 2
TILES = GROUPS * GT
NP = TILES * P
LASTG = N // ROWS
LASTP = (N - LASTG * ROWS) // GT
FULLP = N // TILES
RESTT = N - FULLP * TILES
PAD_KEY = 65535
HYPER = 10000
HGROUPS = 20
CTX = 3125
CTILES = 25
HEADS = 4
SW = 132


class Chain:

    def __init__(self, eng, sem):
        self.eng, self.sem, self.n = eng, sem, 0

    def __call__(self, ins):
        self.n += 1
        ins.then_inc(self.sem, 1)
        self.eng.wait_ge(self.sem, self.n)

    def tell(self, sem, by=1):
        self.eng.sem_inc(sem, by)

    def restart(self):
        self.eng.sem_clear(self.sem)
        self.n = 0


class Phase:

    def __init__(self, nc, name):
        self.nc, self.name, self.ctx, self.sems = nc, name, ExitStack(), []

    def sem(self, name):
        s = self.ctx.enter_context(self.nc.semaphore(f"{self.name}_{name}"))
        self.sems.append(s)
        return s

    def sems2(self, name):
        return [self.sem(f"{name}{b}") for b in range(2)]

    def sb(self, name, shape, dt=FP32):
        return self.ctx.enter_context(self.nc.sbuf_tensor(f"{self.name}_{name}", shape, dt))

    def sb2(self, name, shape, dt=FP32):
        return [self.sb(f"{name}{b}", shape, dt) for b in range(2)]

    def ps(self, name, shape, dt=FP32):
        return self.ctx.enter_context(self.nc.psum_tensor(f"{self.name}_{name}", shape, dt))

    def ps2(self, name, shape, dt=FP32):
        return [self.ps(f"{name}{b}", shape, dt) for b in range(2)]

    def __enter__(self):
        return self

    def __exit__(self, *exc):
        if exc[0] is None:
            with self.nc.Block() as block:
                @block.gpsimd
                def _(pool):
                    pool.dma_reset()
                    for s in self.sems:
                        pool.sem_clear(s)
        self.ctx.close()


def pool_wait(pool, sem, value, went_on):
    pool.wait_ge(sem, value)
    pool.sem_inc(went_on, 1)


def first_credit(nc, C, b, sem):
    nc.gpsimd.dma_start(C.credit[b:b + 1, :], C.eps[0:1, :]).then_inc(sem, 64)


def group_rows(table, g, lo=0, hi=None):
    v = table.rearrange("(g p k) d -> p g k d", p=P, k=GT)
    hi = table.shape[1] if hi is None else hi
    return v[:, ds(g, 1), :, lo:hi].rearrange("p o k d -> p (o k) d")


class Consts:
    pass


def make_consts(nc, ctx, w):
    C = Consts()

    def sb(name, shape, dt=FP32):
        return ctx.enter_context(nc.sbuf_tensor(name, shape, dt))

    C.ident = sb("ident", [P, P])
    C.ones = sb("ones", [P, P])
    C.zeros = sb("zeros", [P, P])
    C.ones_row = sb("ones_row", [1, ROWS])
    C.lower = sb("lower", [P, P], BF16)
    C.unit = sb("unit", [P, 2], BF16)
    C.ones_bf = sb("ones_bf", [P, 1], BF16)
    C.upper = sb("upper", [P, P])
    C.digit_free = sb("digit_free", [P, 256], BF16)
    C.digit_part = sb("digit_part", [P, 2])
    C.eps = sb("eps", [P, 1])
    C.credit = nc.dram_tensor("credit", (4, 1), FP32, kind="Internal").ap()
    C.hw = sb("hw", [P, HGROUPS, GT])
    mats = {"Wl": w["L0_gnn_Wl"], "Wr": w["L0_gnn_Wr"], "W1": w["L1_gnn_W1"], "W2": w["L1_gnn_W2"],
            "V": w["L2_gnn_V_w"]}
    for h in range(HEADS):
        mats[f"W{h}h"] = w["L2_gnn_W_w"][h]
    for k in range(2):
        mats[f"Wctx{k}"] = w["L3_gnn_Wctx"][k]
        mats[f"Wlin{k}"] = w["L3_gnn_Wlin"][k]
        mats[f"Wa{k}"] = w["L3_gnn_Wagt"][k][:, 0:P]
        mats[f"Wb{k}"] = w["L3_gnn_Wagt"][k][:, P:2 * P]
        mats[f"Wq{k}"] = w["L3_gnn_Wq"][k]
        mats[f"Wk{k}"] = w["L3_gnn_Wk"][k]
    names = list(mats)
    raw = sb("raw_weights", [P, len(names), P])
    C.wlr = sb("wlr", [P, 2, P])
    C.heads = sb("heads", [P, HEADS, P])
    C.ctxw = sb("ctxw", [P, 2, 2, P])
    C.t = {}
    for n in names:
        C.t[n] = sb("T_" + n, [P, P])
    vecs = {"bl": w["L0_gnn_bl"], "b2": w["L1_gnn_b2"], "gamma": w["L1_gnn_gamma"], "beta": w["L1_gnn_beta"],
            "Vb": w["L2_gnn_V_b"], "ln_g": w["L2_gnn_ln_g"], "ln_b": w["L2_gnn_ln_b"]}
    for h in range(HEADS):
        vecs[f"Wb{h}"] = w["L2_gnn_W_b"][h]
    for k in range(2):
        for v in ("gnc_w", "gnc_b", "gna_w", "gna_b", "norm_w", "norm_b", "gnl_w", "gnl_b"):
            vecs[f"{v}{k}"] = w[f"L3_gnn_{v}"][k]
    C.v = {n: sb("V_" + n, [P, P]) for n in vecs}
    C.mean_b = sb("mean_b", [P, P])
    C.acol = sb("acol", [P, 2 * HEADS])
    C.bcol = sb("bcol", [P, HEADS])
    C.bwide = sb("bwide", [P, HEADS, P])
    C.score_w = sb("score_w", [P, 2 * HEADS])
    C.score_b = sb("score_b", [P, 2 * HEADS])

    with Phase(nc, "setup") as ph:
        loaded, made, ready, moved = ph.sem("loaded"), ph.sem("made"), ph.sem("ready"), ph.sem("moved")
        hwset = ph.sem("hwset")
        chain_s, chain_g, chain_a = ph.sem("chain_dve"), ph.sem("chain_pool"), ph.sem("chain_act")
        tp = ph.ps2("tp", [P, P])
        n_loads = [0]
        with nc.Block() as block:
            @block.sync
            def _(sp):
                for j, n in enumerate(names):
                    sp.dma_start(raw[:, j, :], mats[n]).then_inc(loaded, 16)
                    n_loads[0] += 1
                for n, v in vecs.items():
                    sp.dma_start(C.v[n][:, :], v.rearrange("(a n) -> a n", a=1).partition_broadcast(P)
                                 if v.ndim == 1 else v).then_inc(loaded, 16)
                    n_loads[0] += 1
                with nc.allow_non_contiguous_dma(reason="small columns, once"):
                    for half in range(2):
                        sp.dma_start(C.acol[:, half * HEADS:(half + 1) * HEADS],
                                     w["L2_gnn_a"][:, half * P:(half + 1) * P].rearrange("h d -> d h")).then_inc(loaded, 16)
                        n_loads[0] += 1
                    sp.dma_start(C.bcol[:, :], w["L2_gnn_W_b"].rearrange("h d -> d h")).then_inc(loaded, 16)
                    n_loads[0] += 1
                sp.wait_ge(hwset, 1)
                full = HYPER // ROWS
                rest = (HYPER - full * ROWS) // GT
                sp.dma_start(C.hw[:, 0:full, :], w["L1_gnn_hyperedge_weight"][0:full * ROWS]
                             .rearrange("(g p k) -> p g k", p=P, k=GT)).then_inc(loaded, 16)
                sp.dma_start(C.hw[0:rest, full, :], w["L1_gnn_hyperedge_weight"][full * ROWS:HYPER]
                             .rearrange("(p k) -> p k", k=GT)).then_inc(loaded, 16)
                n_loads[0] += 2
                sp.wait_ge(loaded, 16 * n_loads[0])

            @block.gpsimd
            def _(pool):
                link = Chain(pool, chain_g)
                g = nc.gpsimd
                link(g.memset(C.ident[:, :], 0.0))
                link(g.affine_select(out=C.ident[:, :], in_=C.ident[:, :], compare_op=ALU.not_equal, fill=1.0,
                                     base=0, pattern=[[-1, P]], channel_multiplier=1))
                link(g.memset(C.upper[:, :], 1.0))
                link(g.affine_select(out=C.upper[:, :], in_=C.upper[:, :], compare_op=ALU.is_gt, fill=0.0,
                                     base=0, pattern=[[1, P]], channel_multiplier=-1))
                link(g.iota(C.digit_free[:, :], pattern=[[1, 256]], base=0, channel_multiplier=0,
                            allow_small_or_imprecise_dtypes=True))
                link(g.iota(C.digit_part[:, :], pattern=[[P, 2]], base=0, channel_multiplier=1,
                            allow_small_or_imprecise_dtypes=True))
                link.tell(made)

            @block.vector
            def _(dve):
                link = Chain(dve, chain_s)
                v = nc.vector
                link(v.memset(C.hw[:, :, :], 0.0))
                link.tell(hwset)
                v.memset(C.ones[:, :], 1.0)
                v.memset(C.zeros[:, :], 0.0)
                v.memset(C.ones_row[:, :], 1.0)
                v.memset(C.ones_bf[:, :], 1.0)
                link(v.memset(C.unit[:, :], 0.0))
                link(v.memset(C.unit[:, 0:1], 1.0))
                link(v.memset(C.eps[:, :], 1e-5))
                dve.wait_ge(made, 1)
                link(v.tensor_copy(C.lower[:, :], C.upper[:, :]))
                dve.wait_ge(loaded, 16 * n_loads[0])
                link(v.tensor_add(C.mean_b[:, :], C.v["Wb0"][:, :], C.v["Wb1"][:, :]))
                link(v.tensor_add(C.mean_b[:, :], C.mean_b[:, :], C.v["Wb2"][:, :]))
                link(v.tensor_add(C.mean_b[:, :], C.mean_b[:, :], C.v["Wb3"][:, :]))
                link(v.tensor_scalar(C.mean_b[:, :], C.mean_b[:, :], 1.0 / HEADS, None, ALU.mult))
                for h in range(HEADS):
                    link(v.tensor_scalar(C.bwide[:, h, :], C.ones[:, :], C.bcol[:, h:h + 1], None, ALU.mult))
                link.tell(made)

            jobs = []
            for j, n in enumerate(names):
                if n[:2] in ("Wq", "Wk"):
                    continue
                jobs.append((n, raw[:, j, :], C.ident[:, :], P))
            at = {n: j for j, n in enumerate(names)}
            for k in range(2):
                jobs.append((f"Wq{k}", raw[:, at[f"Wk{k}"], :], raw[:, at[f"Wq{k}"], :], P))
            for h in range(HEADS):
                for s in range(2):
                    c = s * HEADS + h
                    jobs.append((("w", c), raw[:, at[f"W{h}h"], :], C.acol[:, c:c + 1], 1))
                    jobs.append((("b", c), C.bwide[:, h, :], C.acol[:, c:c + 1], 1))

            @block.tensor
            def _(pe):
                pe.wait_ge(made, 2)
                pe.wait_ge(loaded, 16 * n_loads[0])
                for j, (n, left, right, width) in enumerate(jobs):
                    if j >= 2:
                        pe.wait_ge(moved, j - 1)
                    nc.tensor.matmul(tp[j % 2][:, 0:width], left, right, start=True, stop=True).then_inc(ready, 1)

            places = {"Wl": C.wlr[:, 0, :], "Wr": C.wlr[:, 1, :]}
            for h in range(HEADS):
                places[f"W{h}h"] = C.heads[:, h, :]
            for k in range(2):
                places[f"Wq{k}"] = C.ctxw[:, k, 0, :]
                places[f"Wctx{k}"] = C.ctxw[:, k, 1, :]
            for c in range(2 * HEADS):
                places["w", c] = C.score_w[:, c:c + 1]
                places["b", c] = C.score_b[:, c:c + 1]

            @block.scalar
            def _(act):
                for j, (n, _, _, width) in enumerate(jobs):
                    act.wait_ge(ready, j + 1)
                    to = places[n] if n in places else C.t[n][:, :]
                    nc.scalar.copy(to, tp[j % 2][:, 0:width]).then_inc(moved, 1)
                act.wait_ge(moved, len(jobs))
    return C


def load_edges(nc, A, keys, others, name):
    with Phase(nc, "edges_" + name) as ph:
        raw = [ph.sb("key", [P, TILES], I32), ph.sb("other", [P, TILES], I32)]
        loaded, padded, chain = ph.sem("loaded"), ph.sem("padded"), ph.sem("chain")
        with nc.Block() as block:
            @block.sync
            def _(sp):
                sp.wait_ge(padded, 1)
                for r, v in zip(raw, (keys, others)):
                    sp.dma_start(r[0:FULLP, :], v[0:FULLP * TILES].rearrange("(p t) -> p t", t=TILES)).then_inc(loaded, 16)
                    sp.dma_start(r[FULLP:FULLP + 1, 0:RESTT], v[FULLP * TILES:N].rearrange("(p t) -> p t", p=1)).then_inc(loaded, 16)
                sp.wait_ge(loaded, 64)

            @block.vector
            def _(dve):
                link = Chain(dve, chain)
                link(nc.vector.memset(raw[0][:, :], PAD_KEY))
                link(nc.vector.memset(raw[1][:, :], 0))
                link.tell(padded)
                dve.wait_ge(loaded, 64)
                link(nc.vector.tensor_copy(A[:, :, 0], raw[0][:, :]))
                link(nc.vector.tensor_copy(A[:, :, 1], raw[1][:, :]))


def sort_pass(nc, C, name, A, table, digit_rows, shift):
    with Phase(nc, name) as ph:
        digit_i = ph.sb("digit_i", [P, TILES], I32)
        digit = ph.sb("digit", [P, TILES])
        rows = ph.sb("rows", [P, GT, P], BF16)
        onehot = ph.sb2("onehot", [P, GT, 256], BF16)
        running = ph.sb("running", [P, 2, TILES])
        counts = ph.sb("counts", [P, 2, TILES])
        base = ph.sb("base", [P, 2])
        start_i = ph.sb("start_i", [P, 2, TILES], I32)
        part_i = ph.sb("part_i", [P, 2, TILES], I32)
        start = ph.sb("start", [P, 2, TILES, 2], BF16)
        wide = ph.sb2("wide", [P, ROWS], BF16)
        member = ph.sb2("member", [P, 2, ROWS], BF16)
        before = ph.sb2("before", [P, GT, P], BF16)
        parts = ph.sb2("parts", [P, GT, 2])
        pos = ph.sb2("pos", [P, GT], I32)
        pos_lo = ph.sb2("pos_lo", [P, GT], I32)
        pos_hi = ph.sb2("pos_hi", [P, GT], I32)
        where = ph.sb2("where", [P, GT], I32)
        pairs = ph.sb2("pairs", [P, GT, 2], I32)
        tp = ph.ps("tp", [P, 4, P])
        count_ps = [ph.ps(f"count{h}", [P, 512]) for h in range(2)]
        base_ps = ph.ps("base_ps", [P, 2])
        pos_ps = ph.ps2("pos_ps", [P, GT, 2])
        digits_ready, turned, rows_ready, rows_out = (ph.sem(x) for x in ("digits_ready", "turned", "rows_ready", "rows_out"))
        chain = ph.sem("chain")
        hot, counted = ph.sems2("hot"), ph.sems2("counted")
        totals_ready, base_ready, start_ready = (ph.sem(x) for x in ("totals_ready", "base_ready", "start_ready"))
        wide_in, wide_used = ph.sems2("wide_in"), ph.sems2("wide_used")
        member_ready, placed, taken = ph.sems2("member_ready"), ph.sems2("placed"), ph.sems2("taken")
        where_ready, scattered = ph.sems2("where_ready"), ph.sems2("scattered")
        went_on = ph.sem("went_on")
        tail = TILES - 3 * P
        digit_tiles = digit_rows.rearrange("(t c) -> t c", c=P)
        with nc.Block() as block:
            @block.sync
            def _(sp):
                for b in range(2):
                    sp.sem_inc(wide_used[b], 1)
                sp.wait_ge(rows_ready, 1)
                sp.dma_start(digit_tiles[0:3 * P, :].rearrange("(j p) c -> p j c", p=P), rows[:, 0:3, :]).then_inc(rows_out, 16)
                sp.dma_start(digit_tiles[3 * P:TILES, :], rows[0:tail, 3, :]).then_inc(rows_out, 16)
                sp.wait_ge(rows_out, 32)
                with nc.sync.Fori(0, STEPS) as i:
                    for b in range(2):
                        sp.wait_ge(wide_used[b], i + 1)
                        sp.dma_start(wide[b][:, :], digit_rows[ds((i * 2 + b) * ROWS, ROWS)]
                                     .rearrange("(a n) -> a n", a=1).partition_broadcast(P)).then_inc(wide_in[b], 16)

            @block.tensor
            def _(pe):
                pe.wait_ge(digits_ready, 1)
                for j in range(4):
                    w = P if j < 3 else tail
                    last = nc.tensor.transpose(tp[0:w, j, :], digit[:, j * P:j * P + w], C.ident[:, :])
                last.then_inc(turned, 1)
                with nc.tensor.Fori(0, STEPS) as i:
                    for b in range(2):
                        pe.wait_ge(hot[b], i + 1)
                        for k in range(GT):
                            for h in range(2):
                                last = nc.tensor.matmul(count_ps[h][:, ds(i * 8 + b * 4 + k, 1)],
                                                        onehot[b][:, k, h * P:(h + 1) * P], C.ones_bf[:, :],
                                                        start=True, stop=True)
                        last.then_inc(counted[b], 1)
                pe.wait_ge(totals_ready, 1)
                nc.tensor.matmul(base_ps[:, 0:1], C.upper[:, :], running[:, 0, TILES - 1:TILES], start=True, stop=True)
                nc.tensor.matmul(base_ps[:, 1:2], C.upper[:, :], running[:, 1, TILES - 1:TILES], start=True, stop=False)
                nc.tensor.matmul(base_ps[:, 1:2], C.ones[:, :], running[:, 0, TILES - 1:TILES], start=False, stop=True).then_inc(base_ready, 1)
                pe.wait_ge(start_ready, 1)
                with nc.tensor.Fori(0, STEPS) as i:
                    for b in range(2):
                        pe.wait_ge(member_ready[b], i + 1)
                        pe.wait_ge(taken[b], i + 1)
                        for k in range(GT):
                            t = i * 8 + b * 4 + k
                            o = pos_ps[b][:, k, :]
                            nc.tensor.matmul(o, before[b][:, k, :], C.unit[:, :], start=True, stop=False)
                            for h in range(2):
                                last = nc.tensor.matmul(o, member[b][:, h, k * P:(k + 1) * P],
                                                        start[:, h, ds(t, 1), :].rearrange("p o c -> p (o c)"),
                                                        start=False, stop=(h == 1))
                        last.then_inc(placed[b], 1)

            @block.scalar
            def _(act):
                act.wait_ge(turned, 1)
                nc.scalar.copy(rows[:, 0:3, :], tp[:, 0:3, :]).then_inc(went_on, 1)
                act.wait_ge(went_on, 1)
                nc.scalar.copy(rows[0:tail, 3, :], tp[0:tail, 3, :]).then_inc(rows_ready, 1)

            @block.vector
            def _(dve):
                v = nc.vector
                link = Chain(dve, chain)
                link(v.tensor_scalar(digit_i[:, :], A[:, :, 0], shift, 255, ALU.logical_shift_right, ALU.bitwise_and))
                link(v.tensor_copy(digit[:, :], digit_i[:, :]))
                link.tell(digits_ready)
                for b in range(2):
                    dve.sem_inc(counted[b], 1)
                    dve.sem_inc(taken[b], 1)
                link.restart()
                with v.Fori(0, STEPS) as i:
                    for b in range(2):
                        dve.wait_ge(counted[b], i + 1)
                        for k in range(GT):
                            last = v.tensor_scalar(onehot[b][:, k, :], C.digit_free[:, :],
                                                   digit[:, ds(i * 8 + b * 4 + k, 1)], None, ALU.is_equal)
                        last.then_inc(hot[b], 1)
                for b in range(2):
                    dve.wait_ge(counted[b], STEPS + 1)
                for h in range(2):
                    link(v.tensor_copy(counts[:, h, :], count_ps[h][:, 0:TILES]))
                    link(v.tensor_tensor_scan(running[:, h, :], counts[:, h, :], counts[:, h, :], 0.0,
                                              ALU.add, ALU.bypass))
                link.tell(totals_ready)
                dve.wait_ge(base_ready, 1)
                link(v.tensor_copy(base[:, :], base_ps[:, :]))
                for h in range(2):
                    link(v.tensor_sub(running[:, h, :], running[:, h, :], counts[:, h, :]))
                    link(v.tensor_scalar(start_i[:, h, :], running[:, h, :], base[:, h:h + 1], None, ALU.add))
                link(v.tensor_scalar(part_i[:, :, :], start_i[:, :, :], 255, None, ALU.bitwise_and))
                link(v.tensor_copy(start[:, :, :, 0], part_i[:, :, :]))
                link(v.tensor_scalar(part_i[:, :, :], start_i[:, :, :], 8, None, ALU.logical_shift_right))
                link(v.tensor_copy(start[:, :, :, 1], part_i[:, :, :]))
                link.tell(start_ready)
                link.restart()
                with v.Fori(0, STEPS) as i:
                    for b in range(2):
                        dve.wait_ge(wide_in[b], i * 16 + 16)
                        for h in range(2):
                            v.tensor_scalar(member[b][:, h, :], wide[b][:, :], C.digit_part[:, h:h + 1], None, ALU.is_equal)
                        for k in range(GT):
                            last = v.scalar_tensor_tensor(before[b][:, k, :], wide[b][:, k * P:(k + 1) * P],
                                                          digit[:, ds(i * 8 + b * 4 + k, 1)], C.lower[:, :],
                                                          ALU.is_equal, ALU.mult)
                        link(last)
                        link.tell(wide_used[b])
                        link.tell(member_ready[b])
                    for b in range(2):
                        dve.wait_ge(placed[b], i + 1)
                        link(v.tensor_copy(parts[b][:, :, :], pos_ps[b][:, :, :]))
                        link.tell(taken[b])
                        dve.wait_ge(scattered[b], i * 64 + 64)
                        link(v.scalar_tensor_tensor(pos[b][:, :], parts[b][:, :, 1], 256.0, parts[b][:, :, 0], ALU.mult, ALU.add))
                        v.tensor_scalar(pos_lo[b][:, :], pos[b][:, :], P - 1, None, ALU.bitwise_and)
                        v.tensor_copy(pairs[b][:, :, :], A[:, ds(i * 8 + b * 4, GT), :])
                        link(v.tensor_scalar(pos_hi[b][:, :], pos[b][:, :], 7, None, ALU.logical_shift_right))
                        link(v.scalar_tensor_tensor(where[b][:, :], pos_lo[b][:, :], float(TILES), pos_hi[b][:, :], ALU.mult, ALU.add))
                        link.tell(where_ready[b])
                    link.restart()

            @block.gpsimd
            def _(pool):
                for b in range(2):
                    first_credit(nc, C, b, scattered[b])
                with nc.gpsimd.Fori(0, STEPS) as i:
                    for b in range(2):
                        pool_wait(pool, where_ready[b], i + 1, went_on)
                        for k in range(GT):
                            nc.gpsimd.indirect_dma_start(
                                out=table, out_offset=bass.IndirectOffsetOnAxis(ap=where[b][:, k:k + 1], axis=0),
                                in_=pairs[b][:, k, :], in_offset=None, bounds_check=NP - 1,
                                oob_is_err=False).then_inc(scattered[b], 16)
                for b in range(2):
                    pool.wait_ge(scattered[b], 64 * (STEPS + 1))


def reload_pairs(nc, A, table, name):
    with Phase(nc, name) as ph:
        loaded = ph.sem("loaded")
        with nc.Block() as block:
            @block.sync
            def _(sp):
                sp.dma_start(A[:, :, :], table.rearrange("(p t) c -> p t c", t=TILES)).then_inc(loaded, 16)
                sp.wait_ge(loaded, 16)


class Order:

    KEY, OTHER, CLAMPED, TARGET = range(4)

    def __init__(self, nc, ctx, name):
        self.name = name
        self.index = nc.dram_tensor(f"{name}_index", (P, GROUPS * 4 * GT), I32, kind="Internal").ap()
        self.same = nc.dram_tensor(f"{name}_same", (NP,), BF16, kind="Internal").ap()
        self.pad_bias = ctx.enter_context(nc.sbuf_tensor(f"{name}_pad_bias", [P, TILES], FP32))

    def index_of(self, g, slot, slots=1):
        at = self.index.rearrange("p (g s) -> p g s", s=4 * GT)
        return at[:, ds(g, 1), slot * GT:(slot + slots) * GT].rearrange("p o s -> p (o s)")


def describe_order(nc, C, A, table, order, limit):
    with Phase(nc, "order_" + order.name) as ph:
        later = ph.sb("later", [P, TILES, 2], I32)
        earlier = ph.sb("earlier", [P, TILES, 2], I32)
        key, nxt, prv = ph.sb("key", [P, TILES]), ph.sb("nxt", [P, TILES]), ph.sb("prv", [P, TILES])
        same, more = ph.sb("same", [P, TILES]), ph.sb("more", [P, TILES])
        packed = ph.sb("packed", [P, GROUPS, 4, GT], I32)
        rows = ph.sb("rows", [P, 4, P], BF16)
        tp = ph.ps("tp", [P, 4, P])
        loaded, cleared, same_ready, turned, rows_ready, packed_ready, stored, chain, chain_act = (ph.sem(x) for x in (
            "loaded", "cleared", "same_ready", "turned", "rows_ready", "packed_ready", "stored", "chain", "chain_act"))
        tail = TILES - 3 * P
        tv = table.rearrange("(p t) c -> p t c", t=TILES)
        same_tiles = order.same.rearrange("(t c) -> t c", c=P)
        with nc.Block() as block:
            @block.sync
            def _(sp):
                sp.dma_start(A[:, :, :], tv).then_inc(loaded, 16)
                sp.wait_ge(cleared, 1)
                sp.dma_start(later[0:P - 1, :, :], tv[1:P, :, :]).then_inc(loaded, 16)
                sp.dma_start(later[P - 1:P, 0:TILES - 1, :], tv[0:1, 1:TILES, :]).then_inc(loaded, 16)
                sp.dma_start(earlier[1:P, :, :], tv[0:P - 1, :, :]).then_inc(loaded, 16)
                sp.dma_start(earlier[0:1, 1:TILES, :], tv[P - 1:P, 0:TILES - 1, :]).then_inc(loaded, 16)
                sp.wait_ge(rows_ready, 1)
                sp.dma_start(same_tiles[0:3 * P, :].rearrange("(j p) c -> p j c", p=P), rows[:, 0:3, :]).then_inc(stored, 16)
                sp.dma_start(same_tiles[3 * P:TILES, :], rows[0:tail, 3, :]).then_inc(stored, 16)
                sp.wait_ge(packed_ready, 1)
                sp.dma_start(order.index, packed[:, :, :, :].rearrange("p g s k -> p (g s k)")).then_inc(stored, 16)
                sp.wait_ge(stored, 48)

            @block.vector
            def _(dve):
                v = nc.vector
                link = Chain(dve, chain)
                v.memset(later[:, :, :], -1)
                link(v.memset(earlier[:, :, :], -1))
                link.tell(cleared)
                dve.wait_ge(loaded, 80)
                v.tensor_copy(key[:, :], A[:, :, 0])
                v.tensor_copy(nxt[:, :], later[:, :, 0])
                link(v.tensor_copy(prv[:, :], earlier[:, :, 0]))
                link(v.tensor_tensor(same[:, :], key[:, :], prv[:, :], ALU.is_equal))
                link.tell(same_ready)
                link(v.tensor_tensor(more[:, :], key[:, :], nxt[:, :], ALU.is_equal))
                link(v.scalar_tensor_tensor(more[:, :], more[:, :], float(PAD_KEY), key[:, :], ALU.mult, ALU.max))
                grouped = [x.rearrange("p (g k) -> p g k", k=GT) for x in (key[:, :], more[:, :])]
                other = A[:, :, 1].rearrange("p (g k) -> p g k", k=GT)
                v.tensor_scalar(packed[:, :, Order.KEY, :], grouped[0], float(NP - 1), None, ALU.min)
                v.tensor_copy(packed[:, :, Order.OTHER, :], other)
                v.tensor_scalar(packed[:, :, Order.CLAMPED, :], other, float(limit - 1), None, ALU.min)
                v.tensor_scalar(order.pad_bias[:, :], key[:, :], float(N), -1e30, ALU.is_ge, ALU.mult)
                link(v.tensor_copy(packed[:, :, Order.TARGET, :], grouped[1]))
                link.tell(packed_ready)

            @block.tensor
            def _(pe):
                pe.wait_ge(same_ready, 1)
                for j in range(4):
                    w = P if j < 3 else tail
                    last = nc.tensor.transpose(tp[0:w, j, :], same[:, j * P:j * P + w], C.ident[:, :])
                last.then_inc(turned, 1)

            @block.scalar
            def _(act):
                link = Chain(act, chain_act)
                act.wait_ge(turned, 1)
                link(nc.scalar.copy(rows[:, 0:3, :], tp[:, 0:3, :]))
                nc.scalar.copy(rows[0:tail, 3, :], tp[0:tail, 3, :]).then_inc(rows_ready, 1)


def fill_zero(nc, C, tables):
    with Phase(nc, "zero") as ph:
        z = ph.sb("z", [P, 14 * SW])
        cleared, stored = ph.sem("cleared"), ph.sem("stored")
        chunk = P * 14
        count = NP // chunk
        with nc.Block() as block:
            @block.vector
            def _(dve):
                nc.vector.memset(z[:, :], 0.0).then_inc(cleared, 1)

            @block.sync
            def _(sp):
                sp.wait_ge(cleared, 1)
                for t in tables:
                    v = t.rearrange("(c p r) w -> c p (r w)", p=P, r=14)
                    for c in range(count):
                        sp.dma_start(v[c], z[:, :]).then_inc(stored, 16)
                sp.wait_ge(stored, 16 * count * len(tables))


def gather(nc, to, table, index, sem, rows):
    nc.gpsimd.indirect_dma_start(out=to, out_offset=None, in_=table,
                                 in_offset=bass.IndirectOffsetOnAxis(ap=index, axis=0),
                                 bounds_check=rows - 1, oob_is_err=False).then_inc(sem, 16)


def edge_loaders(nc, order, block, slot, slots, gather_index, target, same, gather_index_in, target_in, same_in,
                 gathered, scattered, same_used, unit):
    @block.sync
    def _(sp):
        for b in range(2):
            sp.sem_inc(same_used[b], 1)
        with nc.sync.Fori(0, STEPS) as i:
            for b in range(2):
                g = i * 2 + b
                sp.wait_ge(gathered[b], i * unit + unit)
                sp.dma_start(gather_index[b][:, :], order.index_of(g, slot, slots)).then_inc(gather_index_in[b], 16)
                sp.wait_ge(same_used[b], i + 1)
                sp.dma_start(same[b][:, :], order.same[ds(g * ROWS, ROWS)]
                             .rearrange("(a n) -> a n", a=1).partition_broadcast(P)).then_inc(same_in[b], 16)
                sp.wait_ge(scattered[b], i * 64 + 64)
                sp.dma_start(target[b][:, :], order.index_of(g, Order.TARGET)).then_inc(target_in[b], 16)


def edge_pool(nc, C, block, gathers, sums, rows_out, target, target_in, rows_ready, gathered, scattered,
              gather_index_in, gathers_free, went_on, unit):
    @block.gpsimd
    def _(pool):
        for b in range(2):
            nc.gpsimd.dma_start(C.credit[b:b + 1, :], C.eps[0:1, :]).then_inc(gathered[b], unit)
            nc.gpsimd.dma_start(C.credit[2 + b:3 + b, :], C.eps[0:1, :]).then_inc(scattered[b], 64)

        def take(i, b):
            pool_wait(pool, gather_index_in[b], i * 16 + 16, went_on)
            pool_wait(pool, gathers_free[b], i + 1, went_on)
            gathers(b)

        def put(i, b):
            pool_wait(pool, target_in[b], i * 16 + 16, went_on)
            pool_wait(pool, rows_ready[b], i + 1, went_on)
            for k in range(GT):
                nc.gpsimd.indirect_dma_start(
                    out=sums, out_offset=bass.IndirectOffsetOnAxis(ap=target[b][:, k:k + 1], axis=0),
                    in_=rows_out[b][:, k, :], in_offset=None, bounds_check=NP - 1,
                    oob_is_err=False).then_inc(scattered[b], 16)

        take(0, 0)
        with nc.gpsimd.Fori(0, STEPS - 1) as i:
            take(i, 1)
            put(i, 0)
            take(i + 1, 0)
            put(i, 1)
        take(STEPS - 1, 1)
        put(STEPS - 1, 0)
        put(STEPS - 1, 1)
        for b in range(2):
            pool.wait_ge(scattered[b], 64 * (STEPS + 1))


def plain_pass(nc, C, name, order, table, width, slot, weight, sums):
    counts = width == P
    with Phase(nc, name) as ph:
        rows = ph.sb2("rows", [P, GT, width])
        gather_index, target = ph.sb2("gather_index", [P, GT], I32), ph.sb2("target", [P, GT], I32)
        same = ph.sb2("same", [P, ROWS], BF16)
        total, scalar_total = ph.sb2("total", [P, ROWS]), ph.sb2("scalar_total", [1, ROWS])
        out_rows = ph.sb2("out_rows", [P, GT, SW])
        turned_ps, product = ph.ps2("turned_ps", [P, ROWS]), ph.ps2("product", [P, GT, P])
        scalar_ps, scalar_back = ph.ps2("scalar_ps", [1, ROWS]), ph.ps2("scalar_back", [P, GT])
        names = ("gather_index_in", "target_in", "same_in", "gathered", "scattered", "same_used",
                 "turned", "scanned", "projected", "copied", "rows_ready")
        (gather_index_in, target_in, same_in, gathered, scattered, same_used,
         turned, scanned, projected, copied, rows_ready) = (ph.sems2(x) for x in names)
        went_on, chain, chain_act, cleared = ph.sem("went_on"), ph.sem("chain"), ph.sem("chain_act"), ph.sem("cleared")
        unit = 64
        with nc.Block() as block:
            edge_loaders(nc, order, block, slot, 1, gather_index, target, same, gather_index_in, target_in, same_in,
                         gathered, scattered, same_used, unit)

            def gathers(b):
                for k in range(GT):
                    gather(nc, rows[b][:, k, :], table, gather_index[b][:, k:k + 1], gathered[b], table.shape[0])

            edge_pool(nc, C, block, gathers, sums, out_rows, target, target_in, rows_ready, gathered, scattered,
                      gather_index_in, turned, went_on, unit)

            @block.tensor
            def _(pe):
                for b in range(2):
                    pe.sem_inc(turned[b], 1)
                    pe.sem_inc(projected[b], 1)
                with nc.tensor.Fori(0, STEPS) as i:
                    for b in range(2):
                        pe.wait_ge(gathered[b], i * unit + 2 * unit)
                        pe.wait_ge(scanned[b], i + 1)
                        for k in range(GT):
                            if not counts:
                                nc.tensor.matmul(scalar_ps[b][:, k * P:(k + 1) * P], rows[b][:, k, P:P + 1],
                                                 C.ident[:, :], start=True, stop=True)
                            last = nc.tensor.transpose(turned_ps[b][:, k * P:(k + 1) * P], rows[b][:, k, 0:P], C.ident[:, :])
                        last.then_inc(turned[b], 1)
                        pe.wait_ge(scanned[b], i + 2)
                        pe.wait_ge(copied[b], i + 1)
                        for k in range(GT):
                            nc.tensor.matmul(product[b][:, k, :], total[b][:, k * P:(k + 1) * P], weight,
                                             start=True, stop=True)
                            last = nc.tensor.matmul(scalar_back[b][:, k:k + 1], scalar_total[b][:, k * P:(k + 1) * P],
                                                    C.ones[0:1, 0:1], start=True, stop=True)
                        last.then_inc(projected[b], 1)

            @block.vector
            def _(dve):
                v = nc.vector
                link = Chain(dve, chain)
                v.memset(total[1][:, ROWS - 1:ROWS], 0.0)
                link(v.memset(scalar_total[1][:, ROWS - 1:ROWS], 0.0))
                for b in range(2):
                    dve.sem_inc(scanned[b], 1)
                link.restart()
                with v.Fori(0, STEPS) as i:
                    for b in range(2):
                        dve.wait_ge(turned[b], i + 2)
                        dve.wait_ge(same_in[b], i * 16 + 16)
                        dve.wait_ge(projected[b], i + 1)
                        source = C.ones_row[0:1, :] if counts else scalar_ps[b][:, :]
                        v.tensor_tensor_scan(scalar_total[b][:, :], same[b][0:1, :], source,
                                             scalar_total[1 - b][:, ROWS - 1:ROWS], ALU.mult, ALU.add)
                        link(v.tensor_tensor_scan(total[b][:, :], same[b][:, :], turned_ps[b][:, :],
                                                  total[1 - b][:, ROWS - 1:ROWS], ALU.mult, ALU.add))
                        link.tell(scanned[b])
                        link.tell(same_used[b])
                    link.restart()

            @block.scalar
            def _(act):
                link = Chain(act, chain_act)
                for b in range(2):
                    act.sem_inc(copied[b], 1)
                for b in range(2):
                    last = nc.scalar.copy(out_rows[b][:, :, P:SW], C.zeros[:, 0:GT * (SW - P)].rearrange("p (k c) -> p k c", k=GT))
                link(last)
                link.restart()
                with nc.scalar.Fori(0, STEPS) as i:
                    for b in range(2):
                        act.wait_ge(projected[b], i + 2)
                        act.wait_ge(scattered[b], i * 64 + 64)
                        nc.scalar.copy(out_rows[b][:, :, P], scalar_back[b][:, :])
                        link(nc.scalar.copy(out_rows[b][:, :, 0:P], product[b][:, :, :]))
                        link.tell(copied[b])
                        link.tell(rows_ready[b])
                    link.restart()


def attention_pass(nc, C, order, table, scores, sums):
    scale = float((P * HEADS) ** -0.5)
    with Phase(nc, "gat") as ph:
        rows, mine = ph.sb2("rows", [P, GT, P + HEADS]), ph.sb2("mine", [P, GT, HEADS])
        gather_index, target = ph.sb2("gather_index", [P, 2 * GT], I32), ph.sb2("target", [P, GT], I32)
        same = ph.sb2("same", [P, ROWS], BF16)
        e, ee, t1 = ph.sb2("e", [P, GT, HEADS]), ph.sb2("ee", [P, GT, HEADS]), ph.sb("t1", [P, GT, HEADS])
        weighted = ph.sb2("weighted", [P, HEADS, GT, P])
        total, scalar_total = ph.sb2("total", [P, HEADS, ROWS]), ph.sb2("scalar_total", [HEADS, ROWS])
        out_rows = ph.sb2("out_rows", [P, GT, SW])
        wsum, empty, winv = ph.sb("wsum", [P, GT, HEADS]), ph.sb("empty", [P, GT, HEADS]), ph.sb("winv", [P, GT, HEADS])
        turned_ps = [ph.ps(f"turned_ps{h}", [P, ROWS]) for h in range(HEADS)]
        product = ph.ps2("product", [P, HEADS, P])
        scalar_ps, scalar_back = ph.ps("scalar_ps", [HEADS, ROWS]), ph.ps("scalar_back", [P, GT, HEADS])
        names = ("gather_index_in", "target_in", "same_in", "gathered", "scattered", "same_used", "scores_ready",
                 "weighted_ready", "turned", "scanned", "product_ready", "product_used", "rows_ready")
        (gather_index_in, target_in, same_in, gathered, scattered, same_used, scores_ready,
         weighted_ready, turned, scanned, product_ready, product_used, rows_ready) = (ph.sems2(x) for x in names)
        sums_back, sums_used = ph.sem("sums_back"), ph.sem("sums_used")
        went_on, chain, chain_act = ph.sem("went_on"), ph.sem("chain"), ph.sem("chain_act")
        unit = 128
        with nc.Block() as block:
            edge_loaders(nc, order, block, Order.KEY, 2, gather_index, target, same, gather_index_in, target_in,
                         same_in, gathered, scattered, same_used, unit)

            def gathers(b):
                for k in range(GT):
                    gather(nc, rows[b][:, k, :], table, gather_index[b][:, GT + k:GT + k + 1], gathered[b], NP)
                    gather(nc, mine[b][:, k, :], scores, gather_index[b][:, k:k + 1], gathered[b], NP)

            edge_pool(nc, C, block, gathers, sums, out_rows, target, target_in, rows_ready, gathered, scattered,
                      gather_index_in, weighted_ready, went_on, unit)

            @block.scalar
            def _(act):
                link = Chain(act, chain_act)
                for b in range(2):
                    act.sem_inc(weighted_ready[b], 1)
                with nc.scalar.Fori(0, STEPS) as i:
                    for b in range(2):
                        act.wait_ge(scores_ready[b], i + 1)
                        act.wait_ge(turned[b], i + 1)
                        link(nc.scalar.activation(ee[b][:, :, :], e[b][:, :, :], ACT.Exp, scale=scale))
                        for h in range(HEADS):
                            for k in range(GT):
                                last = nc.scalar.activation(weighted[b][:, h, k, :], rows[b][:, k, 0:P], ACT.Copy,
                                                            scale=ee[b][:, k, h:h + 1])
                        link(last)
                        link.tell(weighted_ready[b])
                    link.restart()

            @block.tensor
            def _(pe):
                for b in range(2):
                    pe.sem_inc(turned[b], 1)
                pe.sem_inc(sums_back, 1)
                with nc.tensor.Fori(0, STEPS) as i:
                    for b in range(2):
                        pe.wait_ge(weighted_ready[b], i + 2)
                        pe.wait_ge(scanned[1 - b], i + 1 + b)
                        for k in range(GT):
                            nc.tensor.matmul(scalar_ps[:, k * P:(k + 1) * P], ee[b][:, k, :], C.ident[:, :],
                                             start=True, stop=True)
                            for h in range(HEADS):
                                last = nc.tensor.transpose(turned_ps[h][:, k * P:(k + 1) * P], weighted[b][:, h, k, :], C.ident[:, :])
                        last.then_inc(turned[b], 1)
                        pe.wait_ge(scanned[b], i + 1 + 1)
                        pe.wait_ge(sums_used, i * 2 + b + 1)
                        for k in range(GT):
                            last = nc.tensor.matmul(scalar_back[:, k, :], scalar_total[b][:, k * P:(k + 1) * P],
                                                    C.ident[0:HEADS, 0:HEADS], start=True, stop=True)
                        last.then_inc(sums_back, 1)
                        for k in range(GT):
                            pe.wait_ge(product_used[k % 2], i * 4 + b * 2 + k // 2 + 1)
                            for h in range(HEADS):
                                last = nc.tensor.matmul(product[k % 2][:, h, :], total[b][:, h, k * P:(k + 1) * P],
                                                        C.heads[:, h, :], start=True, stop=True)
                            last.then_inc(product_ready[k % 2], 1)

            @block.vector
            def _(dve):
                v = nc.vector
                link = Chain(dve, chain)
                v.memset(total[1][:, :, ROWS - 1:ROWS], 0.0)
                link(v.memset(scalar_total[1][:, ROWS - 1:ROWS], 0.0))
                link.restart()
                for b in range(2):
                    dve.sem_inc(scanned[b], 1)
                    dve.sem_inc(product_used[b], 1)
                dve.sem_inc(sums_used, 1)

                def score(i, b):
                    dve.wait_ge(gathered[b], i * unit + 2 * unit)
                    dve.wait_ge(weighted_ready[b], i + 1)
                    link(v.tensor_add(t1[:, :, :], rows[b][:, :, P:P + HEADS], mine[b][:, :, :]))
                    link(v.scalar_tensor_tensor(e[b][:, :, :], t1[:, :, :], 0.2, t1[:, :, :], ALU.mult, ALU.max))
                    link.tell(scores_ready[b])

                def scan(i, b):
                    dve.wait_ge(turned[b], i + 2)
                    dve.wait_ge(same_in[b], i * 16 + 16)
                    v.tensor_tensor_scan(scalar_total[b][:, :], same[b][0:HEADS, :], scalar_ps[:, :],
                                         scalar_total[1 - b][:, ROWS - 1:ROWS], ALU.mult, ALU.add)
                    for h in range(HEADS):
                        last = v.tensor_tensor_scan(total[b][:, h, :], same[b][:, :], turned_ps[h][:, :],
                                                    total[1 - b][:, h, ROWS - 1:ROWS], ALU.mult, ALU.add)
                    link(last)
                    link.tell(scanned[b])
                    link.tell(same_used[b])

                def combine(i, b):
                    dve.wait_ge(sums_back, i * 2 + b + 2)
                    link(v.tensor_copy(wsum[:, :, :], scalar_back[:, :, :]))
                    link.tell(sums_used)
                    link(v.tensor_scalar(empty[:, :, :], wsum[:, :, :], 0.0, None, ALU.is_equal))
                    link(v.tensor_add(wsum[:, :, :], wsum[:, :, :], empty[:, :, :]))
                    link(v.reciprocal(winv[:, :, :], wsum[:, :, :]))
                    dve.wait_ge(scattered[b], i * 64 + 64)
                    v.tensor_scalar(out_rows[b][:, :, P:P + HEADS], empty[:, :, :], -1.0, 1.0, ALU.mult, ALU.add)
                    link(v.tensor_scalar(winv[:, :, :], winv[:, :, :], 1.0 / HEADS, None, ALU.mult))
                    for k in range(GT):
                        dve.wait_ge(product_ready[k % 2], i * 4 + b * 2 + k // 2 + 1)
                        o = out_rows[b][:, k, 0:P]
                        link(v.tensor_scalar(o, product[k % 2][:, 0, :], winv[:, k, 0:1], None, ALU.mult))
                        for h in range(1, HEADS):
                            link(v.scalar_tensor_tensor(o, product[k % 2][:, h, :], winv[:, k, h:h + 1], o, ALU.mult, ALU.add))
                        link.tell(product_used[k % 2])
                    link.tell(rows_ready[b])

                score(0, 0)
                link.restart()
                with v.Fori(0, STEPS - 1) as i:
                    scan(i, 0)
                    score(i, 1)
                    combine(i, 0)
                    scan(i, 1)
                    score(i + 1, 0)
                    combine(i, 1)
                    link.restart()
                scan(STEPS - 1, 0)
                score(STEPS - 1, 1)
                combine(STEPS - 1, 0)
                scan(STEPS - 1, 1)
                combine(STEPS - 1, 1)


def context_pass(nc, C, block_no, order, ctx_table, agents, sums, last_max):
    with Phase(nc, f"ctx{block_no}") as ph:
        rows, mine = ph.sb2("rows", [P, GT, 2 * P]), ph.sb2("mine", [P, GT, P])
        gather_index, target = ph.sb2("gather_index", [P, 3 * GT], I32), ph.sb2("target", [P, GT], I32)
        same = ph.sb2("same", [P, ROWS], BF16)
        prod = ph.sb("prod", [P, GT, P])
        c, ee = ph.sb2("c", [P, GT]), ph.sb2("ee", [P, GT])
        part_max, all_max, running = ph.sb("part_max", [P, 1]), ph.sb("all_max", [1, 1]), ph.sb("running", [1, 1])
        shift, neg_shift, fade = ph.sb2("shift", [P, 1]), ph.sb2("neg_shift", [P, 1]), ph.sb2("fade", [P, 1])
        begin, scalar_begin = ph.sb("begin", [P, 1]), ph.sb("scalar_begin", [1, 1])
        weighted = ph.sb2("weighted", [P, GT, P])
        total, scalar_total = ph.sb2("total", [P, ROWS]), ph.sb2("scalar_total", [1, ROWS])
        out_rows = ph.sb2("out_rows", [P, GT, SW])
        turned_ps, product = ph.ps2("turned_ps", [P, ROWS]), ph.ps2("product", [P, GT, P])
        scalar_ps, scalar_back = ph.ps("scalar_ps", [1, ROWS]), ph.ps("scalar_back", [P, GT])
        max_row, max_wide = ph.ps("max_row", [1, P]), ph.ps("max_wide", [P, 1])
        names = ("gather_index_in", "target_in", "same_in", "gathered", "scattered", "same_used", "shift_ready",
                 "weighted_ready", "turned", "scanned", "projected", "copied", "rows_ready")
        (gather_index_in, target_in, same_in, gathered, scattered, same_used, shift_ready,
         weighted_ready, turned, scanned, projected, copied, rows_ready) = (ph.sems2(x) for x in names)
        parts_ready, row_ready, max_ready, wide_ready = (ph.sem(x) for x in ("parts_ready", "row_ready", "max_ready", "wide_ready"))
        went_on, chain, chain_act = ph.sem("went_on"), ph.sem("chain"), ph.sem("chain_act")
        unit = 128
        with nc.Block() as block:
            edge_loaders(nc, order, block, Order.KEY, 3, gather_index, target, same, gather_index_in, target_in,
                         same_in, gathered, scattered, same_used, unit)

            def gathers(b):
                for k in range(GT):
                    gather(nc, rows[b][:, k, :], ctx_table, gather_index[b][:, 2 * GT + k:2 * GT + k + 1], gathered[b], CTX)
                    gather(nc, mine[b][:, k, :], agents, gather_index[b][:, k:k + 1], gathered[b], NP)

            edge_pool(nc, C, block, gathers, sums, out_rows, target, target_in, rows_ready, gathered, scattered,
                      gather_index_in, weighted_ready, went_on, unit)

            @block.vector
            def _(dve):
                v = nc.vector
                link = Chain(dve, chain)
                v.memset(total[1][:, ROWS - 1:ROWS], 0.0)
                v.memset(scalar_total[1][:, ROWS - 1:ROWS], 0.0)
                v.memset(running[:, :], -1e30)
                link(v.memset(shift[1][:, :], -1e30))
                link.restart()
                for b in range(2):
                    dve.sem_inc(scanned[b], 1)

                def score(i, b):
                    g = i * 2 + b
                    dve.wait_ge(gathered[b], i * unit + 2 * unit)
                    dve.wait_ge(copied[b], i + 1)
                    link(v.tensor_mul(prod[:, :, :], rows[b][:, :, 0:P], mine[b][:, :, :]))
                    link(v.tensor_reduce(c[b][:, :], prod[:, :, :], AX.X, ALU.add))
                    link(v.scalar_tensor_tensor(c[b][:, :], c[b][:, :], 0.1, c[b][:, :], ALU.mult, ALU.max))
                    link(v.tensor_add(c[b][:, :], c[b][:, :], order.pad_bias[:, ds(g * GT, GT)]))
                    link(v.tensor_reduce(part_max[:, :], c[b][:, :], AX.X, ALU.max))
                    link.tell(parts_ready)
                    dve.wait_ge(row_ready, g + 1)
                    link(v.tensor_reduce(all_max[:, :], max_row[:, :], AX.X, ALU.max))
                    link(v.tensor_tensor(running[:, :], running[:, :], all_max[:, :], ALU.max))
                    link.tell(max_ready)
                    dve.wait_ge(wide_ready, g + 1)
                    link(v.tensor_copy(shift[b][:, :], max_wide[:, :]))
                    link(v.tensor_scalar(neg_shift[b][:, :], shift[b][:, :], -1.0, None, ALU.mult))
                    link.tell(shift_ready[b])

                def scan(i, b):
                    dve.wait_ge(turned[b], i + 2)
                    dve.wait_ge(same_in[b], i * 16 + 16)
                    dve.wait_ge(projected[b], i + 1)
                    v.tensor_tensor(scalar_begin[:, :], scalar_total[1 - b][:, ROWS - 1:ROWS], fade[b][0:1, :], ALU.mult)
                    link(v.tensor_tensor(begin[:, :], total[1 - b][:, ROWS - 1:ROWS], fade[b][:, :], ALU.mult))
                    v.tensor_tensor_scan(scalar_total[b][:, :], same[b][0:1, :], scalar_ps[:, :], scalar_begin[:, :],
                                         ALU.mult, ALU.add)
                    link(v.tensor_tensor_scan(total[b][:, :], same[b][:, :], turned_ps[b][:, :], begin[:, :],
                                              ALU.mult, ALU.add))
                    link.tell(scanned[b])
                    link.tell(same_used[b])

                score(0, 0)
                link.restart()
                with v.Fori(0, STEPS - 1) as i:
                    scan(i, 0)
                    score(i, 1)
                    scan(i, 1)
                    score(i + 1, 0)
                    link.restart()
                scan(STEPS - 1, 0)
                score(STEPS - 1, 1)
                scan(STEPS - 1, 1)
                link(v.tensor_copy(last_max[:, :], shift[1][:, :]))

            @block.scalar
            def _(act):
                link = Chain(act, chain_act)
                for b in range(2):
                    act.sem_inc(weighted_ready[b], 1)
                    act.sem_inc(copied[b], 1)
                for b in range(2):
                    last = nc.scalar.copy(out_rows[b][:, :, P:SW], C.zeros[:, 0:GT * (SW - P)].rearrange("p (k c) -> p k c", k=GT))
                link(last)
                link.restart()

                def weigh(i, b):
                    act.wait_ge(shift_ready[b], i + 1)
                    act.wait_ge(turned[b], i + 1)
                    act.wait_ge(scanned[b], i + 1)
                    nc.scalar.activation(fade[b][:, :], shift[1 - b][:, :], ACT.Exp, bias=neg_shift[b][:, :])
                    link(nc.scalar.activation(ee[b][:, :], c[b][:, :], ACT.Exp, bias=neg_shift[b][:, :]))
                    for k in range(GT):
                        last = nc.scalar.activation(weighted[b][:, k, :], rows[b][:, k, P:2 * P], ACT.Copy,
                                                    scale=ee[b][:, k:k + 1])
                    link(last)
                    link.tell(weighted_ready[b])

                def copy_out(i, b):
                    act.wait_ge(projected[b], i + 2)
                    act.wait_ge(scattered[b], i * 64 + 64)
                    nc.scalar.activation(out_rows[b][:, :, P + 1], C.zeros[:, 0:GT], ACT.Identity, bias=shift[b][:, :])
                    nc.scalar.copy(out_rows[b][:, :, P], scalar_back[:, :])
                    link(nc.scalar.copy(out_rows[b][:, :, 0:P], product[b][:, :, :]))
                    link.tell(copied[b])
                    link.tell(rows_ready[b])

                weigh(0, 0)
                link.restart()
                with nc.scalar.Fori(0, STEPS - 1) as i:
                    copy_out(i, 0)
                    weigh(i, 1)
                    copy_out(i, 1)
                    weigh(i + 1, 0)
                    link.restart()
                copy_out(STEPS - 1, 0)
                weigh(STEPS - 1, 1)
                copy_out(STEPS - 1, 1)

            @block.tensor
            def _(pe):
                for b in range(2):
                    pe.sem_inc(turned[b], 1)
                    pe.sem_inc(projected[b], 1)

                def maxima(i, b):
                    g = i * 2 + b
                    pe.wait_ge(parts_ready, g + 1)
                    nc.tensor.transpose(max_row[:, :], part_max[:, :], C.ident[:, :]).then_inc(row_ready, 1)
                    pe.wait_ge(max_ready, g + 1)
                    nc.tensor.matmul(max_wide[:, :], C.ones[0:1, :], running[:, :], start=True, stop=True).then_inc(wide_ready, 1)

                def turn(i, b):
                    pe.wait_ge(weighted_ready[b], i + 2)
                    pe.wait_ge(scanned[b], i + 1)
                    pe.wait_ge(scanned[1 - b], i + 1 + b)
                    for k in range(GT):
                        nc.tensor.matmul(scalar_ps[:, k * P:(k + 1) * P], ee[b][:, k:k + 1], C.ident[:, :], start=True, stop=True)
                        last = nc.tensor.transpose(turned_ps[b][:, k * P:(k + 1) * P], weighted[b][:, k, :], C.ident[:, :])
                    last.then_inc(turned[b], 1)

                def project(i, b):
                    pe.wait_ge(scanned[b], i + 2)
                    pe.wait_ge(copied[b], i + 1)
                    pe.wait_ge(copied[1 - b], i + 1 + b)
                    for k in range(GT):
                        nc.tensor.matmul(product[b][:, k, :], total[b][:, k * P:(k + 1) * P], C.t[f"Wb{block_no}"][:, :],
                                         start=True, stop=True)
                        last = nc.tensor.matmul(scalar_back[:, k:k + 1], scalar_total[b][:, k * P:(k + 1) * P],
                                                C.ones[0:1, 0:1], start=True, stop=True)
                    last.then_inc(projected[b], 1)

                maxima(0, 0)
                with nc.tensor.Fori(0, STEPS - 1) as i:
                    turn(i, 0)
                    project(i, 0)
                    maxima(i, 1)
                    turn(i, 1)
                    project(i, 1)
                    maxima(i + 1, 0)
                turn(STEPS - 1, 0)
                project(STEPS - 1, 0)
                maxima(STEPS - 1, 1)
                turn(STEPS - 1, 1)
                project(STEPS - 1, 1)


class Norm:

    def __init__(self, nc, C, ph, per_step, name="ln"):
        self.nc, self.C, self.per_step = nc, C, per_step
        self.stats = ph.sb2(name + "_stats", [P, GT, 6])
        self.mean_var = ph.sb2(name + "_mean_var", [P, GT, 2])
        self.root = ph.sb2(name + "_root", [P, GT])
        self.inv = ph.sb2(name + "_inv", [P, GT])
        self.var_ready, self.root_ready = ph.sems2(name + "_var_ready"), ph.sems2(name + "_root_ready")

    def stats_dve(self, link, b, x):
        v = self.nc.vector
        for k in range(GT):
            last = v.bn_stats(self.stats[b][:, k, :], x[:, k, :])
        link(last)
        for k in range(GT):
            last = v.bn_aggr(self.mean_var[b][:, k, :], self.stats[b][:, k, :])
        link(last)
        link.tell(self.var_ready[b])

    def root_act(self, act, i, b, n=0, scale=1.0, eps=True):
        act.wait_ge(self.var_ready[b], i * self.per_step + n + 1)
        kw = {"bias": self.C.eps[:, :]} if eps else {}
        self.nc.scalar.activation(self.root[b][:, :], self.mean_var[b][:, :, 1], ACT.Sqrt, scale=scale,
                                  **kw).then_inc(self.root_ready[b], 1)

    def apply_dve(self, dve, link, i, b, x, y, n=0, add=0.0):
        v = self.nc.vector
        dve.wait_ge(self.root_ready[b], i * self.per_step + n + 1)
        if add:
            link(v.tensor_scalar(self.root[b][:, :], self.root[b][:, :], add, None, ALU.add))
        link(v.reciprocal(self.inv[b][:, :], self.root[b][:, :]))
        for k in range(GT):
            last = v.tensor_scalar(y[:, k, :], x[:, k, :], self.mean_var[b][:, k, 0:1], self.inv[b][:, k:k + 1],
                                   ALU.subtract, ALU.mult)
        link(last)


def spread(vec):
    return vec[:, :].rearrange("p (o d) -> p o d", o=1).to_broadcast([P, GT, P])


def node_steps(eng, body, peel):
    if peel:
        with eng.Fori(0, STEPS - 1) as i:
            body(i, False)
        body(STEPS - 1, True)
    else:
        with eng.Fori(0, STEPS) as i:
            body(i, False)


def load_x(sp, buf, x, i, b, last, sem):
    if last and b == 1:
        sp.dma_start(buf[0:LASTP, :, :], x[LASTG * ROWS:N, :].rearrange("(p k) d -> p k d", k=GT)).then_inc(sem, 16)
    else:
        v = x[0:LASTG * ROWS, :].rearrange("(g p k) d -> p g k d", p=P, k=GT)
        sp.dma_start(buf[:, :, :], v[:, ds(i * 2 + b, 1), :, :].rearrange("p o k d -> p (o k) d")).then_inc(sem, 16)


class NodePhase(Phase):

    def __init__(self, nc, C, name):
        super().__init__(nc, name)
        self.C = C
        self.loaded, self.used = self.sems2("loaded"), self.sems2("used")
        self.done, self.stored = self.sems2("done"), self.sems2("stored")
        self.chain, self.chain_act, self.went_on = self.sem("chain"), self.sem("chain_act"), self.sem("went_on")

    def storer(self, block, stores, count, peel=False):
        nc = self.nc

        @block.gpsimd
        def _(pool):
            for b in range(2):
                nc.gpsimd.dma_start(self.C.credit[b:b + 1, :], self.C.eps[0:1, :]).then_inc(self.stored[b], 16 * count)

            def body(i, last):
                for b in range(2):
                    pool_wait(pool, self.done[b], i + 1, self.went_on)
                    for to, of in stores(i, b, last):
                        nc.gpsimd.dma_start(to, of).then_inc(self.stored[b], 16)
            node_steps(nc.gpsimd, body, peel)
            for b in range(2):
                pool.wait_ge(self.stored[b], 16 * count * (STEPS + 1))


def norm_input(nc, C, x, h_out):
    with NodePhase(nc, C, "n0") as ph:
        X, Y, H = (ph.sb2(n, [P, GT, P]) for n in "XYH")
        norm = Norm(nc, C, ph, 1)
        applied = ph.sems2("applied")
        with nc.Block() as block:
            @block.sync
            def _(sp):
                def body(i, last):
                    for b in range(2):
                        sp.wait_ge(ph.used[b], i + 1)
                        load_x(sp, X[b], x, i, b, last, ph.loaded[b])
                node_steps(nc.sync, body, True)

            @block.vector
            def _(dve):
                link = Chain(dve, ph.chain)
                for b in range(2):
                    link(nc.vector.memset(X[b][:, :, :], 0.0))
                    link.tell(ph.used[b])
                link.restart()
                with nc.vector.Fori(0, STEPS) as i:
                    for b in range(2):
                        dve.wait_ge(ph.loaded[b], i * 16 + 16)
                        norm.stats_dve(link, b, X[b])
                    for b in range(2):
                        dve.wait_ge(ph.done[b], i + 1)
                        norm.apply_dve(dve, link, i, b, X[b], Y[b])
                        link.tell(ph.used[b])
                        link.tell(applied[b])
                    link.restart()

            @block.scalar
            def _(act):
                link = Chain(act, ph.chain_act)
                for b in range(2):
                    act.sem_inc(ph.done[b], 1)
                with nc.scalar.Fori(0, STEPS) as i:
                    for b in range(2):
                        norm.root_act(act, i, b)
                    for b in range(2):
                        act.wait_ge(applied[b], i + 1)
                        act.wait_ge(ph.stored[b], i * 16 + 16)
                        link(nc.scalar.activation(H[b][:, :, :], Y[b][:, :, :], ACT.Relu))
                        link.tell(ph.done[b])
                    link.restart()

            @block.gpsimd
            def _(pool):
                for b in range(2):
                    nc.gpsimd.dma_start(C.credit[b:b + 1, :], C.eps[0:1, :]).then_inc(ph.stored[b], 16)
                with nc.gpsimd.Fori(0, STEPS) as i:
                    for b in range(2):
                        pool_wait(pool, ph.done[b], i + 2, ph.went_on)
                        nc.gpsimd.dma_start(group_rows(h_out, i * 2 + b), H[b][:, :, :]).then_inc(ph.stored[b], 16)
                for b in range(2):
                    pool.wait_ge(ph.stored[b], 16 * (STEPS + 1))


def sage_nodes(nc, C, x, h, sums, x_out, h_out):
    with NodePhase(nc, C, "n1") as ph:
        X, X1, H, HT, Y, H1 = (ph.sb2(n, [P, GT, P]) for n in ("X", "X1", "H", "HT", "Y", "H1"))
        S = ph.sb2("S", [P, GT, SW])
        inv, own = ph.sb2("inv", [P, GT]), ph.sb2("own", [P, GT])
        tp, po = ph.ps2("tp", [P, GT, P]), ph.ps2("po", [P, GT, 2, P])
        norm = Norm(nc, C, ph, 1)
        turned, moved, product, applied = (ph.sems2(n) for n in ("turned", "moved", "product", "applied"))
        with nc.Block() as block:
            @block.sync
            def _(sp):
                def body(i, last):
                    for b in range(2):
                        sp.wait_ge(ph.used[b], i + 1)
                        load_x(sp, X[b], x, i, b, last, ph.loaded[b])
                        sp.dma_start(S[b][:, :, :], group_rows(sums, i * 2 + b)).then_inc(ph.loaded[b], 16)
                        sp.dma_start(H[b][:, :, :], group_rows(h, i * 2 + b)).then_inc(ph.loaded[b], 16)
                node_steps(nc.sync, body, True)

            @block.tensor
            def _(pe):
                with nc.tensor.Fori(0, STEPS) as i:
                    for b in range(2):
                        pe.wait_ge(ph.loaded[b], i * 48 + 48)
                        for k in range(GT):
                            last = nc.tensor.transpose(tp[b][:, k, :], H[b][:, k, :], C.ident[:, :])
                        last.then_inc(turned[b], 1)
                    for b in range(2):
                        pe.wait_ge(moved[b], i + 1)
                        pe.wait_ge(ph.used[b], i + 1)
                        for k in range(GT):
                            last = nc.tensor.matmul(po[b][:, k, :, :].rearrange("p a d -> p (a d)"), HT[b][:, k, :],
                                                    C.wlr[:, :, :].rearrange("p a d -> p (a d)"), start=True, stop=True)
                        last.then_inc(product[b], 1)

            @block.vector
            def _(dve):
                v = nc.vector
                link = Chain(dve, ph.chain)
                for b in range(2):
                    link(v.memset(X[b][:, :, :], 0.0))
                    link.tell(ph.used[b])
                link.restart()
                with v.Fori(0, STEPS) as i:
                    for b in range(2):
                        dve.wait_ge(ph.loaded[b], i * 48 + 48)
                        link(v.tensor_scalar(inv[b][:, :], S[b][:, :, P], 1.0, None, ALU.max))
                        link(v.reciprocal(inv[b][:, :], inv[b][:, :]))
                        v.tensor_scalar(own[b][:, :], S[b][:, :, P], 0.0, -1.0, ALU.is_gt, ALU.mult)
                        dve.wait_ge(ph.stored[b], i * 32 + 32)
                        link(v.tensor_add(X1[b][:, :, :], X[b][:, :, :], spread(C.v["bl"])))
                        for k in range(GT):
                            last = v.scalar_tensor_tensor(X1[b][:, k, :], S[b][:, k, 0:P], inv[b][:, k:k + 1], X1[b][:, k, :],
                                                          ALU.mult, ALU.add)
                        link(last)
                        dve.wait_ge(product[b], i + 1)
                        for k in range(GT):
                            last = v.scalar_tensor_tensor(X1[b][:, k, :], po[b][:, k, 0, :], own[b][:, k:k + 1], X1[b][:, k, :],
                                                          ALU.mult, ALU.add)
                        link(last)
                        link(v.tensor_add(X1[b][:, :, :], X1[b][:, :, :], po[b][:, :, 1, :]))
                        link.tell(ph.used[b])
                        norm.stats_dve(link, b, X1[b])
                    for b in range(2):
                        norm.apply_dve(dve, link, i, b, X1[b], Y[b])
                        link.tell(applied[b])
                    link.restart()

            @block.scalar
            def _(act):
                link = Chain(act, ph.chain_act)
                with nc.scalar.Fori(0, STEPS) as i:
                    for b in range(2):
                        act.wait_ge(turned[b], i + 1)
                        nc.scalar.copy(HT[b][:, :, :], tp[b][:, :, :]).then_inc(moved[b], 1)
                    for b in range(2):
                        norm.root_act(act, i, b)
                    for b in range(2):
                        act.wait_ge(applied[b], i + 1)
                        act.wait_ge(ph.stored[b], i * 32 + 32)
                        link(nc.scalar.activation(H1[b][:, :, :], Y[b][:, :, :], ACT.Relu))
                        link.tell(ph.done[b])
                    link.restart()

            ph.storer(block, lambda i, b, last: ((group_rows(x_out, i * 2 + b), X1[b][:, :, :]),
                                                 (group_rows(h_out, i * 2 + b), H1[b][:, :, :])), 2)


def hyper_rows(nc, C, name, sums, e_out, affine):
    steps = HGROUPS // 2
    with NodePhase(nc, C, name) as ph:
        S, E = ph.sb2("S", [P, GT, SW]), ph.sb2("E", [P, GT, P + 1])
        inv, has = ph.sb2("inv", [P, GT]), ph.sb2("has", [P, GT])
        with nc.Block() as block:
            @block.sync
            def _(sp):
                for b in range(2):
                    sp.sem_inc(ph.used[b], 1)
                with nc.sync.Fori(0, steps) as i:
                    for b in range(2):
                        sp.wait_ge(ph.used[b], i + 1)
                        sp.dma_start(S[b][:, :, :], group_rows(sums, i * 2 + b)).then_inc(ph.loaded[b], 16)

            @block.vector
            def _(dve):
                v = nc.vector
                link = Chain(dve, ph.chain)
                with v.Fori(0, steps) as i:
                    for b in range(2):
                        dve.wait_ge(ph.loaded[b], i * 16 + 16)
                        v.tensor_scalar(has[b][:, :], S[b][:, :, P], 0.0, None, ALU.is_gt)
                        link(v.tensor_scalar(inv[b][:, :], S[b][:, :, P], 1.0, None, ALU.max))
                        link(v.reciprocal(inv[b][:, :], inv[b][:, :]))
                        dve.wait_ge(ph.stored[b], i * 16 + 16)
                        v.tensor_copy(E[b][:, :, P], C.hw[:, ds(i * 2 + b, 1), :].rearrange("p o k -> p (o k)"))
                        for k in range(GT):
                            last = v.tensor_scalar(E[b][:, k, 0:P], S[b][:, k, 0:P], inv[b][:, k:k + 1], None, ALU.mult)
                        link(last)
                        if affine:
                            link(v.tensor_mul(E[b][:, :, 0:P], E[b][:, :, 0:P], spread(C.bn_scale)))
                            for k in range(GT):
                                last = v.scalar_tensor_tensor(E[b][:, k, 0:P], C.bn_bias[:, :], has[b][:, k:k + 1],
                                                              E[b][:, k, 0:P], ALU.mult, ALU.add)
                            link(last)
                        link.tell(ph.used[b])
                        link.tell(ph.done[b])
                    link.restart()

            @block.gpsimd
            def _(pool):
                for b in range(2):
                    nc.gpsimd.dma_start(C.credit[b:b + 1, :], C.eps[0:1, :]).then_inc(ph.stored[b], 16)
                with nc.gpsimd.Fori(0, steps) as i:
                    for b in range(2):
                        pool_wait(pool, ph.done[b], i + 1, ph.went_on)
                        nc.gpsimd.dma_start(group_rows(e_out, i * 2 + b), E[b][:, :, :]).then_inc(ph.stored[b], 16)
                for b in range(2):
                    pool.wait_ge(ph.stored[b], 16 * (steps + 1))


def inverse_degree(link, v, d, one, inv):
    link(v.tensor_scalar(one, d, 0.0, None, ALU.is_gt))
    link(v.tensor_tensor(inv, d, one, ALU.mult))
    link(v.scalar_tensor_tensor(inv, one, -1.0, inv, ALU.mult, ALU.add))
    link(v.tensor_scalar(inv, inv, 1.0, None, ALU.add))
    link(v.reciprocal(inv, inv))
    link(v.tensor_tensor(inv, inv, one, ALU.mult))


def hyper_nodes1(nc, C, sums, g_out):
    with NodePhase(nc, C, "n3") as ph:
        S, G, Q = ph.sb2("S", [P, GT, SW]), ph.sb2("G", [P, GT, P]), ph.sb2("Q", [P, GT, P])
        one, inv = ph.sb2("one", [P, GT]), ph.sb2("inv", [P, GT])
        sum_ps, square_ps = ph.ps("sum_ps", [1, ROWS]), ph.ps("square_ps", [1, ROWS])
        wide_ps = ph.ps("wide_ps", [P, 2, P])
        part = ph.sb("part", [1, 2, ROWS])
        mean, second, var, row = ph.sb("mean", [1, P]), ph.sb("second", [1, P]), ph.sb("var", [1, P]), ph.sb("row", [1, 2, P])
        summed = ph.sems2("summed")
        squared = ph.sems2("squared")
        all_summed, var_ready, root_ready, row_ready, wide_ready = (ph.sem(n) for n in (
            "all_summed", "var_ready", "root_ready", "row_ready", "wide_ready"))
        with nc.Block() as block:
            @block.sync
            def _(sp):
                for b in range(2):
                    sp.sem_inc(ph.used[b], 1)
                with nc.sync.Fori(0, STEPS) as i:
                    for b in range(2):
                        sp.wait_ge(ph.used[b], i + 1)
                        sp.dma_start(S[b][:, :, :], group_rows(sums, i * 2 + b)).then_inc(ph.loaded[b], 16)

            @block.vector
            def _(dve):
                v = nc.vector
                link = Chain(dve, ph.chain)
                with v.Fori(0, STEPS) as i:
                    for b in range(2):
                        dve.wait_ge(ph.loaded[b], i * 16 + 16)
                        inverse_degree(link, v, S[b][:, :, P], one[b][:, :], inv[b][:, :])
                        dve.wait_ge(ph.stored[b], i * 16 + 16)
                        dve.wait_ge(summed[b], i + 1)
                        for k in range(GT):
                            last = v.tensor_scalar(G[b][:, k, :], S[b][:, k, 0:P], inv[b][:, k:k + 1], None, ALU.mult)
                        link(last)
                        link.tell(ph.used[b])
                        link.tell(ph.done[b])
                    link.restart()
                dve.wait_ge(all_summed, 1)
                v.tensor_copy(part[:, 0, :], sum_ps[:, :])
                link(v.tensor_copy(part[:, 1, :], square_ps[:, :]))
                for j, to in enumerate((mean, second)):
                    link(v.tensor_add(part[:, j, 0:2 * P], part[:, j, 0:2 * P], part[:, j, 2 * P:4 * P]))
                    link(v.tensor_add(part[:, j, 0:P], part[:, j, 0:P], part[:, j, P:2 * P]))
                    link(v.tensor_scalar(to[:, :], part[:, j, 0:P], 1.0 / N, None, ALU.mult))
                link(v.tensor_mul(var[:, :], mean[:, :], mean[:, :]))
                link(v.tensor_sub(var[:, :], second[:, :], var[:, :]))
                link(v.tensor_scalar(var[:, :], var[:, :], 0.0, None, ALU.max))
                link.tell(var_ready)
                dve.wait_ge(root_ready, 1)
                link(v.reciprocal(var[:, :], var[:, :]))
                link(v.tensor_mul(row[:, 0, :], var[:, :], C.v["gamma"][0:1, :]))
                link(v.tensor_mul(mean[:, :], mean[:, :], row[:, 0, :]))
                link(v.tensor_sub(row[:, 1, :], C.v["beta"][0:1, :], mean[:, :]))
                link.tell(row_ready)
                dve.wait_ge(wide_ready, 1)
                v.tensor_copy(C.bn_scale[:, :], wide_ps[:, 0, :])
                link(v.tensor_copy(C.bn_bias[:, :], wide_ps[:, 1, :]))

            @block.scalar
            def _(act):
                with nc.scalar.Fori(0, STEPS) as i:
                    for b in range(2):
                        act.wait_ge(ph.done[b], i + 1)
                        act.wait_ge(summed[b], i + 1)
                        nc.scalar.activation(Q[b][:, :, :], G[b][:, :, :], ACT.Square).then_inc(squared[b], 1)
                act.wait_ge(var_ready, 1)
                nc.scalar.activation(var[:, :], var[:, :], ACT.Sqrt, bias=C.eps[0:1, :]).then_inc(root_ready, 1)

            @block.tensor
            def _(pe):
                for b in range(2):
                    pe.sem_inc(summed[b], 1)
                z = C.zeros[:, 0:1]
                for o in (sum_ps, square_ps):
                    for k in range(GT):
                        nc.tensor.matmul(o[:, k * P:(k + 1) * P], z, C.zeros[:, :], start=(k == 0), stop=False,
                                         skip_group_check=True)
                with nc.tensor.Fori(0, STEPS) as i:
                    for b in range(2):
                        pe.wait_ge(squared[b], i + 1)
                        nc.tensor.matmul(sum_ps[:, :], C.ones[:, 0:1], G[b][:, :, :].rearrange("p k d -> p (k d)"),
                                         start=False, stop=False, skip_group_check=True)
                        nc.tensor.matmul(square_ps[:, :], C.ones[:, 0:1], Q[b][:, :, :].rearrange("p k d -> p (k d)"),
                                         start=False, stop=False, skip_group_check=True).then_inc(summed[b], 1)
                for o in (sum_ps, square_ps):
                    last = nc.tensor.matmul(o[:, 0:P], z, C.zeros[:, :], start=False, stop=True, skip_group_check=True)
                last.then_inc(all_summed, 1)
                pe.wait_ge(row_ready, 1)
                nc.tensor.matmul(wide_ps[:, :, :].rearrange("p a d -> p (a d)"), C.ones[0:1, :],
                                 row[:, :, :].rearrange("p a d -> p (a d)"), start=True, stop=True).then_inc(wide_ready, 1)

            ph.storer(block, lambda i, b, last: ((group_rows(g_out, i * 2 + b), G[b][:, :, :]),), 1)


def hyper_nodes2(nc, C, x, sums, x_out, h_out, score_out):
    with NodePhase(nc, C, "n4") as ph:
        X, X2, HT, Y = (ph.sb2(n, [P, GT, P]) for n in ("X", "X2", "HT", "Y"))
        S, H = ph.sb2("S", [P, GT, SW]), ph.sb2("H", [P, GT, P + HEADS])
        scores = ph.sb2("scores", [P, GT, HEADS])
        one, inv = ph.sb2("one", [P, GT]), ph.sb2("inv", [P, GT])
        tp, sp_ps = ph.ps2("tp", [P, GT, P]), ph.ps2("scores_ps", [P, GT, 2 * HEADS])
        norm = Norm(nc, C, ph, 1)
        turned, moved, product, applied, relued = (ph.sems2(n) for n in ("turned", "moved", "product", "applied", "relued"))
        with nc.Block() as block:
            @block.sync
            def _(sp):
                for b in range(2):
                    sp.sem_inc(ph.used[b], 1)
                with nc.sync.Fori(0, STEPS) as i:
                    for b in range(2):
                        sp.wait_ge(ph.used[b], i + 1)
                        sp.dma_start(X[b][:, :, :], group_rows(x, i * 2 + b)).then_inc(ph.loaded[b], 16)
                        sp.dma_start(S[b][:, :, :], group_rows(sums, i * 2 + b)).then_inc(ph.loaded[b], 16)

            @block.vector
            def _(dve):
                v = nc.vector
                link = Chain(dve, ph.chain)
                with v.Fori(0, STEPS) as i:
                    for b in range(2):
                        dve.wait_ge(ph.loaded[b], i * 32 + 32)
                        inverse_degree(link, v, S[b][:, :, P], one[b][:, :], inv[b][:, :])
                        dve.wait_ge(ph.stored[b], i * 48 + 48)
                        link(v.tensor_add(X2[b][:, :, :], X[b][:, :, :], spread(C.v["b2"])))
                        for k in range(GT):
                            last = v.scalar_tensor_tensor(X2[b][:, k, :], S[b][:, k, 0:P], inv[b][:, k:k + 1], X2[b][:, k, :],
                                                          ALU.mult, ALU.add)
                        link(last)
                        link.tell(ph.used[b])
                        norm.stats_dve(link, b, X2[b])
                    for b in range(2):
                        norm.apply_dve(dve, link, i, b, X2[b], Y[b])
                        link.tell(applied[b])
                    for b in range(2):
                        dve.wait_ge(product[b], i + 1)
                        for k in range(GT):
                            v.tensor_add(scores[b][:, k, :], sp_ps[b][:, k, 0:HEADS], C.score_b[:, 0:HEADS])
                            last = v.tensor_add(H[b][:, k, P:P + HEADS], sp_ps[b][:, k, HEADS:2 * HEADS],
                                                C.score_b[:, HEADS:2 * HEADS])
                        link(last)
                        link.tell(ph.done[b])
                    link.restart()

            @block.scalar
            def _(act):
                with nc.scalar.Fori(0, STEPS) as i:
                    for b in range(2):
                        norm.root_act(act, i, b)
                    for b in range(2):
                        act.wait_ge(applied[b], i + 1)
                        act.wait_ge(ph.stored[b], i * 48 + 48)
                        nc.scalar.activation(H[b][:, :, 0:P], Y[b][:, :, :], ACT.Relu).then_inc(relued[b], 1)
                    for b in range(2):
                        act.wait_ge(turned[b], i + 1)
                        nc.scalar.copy(HT[b][:, :, :], tp[b][:, :, :]).then_inc(moved[b], 1)

            @block.tensor
            def _(pe):
                with nc.tensor.Fori(0, STEPS) as i:
                    for b in range(2):
                        pe.wait_ge(relued[b], i + 1)
                        for k in range(GT):
                            last = nc.tensor.transpose(tp[b][:, k, :], H[b][:, k, 0:P], C.ident[:, :])
                        last.then_inc(turned[b], 1)
                    for b in range(2):
                        pe.wait_ge(moved[b], i + 1)
                        for k in range(GT):
                            last = nc.tensor.matmul(sp_ps[b][:, k, :], HT[b][:, k, :], C.score_w[:, :], start=True, stop=True)
                        last.then_inc(product[b], 1)

            ph.storer(block, lambda i, b, last: ((group_rows(x_out, i * 2 + b), X2[b][:, :, :]),
                                                 (group_rows(h_out, i * 2 + b), H[b][:, :, :]),
                                                 (group_rows(score_out, i * 2 + b), scores[b][:, :, :])), 3)


def attention_nodes(nc, C, x, h, sums, x_out, h_out):
    with NodePhase(nc, C, "n5") as ph:
        X, X3, H, HT, A, Y, R = (ph.sb2(n, [P, GT, P]) for n in ("X", "X3", "H", "HT", "A", "Y", "R"))
        H3 = ph.sb2("H3", [P, GT, P])
        S = ph.sb2("S", [P, GT, SW])
        empty = ph.sb2("empty", [P, GT, HEADS])
        tp, out_ps = ph.ps2("tp", [P, GT, P]), ph.ps2("out_ps", [P, GT, P])
        heads_ps = [ph.ps(f"heads_ps{k}", [P, HEADS, P]) for k in range(GT)]
        norm = Norm(nc, C, ph, 2)
        turned, moved, product, applied, relued = (ph.sems2(n) for n in ("turned", "moved", "product", "applied", "relued"))
        heads_ready, heads_used = ph.sem("heads_ready"), ph.sem("heads_used")
        with nc.Block() as block:
            @block.sync
            def _(sp):
                for b in range(2):
                    sp.sem_inc(ph.used[b], 1)
                with nc.sync.Fori(0, STEPS) as i:
                    for b in range(2):
                        sp.wait_ge(ph.used[b], i + 1)
                        sp.dma_start(X[b][:, :, :], group_rows(x, i * 2 + b)).then_inc(ph.loaded[b], 16)
                        sp.dma_start(S[b][:, :, :], group_rows(sums, i * 2 + b)).then_inc(ph.loaded[b], 16)
                        sp.dma_start(H[b][:, :, :], group_rows(h, i * 2 + b, 0, P)).then_inc(ph.loaded[b], 16)

            @block.tensor
            def _(pe):
                pe.sem_inc(heads_used, 1)
                with nc.tensor.Fori(0, STEPS) as i:
                    for b in range(2):
                        pe.wait_ge(ph.loaded[b], i * 48 + 48)
                        for k in range(GT):
                            last = nc.tensor.transpose(tp[b][:, k, :], H[b][:, k, :], C.ident[:, :])
                        last.then_inc(turned[b], 1)
                    for b in range(2):
                        pe.wait_ge(moved[b], i * 2 + 1)
                        pe.wait_ge(heads_used, i * 2 + b + 1)
                        for k in range(GT):
                            last = nc.tensor.matmul(heads_ps[k][:, :, :].rearrange("p a d -> p (a d)"), HT[b][:, k, :],
                                                    C.heads[:, :, :].rearrange("p a d -> p (a d)"), start=True, stop=True)
                        last.then_inc(heads_ready, 1)
                    for b in range(2):
                        pe.wait_ge(relued[b], i + 1)
                        for k in range(GT):
                            last = nc.tensor.transpose(tp[b][:, k, :], R[b][:, k, :], C.ident[:, :])
                        last.then_inc(turned[b], 1)
                    for b in range(2):
                        pe.wait_ge(moved[b], i * 2 + 2)
                        for k in range(GT):
                            last = nc.tensor.matmul(out_ps[b][:, k, :], HT[b][:, k, :], C.t["V"][:, :], start=True, stop=True)
                        last.then_inc(product[b], 1)

            @block.vector
            def _(dve):
                v = nc.vector
                link = Chain(dve, ph.chain)
                with v.Fori(0, STEPS) as i:
                    for b in range(2):
                        dve.wait_ge(ph.loaded[b], i * 48 + 48)
                        v.tensor_scalar(empty[b][:, :, :], S[b][:, :, P:P + HEADS], -1.0 / HEADS, 1.0 / HEADS, ALU.mult, ALU.add)
                        link(v.tensor_add(A[b][:, :, :], S[b][:, :, 0:P], spread(C.mean_b)))
                        dve.wait_ge(heads_ready, i * 2 + b + 1)
                        for a in range(HEADS):
                            for k in range(GT):
                                last = v.scalar_tensor_tensor(A[b][:, k, :], heads_ps[k][:, a, :], empty[b][:, k, a:a + 1],
                                                              A[b][:, k, :], ALU.mult, ALU.add)
                            link(last)
                        link.tell(heads_used)
                        norm.stats_dve(link, b, A[b])
                    for b in range(2):
                        norm.apply_dve(dve, link, i, b, A[b], Y[b], n=0, add=1e-6)
                        link(v.tensor_mul(Y[b][:, :, :], Y[b][:, :, :], spread(C.v["ln_g"])))
                        link(v.tensor_add(Y[b][:, :, :], Y[b][:, :, :], spread(C.v["ln_b"])))
                        link.tell(applied[b])
                        dve.wait_ge(ph.stored[b], i * 32 + 32)
                        link(v.tensor_add(X3[b][:, :, :], X[b][:, :, :], spread(C.v["Vb"])))
                        link.tell(ph.used[b])
                    for b in range(2):
                        dve.wait_ge(product[b], i + 1)
                        link(v.tensor_add(X3[b][:, :, :], X3[b][:, :, :], out_ps[b][:, :, :]))
                        norm.stats_dve(link, b, X3[b])
                    for b in range(2):
                        norm.apply_dve(dve, link, i, b, X3[b], Y[b], n=1)
                        link.tell(applied[b])
                    link.restart()

            @block.scalar
            def _(act):
                link = Chain(act, ph.chain_act)
                with nc.scalar.Fori(0, STEPS) as i:
                    for b in range(2):
                        act.wait_ge(turned[b], i * 2 + 1)
                        nc.scalar.copy(HT[b][:, :, :], tp[b][:, :, :]).then_inc(moved[b], 1)
                    for b in range(2):
                        norm.root_act(act, i, b, n=0, scale=P / (P - 1.0), eps=False)
                    for b in range(2):
                        act.wait_ge(applied[b], i * 2 + 1)
                        nc.scalar.activation(R[b][:, :, :], Y[b][:, :, :], ACT.Relu).then_inc(relued[b], 1)
                    for b in range(2):
                        act.wait_ge(turned[b], i * 2 + 2)
                        nc.scalar.copy(HT[b][:, :, :], tp[b][:, :, :]).then_inc(moved[b], 1)
                    for b in range(2):
                        norm.root_act(act, i, b, n=1)
                    for b in range(2):
                        act.wait_ge(applied[b], i * 2 + 2)
                        act.wait_ge(ph.stored[b], i * 32 + 32)
                        link(nc.scalar.activation(H3[b][:, :, :], Y[b][:, :, :], ACT.Relu))
                        link.tell(ph.done[b])
                    link.restart()

            ph.storer(block, lambda i, b, last: ((group_rows(x_out, i * 2 + b), X3[b][:, :, :]),
                                                 (group_rows(h_out, i * 2 + b), H3[b][:, :, :])), 2)


def context_tables(nc, C, context, tables):
    full = CTX // P
    rest = CTX - full * P
    with Phase(nc, "ctxt") as ph:
        X = ph.sb("X", [P, CTILES, P])
        XC, XT = ph.sb("XC", [P, P]), ph.sb("XT", [P, P])
        T = ph.sb("T", [P, CTILES, 2, 2, P])
        stats, pair, work = ph.sb("stats", [P, 2, 6]), ph.sb("pair", [P, 2, 2]), ph.sb("work", [P, 2, P])
        mean_var, root = ph.sb("mean_var", [P, CTILES, 2, 2]), ph.sb("root", [P, CTILES, 2])
        tp, po = ph.ps("tp", [P, P]), ph.ps("po", [P, 2, 2, P])
        loaded, cleared, fetched, turned, moved, product, copied, var_ready, root_ready, done, stored, chain = (
            ph.sem(n) for n in ("loaded", "cleared", "fetched", "turned", "moved", "product", "copied", "var_ready",
                                "root_ready", "done", "stored", "chain"))
        with nc.Block() as block:
            @block.sync
            def _(sp):
                sp.wait_ge(cleared, 1)
                sp.dma_start(X[:, 0:full, :], context[0:full * P, :].rearrange("(t p) d -> p t d", p=P)).then_inc(loaded, 16)
                sp.dma_start(X[0:rest, full, :], context[full * P:CTX, :]).then_inc(loaded, 16)
                sp.wait_ge(done, 1)
                for k in range(2):
                    sp.dma_start(tables[k][0:full * P, :].rearrange("(t p) c -> p t c", p=P),
                                 T[:, 0:full, k, :, :].rearrange("p t a d -> p t (a d)")).then_inc(stored, 16)
                    sp.dma_start(tables[k][full * P:CTX, :], T[0:rest, full, k, :, :].rearrange("p a d -> p (a d)")).then_inc(stored, 16)
                sp.wait_ge(stored, 64)

            @block.tensor
            def _(pe):
                with nc.tensor.Fori(0, CTILES) as t:
                    pe.wait_ge(fetched, t + 1)
                    nc.tensor.transpose(tp[:, :], XC[:, :], C.ident[:, :]).then_inc(turned, 1)
                    pe.wait_ge(moved, t + 1)
                    nc.tensor.matmul(po[:, :, :, :].rearrange("p k a d -> p (k a d)"), XT[:, :],
                                     C.ctxw[:, :, :, :].rearrange("p k a d -> p (k a d)"), start=True, stop=True).then_inc(product, 1)

            @block.scalar
            def _(act):
                act.wait_ge(loaded, 32)
                with nc.scalar.Fori(0, CTILES) as t:
                    nc.scalar.copy(XC[:, :], X[:, ds(t, 1), :].rearrange("p o d -> p (o d)")).then_inc(fetched, 1)
                    act.wait_ge(turned, t + 1)
                    nc.scalar.copy(XT[:, :], tp[:, :]).then_inc(moved, 1)
                    act.wait_ge(product, t + 1)
                    nc.scalar.copy(T[:, ds(t, 1), :, :, :].rearrange("p o k a d -> p (o k a d)"),
                                   po[:, :, :, :].rearrange("p k a d -> p (k a d)")).then_inc(copied, 1)
                    act.wait_ge(copied, t + 1)
                act.wait_ge(var_ready, 1)
                nc.scalar.activation(root[:, :, :], mean_var[:, :, :, 1], ACT.Sqrt, bias=C.eps[:, :]).then_inc(root_ready, 1)

            @block.vector
            def _(dve):
                v = nc.vector
                link = Chain(dve, chain)
                link(v.memset(X[:, :, :], 0.0))
                link.tell(cleared)
                link.restart()

                def projected(t, k):
                    return T[:, ds(t, 1), k, 1, :].rearrange("p o d -> p (o d)")

                with v.Fori(0, CTILES) as t:
                    dve.wait_ge(copied, t + 1)
                    for k in range(2):
                        last = v.bn_stats(stats[:, k, :], projected(t, k))
                    link(last)
                    for k in range(2):
                        last = v.bn_aggr(pair[:, k, :], stats[:, k, :])
                    link(last)
                    link(v.tensor_copy(mean_var[:, ds(t, 1), :, :].rearrange("p o k c -> p (o k) c"), pair[:, :, :]))
                    link.restart()
                link.tell(var_ready)
                dve.wait_ge(root_ready, 1)
                link(v.reciprocal(root[:, :, :], root[:, :, :]))
                link.restart()
                with v.Fori(0, CTILES) as t:
                    link(v.tensor_copy(pair[:, :, 0], mean_var[:, ds(t, 1), :, 0].rearrange("p o k -> p (o k)")))
                    link(v.tensor_copy(pair[:, :, 1], root[:, ds(t, 1), :].rearrange("p o k -> p (o k)")))
                    for k in range(2):
                        link(v.tensor_scalar(work[:, k, :], projected(t, k), pair[:, k, 0:1], pair[:, k, 1:2],
                                             ALU.subtract, ALU.mult))
                        link(v.tensor_mul(work[:, k, :], work[:, k, :], C.v[f"gnc_w{k}"][:, :]))
                        link(v.tensor_add(projected(t, k), work[:, k, :], C.v[f"gnc_b{k}"][:, :]))
                    link.restart()
                link.tell(done)


def agent_nodes(nc, C, block_no, agents, sums, last_max, agents_out, x, out):
    final = out is not None
    loads = 3 if final else 2
    with NodePhase(nc, C, f"n6{block_no}") as ph:
        A, AT, Y, Z, R, O = (ph.sb2(n, [P, GT, P]) for n in ("A", "AT", "Y", "Z", "R", "O"))
        S = ph.sb2("S", [P, GT, SW])
        X, F = (ph.sb2("X", [P, GT, P]), ph.sb2("F", [P, GT, P])) if final else (None, None)
        low, fade, share = ph.sb2("low", [P, GT]), ph.sb2("fade", [P, GT]), ph.sb2("share", [P, GT])
        neg_max = ph.sb("neg_max", [P, 1])
        tp, own_ps, lin_ps = ph.ps2("tp", [P, GT, P]), ph.ps2("own_ps", [P, GT, P]), ph.ps2("lin_ps", [P, GT, P])
        norm = Norm(nc, C, ph, 3)
        turned, moved, product, applied, relued, faded, low_ready = (ph.sems2(n) for n in (
            "turned", "moved", "product", "applied", "relued", "faded", "low_ready"))
        added = ph.sems2("added")
        with nc.Block() as block:
            @block.sync
            def _(sp):
                for b in range(2):
                    sp.sem_inc(ph.used[b], 1)

                def body(i, last):
                    for b in range(2):
                        sp.wait_ge(ph.used[b], i + 1)
                        sp.dma_start(A[b][:, :, :], group_rows(agents, i * 2 + b)).then_inc(ph.loaded[b], 16)
                        sp.dma_start(S[b][:, :, :], group_rows(sums, i * 2 + b)).then_inc(ph.loaded[b], 16)
                        if final:
                            sp.dma_start(X[b][:, :, :], group_rows(x, i * 2 + b)).then_inc(ph.loaded[b], 16)
                node_steps(nc.sync, body, False)

            @block.tensor
            def _(pe):
                with nc.tensor.Fori(0, STEPS) as i:
                    for b in range(2):
                        pe.wait_ge(ph.loaded[b], i * 16 * loads + 16 * loads)
                        for k in range(GT):
                            last = nc.tensor.transpose(tp[b][:, k, :], A[b][:, k, :], C.ident[:, :])
                        last.then_inc(turned[b], 1)
                    for b in range(2):
                        pe.wait_ge(moved[b], i * 2 + 1)
                        for k in range(GT):
                            last = nc.tensor.matmul(own_ps[b][:, k, :], AT[b][:, k, :], C.t[f"Wa{block_no}"][:, :], start=True, stop=True)
                        last.then_inc(product[b], 1)
                    for b in range(2):
                        pe.wait_ge(relued[b], i + 1)
                        for k in range(GT):
                            last = nc.tensor.transpose(tp[b][:, k, :], R[b][:, k, :], C.ident[:, :])
                        last.then_inc(turned[b], 1)
                    for b in range(2):
                        pe.wait_ge(moved[b], i * 2 + 2)
                        for k in range(GT):
                            last = nc.tensor.matmul(lin_ps[b][:, k, :], AT[b][:, k, :], C.t[f"Wlin{block_no}"][:, :], start=True, stop=True)
                        last.then_inc(product[b], 1)

            @block.vector
            def _(dve):
                v = nc.vector
                link = Chain(dve, ph.chain)
                link(v.tensor_scalar(neg_max[:, :], last_max[:, :], -1.0, None, ALU.mult))
                link.restart()

                def affine(b, y, w):
                    link(v.tensor_mul(y[b][:, :, :], y[b][:, :, :], spread(C.v[f"{w}_w{block_no}"])))
                    link(v.tensor_add(y[b][:, :, :], y[b][:, :, :], spread(C.v[f"{w}_b{block_no}"])))

                with v.Fori(0, STEPS) as i:
                    for b in range(2):
                        dve.wait_ge(ph.loaded[b], i * 16 * loads + 16 * loads)
                        link(v.tensor_scalar(low[b][:, :], S[b][:, :, P + 1], neg_max[:, :], 0.0, ALU.add, ALU.min))
                        link.tell(low_ready[b])
                    for b in range(2):
                        dve.wait_ge(faded[b], i + 1)
                        link(v.tensor_tensor(share[b][:, :], fade[b][:, :], S[b][:, :, P], ALU.mult))
                        link(v.tensor_scalar(share[b][:, :], share[b][:, :], 1e-16, None, ALU.add))
                        link(v.reciprocal(share[b][:, :], share[b][:, :]))
                        link(v.tensor_tensor(share[b][:, :], share[b][:, :], fade[b][:, :], ALU.mult))
                        dve.wait_ge(product[b], i * 2 + 1)
                        for k in range(GT):
                            v.tensor_scalar(Y[b][:, k, :], S[b][:, k, 0:P], share[b][:, k:k + 1], None, ALU.mult).then_inc(ph.chain, 1)
                            link.n += 1
                        dve.wait_ge(ph.chain, link.n)
                        link(v.tensor_add(Y[b][:, :, :], Y[b][:, :, :], own_ps[b][:, :, :]))
                        norm.stats_dve(link, b, Y[b])
                    for n, w in enumerate(("gna", "norm")):
                        for b in range(2):
                            norm.apply_dve(dve, link, i, b, Y[b], Z[b] if n else Y[b], n=n)
                            affine(b, Z if n else Y, w)
                            if n == 0:
                                norm.stats_dve(link, b, Y[b])
                            else:
                                link.tell(applied[b])
                    for b in range(2):
                        dve.wait_ge(product[b], i * 2 + 2)
                        norm.stats_dve(link, b, lin_ps[b])
                    for b in range(2):
                        norm.apply_dve(dve, link, i, b, lin_ps[b], Y[b], n=2)
                        affine(b, Y, "gnl")
                        link(v.tensor_add(Y[b][:, :, :], Y[b][:, :, :], A[b][:, :, :]))
                        link.tell(applied[b])
                        if not final:
                            link.tell(ph.used[b])
                    if final:
                        for b in range(2):
                            dve.wait_ge(added[b], i + 1)
                            dve.wait_ge(ph.stored[b], i * 16 + 16)
                            link(v.tensor_add(F[b][:, :, :], O[b][:, :, :], X[b][:, :, :]))
                            link.tell(ph.used[b])
                            link.tell(ph.done[b])
                    link.restart()

            @block.scalar
            def _(act):
                link = Chain(act, ph.chain_act)
                with nc.scalar.Fori(0, STEPS) as i:
                    for b in range(2):
                        act.wait_ge(low_ready[b], i + 1)
                        nc.scalar.activation(fade[b][:, :], low[b][:, :], ACT.Exp).then_inc(faded[b], 1)
                    for b in range(2):
                        act.wait_ge(turned[b], i * 2 + 1)
                        nc.scalar.copy(AT[b][:, :, :], tp[b][:, :, :]).then_inc(moved[b], 1)
                    for n in range(2):
                        for b in range(2):
                            norm.root_act(act, i, b, n=n)
                    for b in range(2):
                        act.wait_ge(applied[b], i * 2 + 1)
                        nc.scalar.activation(R[b][:, :, :], Z[b][:, :, :], ACT.Relu).then_inc(relued[b], 1)
                    for b in range(2):
                        act.wait_ge(turned[b], i * 2 + 2)
                        nc.scalar.copy(AT[b][:, :, :], tp[b][:, :, :]).then_inc(moved[b], 1)
                    for b in range(2):
                        norm.root_act(act, i, b, n=2)
                    for b in range(2):
                        act.wait_ge(applied[b], i * 2 + 2)
                        if not final:
                            act.wait_ge(ph.stored[b], i * 16 + 16)
                        link(nc.scalar.activation(O[b][:, :, :], Y[b][:, :, :], ACT.Relu))
                        link.tell(added[b] if final else ph.done[b])
                    link.restart()

            def stores(i, b, last):
                if not final:
                    return ((group_rows(agents_out, i * 2 + b), O[b][:, :, :]),)
                if last and b == 1:
                    return ((out[LASTG * ROWS:N, :].rearrange("(p k) d -> p k d", k=GT), F[b][0:LASTP, :, :]),)
                o = out[0:LASTG * ROWS, :].rearrange("(g p k) d -> p g k d", p=P, k=GT)
                return ((o[:, ds(i * 2 + b, 1), :, :].rearrange("p o k d -> p (o k) d"), F[b][:, :, :]),)

            ph.storer(block, stores, 1, peel=final)


def gnn_layers(nc, w, out):
    with ExitStack() as ctx:
        def dram(name, shape, dt=FP32):
            return nc.dram_tensor(name, shape, dt, kind="Internal").ap()

        C = make_consts(nc, ctx, w)
        C.bn_scale = ctx.enter_context(nc.sbuf_tensor("bn_scale", [P, P], FP32))
        C.bn_bias = ctx.enter_context(nc.sbuf_tensor("bn_bias", [P, P], FP32))
        last_max = ctx.enter_context(nc.sbuf_tensor("last_max", [P, 1], FP32))
        by_dst_sums, by_src_sums = dram("by_dst_sums", (NP, SW)), dram("by_src_sums", (NP, SW))
        digit_rows = dram("digit_rows", (NP,), BF16)
        h0, h1, g, x1, x2, x3, a0, a1 = (dram(n, (NP, P)) for n in ("h0", "h1", "g", "x1", "x2", "x3", "a0", "a1"))
        h2, src_scores = dram("h2", (NP, P + HEADS)), dram("src_scores", (NP, HEADS))
        hyper = dram("hyper", (HGROUPS * ROWS, P + 1))
        ctx_tables = [dram(f"ctx_table{k}", (CTX, 2 * P)) for k in range(2)]

        fill_zero(nc, C, (by_dst_sums, by_src_sums))
        orders = {name: Order(nc, ctx, name) for name in ("by_src", "by_dst")}
        with ExitStack() as sorting:
            A = sorting.enter_context(nc.sbuf_tensor("pairs", [P, TILES, 2], I32))
            for name, key, other, limit in (("by_src", "src", "dst", HYPER), ("by_dst", "dst", "src", CTX)):
                once, twice = dram(f"{name}_once", (NP, 2), I32), dram(f"{name}_twice", (NP, 2), I32)
                load_edges(nc, A, w[key], w[other], name)
                sort_pass(nc, C, name + "_low", A, once, digit_rows, 0)
                reload_pairs(nc, A, once, name + "_reload")
                sort_pass(nc, C, name + "_high", A, twice, digit_rows, 8)
                describe_order(nc, C, A, twice, orders[name], limit)
        by_src, by_dst = orders["by_src"], orders["by_dst"]
        norm_input(nc, C, w["x"], h0)
        plain_pass(nc, C, "sage", by_dst, h0, P, Order.OTHER, C.wlr[:, 0, :], by_dst_sums)
        sage_nodes(nc, C, w["x"], h0, by_dst_sums, x1, h1)
        for step, (rows, weight) in enumerate(((h1, "W1"), (g, "W2"))):
            plain_pass(nc, C, f"hyper_in{step}", by_dst, rows, P, Order.OTHER, C.ident[:, :], by_dst_sums)
            hyper_rows(nc, C, f"hyper_rows{step}", by_dst_sums, hyper, affine=step == 1)
            plain_pass(nc, C, f"hyper_out{step}", by_src, hyper, P + 1, Order.CLAMPED, C.t[weight][:, :], by_src_sums)
            if step == 0:
                hyper_nodes1(nc, C, by_src_sums, g)
        hyper_nodes2(nc, C, x1, by_src_sums, x2, h2, src_scores)
        attention_pass(nc, C, by_src, h2, src_scores, by_src_sums)
        attention_nodes(nc, C, x2, h2, by_src_sums, x3, a0)
        context_tables(nc, C, w["L3_gnn_ctx"], ctx_tables)
        for k in range(2):
            agents = (a0, a1)[k]
            context_pass(nc, C, k, by_dst, ctx_tables[k], agents, by_dst_sums, last_max)
            agent_nodes(nc, C, k, agents, by_dst_sums, last_max, a1, x3, out if k == 1 else None)


_OUTS = [((50000, 128), "float32")]


def kernel(**inputs):
    import numpy as _np
    import concourse.bacc as _bacc
    from concourse import mybir as _mybir
    from concourse.bass_utils import run_bass_kernel_spmd as _run

    nc = _bacc.Bacc("TRN2", target_bir_lowering=False, num_devices=1)
    arrays, args = {}, {}
    for name, value in inputs.items():
        a = _np.ascontiguousarray(value)
        arrays[f"in_{name}_dram"] = a
        args[name] = nc.dram_tensor(f"in_{name}_dram", a.shape, _mybir.dt.from_np(a.dtype), kind="ExternalInput").ap()
    out = nc.dram_tensor("out_0_dram", _OUTS[0][0], _mybir.dt.float32, kind="ExternalOutput").ap()
    gnn_layers(nc, args, out)
    r = _run(nc, [arrays], core_ids=[0])
    return r.results[0]["out_0_dram"]
```

```python
import concourse.bass as bass
from concourse import mybir
from contextlib import ExitStack, contextmanager

FP32 = mybir.dt.float32
BF16 = mybir.dt.bfloat16
I32 = mybir.dt.int32
ALU = mybir.AluOpType
ACT = mybir.ActivationFunctionType
AX = mybir.AxisListType
ds = bass.ds

P = 128
N = 50000
GT = 4
ROWS = GT * P
GROUPS = -(-N // (2 * ROWS)) * 2
STEPS = GROUPS // 2
TILES = GROUPS * GT
NP = TILES * P
LASTG = N // ROWS
LASTP = (N - LASTG * ROWS) // GT
FULLP = N // TILES
RESTT = N - FULLP * TILES
PAD_KEY = 65535
HYPER = 10000
HGROUPS = 20
WAYS = 4
NODE_STEPS = 25
NODE_ROWS = NODE_STEPS * WAYS * ROWS
CTX = 3125
CTILES = 25
HEADS = 4
SW = 132


class Chain:

    def __init__(self, eng, sem):
        self.eng, self.sem, self.n = eng, sem, 0

    def __call__(self, ins):
        self.n += 1
        ins.then_inc(self.sem, 1)
        self.eng.wait_ge(self.sem, self.n)

    def tell(self, sem, by=1):
        self.eng.sem_inc(sem, by)

    def restart(self):
        self.eng.sem_clear(self.sem)
        self.n = 0


class Phase:

    def __init__(self, nc, name):
        self.nc, self.name, self.ctx, self.sems = nc, name, ExitStack(), []

    def sem(self, name):
        s = self.ctx.enter_context(self.nc.semaphore(f"{self.name}_{name}"))
        self.sems.append(s)
        return s

    def sems2(self, name):
        return [self.sem(f"{name}{b}") for b in range(2)]

    def ways_sem(self, *names):
        return [[self.sem(f"{n}{b}") for b in range(WAYS)] for n in names]

    def ways_sb(self, shape, *names):
        return [[self.sb(f"{n}{b}", shape) for b in range(WAYS)] for n in names]

    def sb(self, name, shape, dt=FP32):
        return self.ctx.enter_context(self.nc.sbuf_tensor(f"{self.name}_{name}", shape, dt))

    def sb2(self, name, shape, dt=FP32):
        return [self.sb(f"{name}{b}", shape, dt) for b in range(2)]

    def ps(self, name, shape, dt=FP32):
        return self.ctx.enter_context(self.nc.psum_tensor(f"{self.name}_{name}", shape, dt))

    def ps2(self, name, shape, dt=FP32):
        return [self.ps(f"{name}{b}", shape, dt) for b in range(2)]

    def __enter__(self):
        return self

    def __exit__(self, *exc):
        if exc[0] is None:
            with self.nc.Block() as block:
                @block.gpsimd
                def _(pool):
                    pool.dma_reset()
                    for s in self.sems:
                        pool.sem_clear(s)
        self.ctx.close()


def pool_wait(pool, sem, value, went_on):
    pool.wait_ge(sem, value)
    pool.sem_inc(went_on, 1)


def first_credit(nc, C, b, sem):
    nc.gpsimd.dma_start(C.credit[b:b + 1, :], C.eps[0:1, :]).then_inc(sem, 64)


def group_rows(table, g, lo=0, hi=None):
    v = table.rearrange("(g p k) d -> p g k d", p=P, k=GT)
    hi = table.shape[1] if hi is None else hi
    return v[:, ds(g, 1), :, lo:hi].rearrange("p o k d -> p (o k) d")


class Consts:
    pass


def make_consts(nc, ctx, w):
    C = Consts()

    def sb(name, shape, dt=FP32):
        return ctx.enter_context(nc.sbuf_tensor(name, shape, dt))

    C.ident = sb("ident", [P, P])
    C.ones = sb("ones", [P, P])
    C.zeros = sb("zeros", [P, P])
    C.ones_row = sb("ones_row", [1, ROWS])
    C.lower = sb("lower", [P, P], BF16)
    C.unit = sb("unit", [P, 2], BF16)
    C.ones_bf = sb("ones_bf", [P, 1], BF16)
    C.upper = sb("upper", [P, P])
    C.digit_free = sb("digit_free", [P, 256], BF16)
    C.digit_part = sb("digit_part", [P, 2])
    C.eps = sb("eps", [P, 1])
    C.credit = nc.dram_tensor("credit", (4, 1), FP32, kind="Internal").ap()
    C.hw = sb("hw", [P, HGROUPS, GT])
    mats = {"Wl": w["L0_gnn_Wl"], "Wr": w["L0_gnn_Wr"], "W1": w["L1_gnn_W1"], "W2": w["L1_gnn_W2"],
            "V": w["L2_gnn_V_w"]}
    for h in range(HEADS):
        mats[f"W{h}h"] = w["L2_gnn_W_w"][h]
    for k in range(2):
        mats[f"Wctx{k}"] = w["L3_gnn_Wctx"][k]
        mats[f"Wlin{k}"] = w["L3_gnn_Wlin"][k]
        mats[f"Wa{k}"] = w["L3_gnn_Wagt"][k][:, 0:P]
        mats[f"Wb{k}"] = w["L3_gnn_Wagt"][k][:, P:2 * P]
        mats[f"Wq{k}"] = w["L3_gnn_Wq"][k]
        mats[f"Wk{k}"] = w["L3_gnn_Wk"][k]
    names = list(mats)
    raw = sb("raw_weights", [P, len(names), P])
    C.wlr = sb("wlr", [P, 2, P])
    C.heads = sb("heads", [P, HEADS, P])
    C.ctxw = sb("ctxw", [P, 2, 2, P])
    C.t = {}
    for n in names:
        C.t[n] = sb("T_" + n, [P, P])
    vecs = {"bl": w["L0_gnn_bl"], "b2": w["L1_gnn_b2"], "gamma": w["L1_gnn_gamma"], "beta": w["L1_gnn_beta"],
            "Vb": w["L2_gnn_V_b"], "ln_g": w["L2_gnn_ln_g"], "ln_b": w["L2_gnn_ln_b"]}
    for h in range(HEADS):
        vecs[f"Wb{h}"] = w["L2_gnn_W_b"][h]
    for k in range(2):
        for v in ("gnc_w", "gnc_b", "gna_w", "gna_b", "norm_w", "norm_b", "gnl_w", "gnl_b"):
            vecs[f"{v}{k}"] = w[f"L3_gnn_{v}"][k]
    C.v = {n: sb("V_" + n, [P, P]) for n in vecs}
    C.mean_b = sb("mean_b", [P, P])
    C.row_mean = sb("row_mean", [P, 1])
    C.acol = sb("acol", [P, 2 * HEADS])
    C.bcol = sb("bcol", [P, HEADS])
    C.bwide = sb("bwide", [P, HEADS, P])
    C.score_w = sb("score_w", [P, 2 * HEADS])
    C.score_b = sb("score_b", [P, 2 * HEADS])

    with Phase(nc, "setup") as ph:
        loaded, made, ready, moved = ph.sem("loaded"), ph.sem("made"), ph.sem("ready"), ph.sem("moved")
        hwset = ph.sem("hwset")
        chain_s, chain_g, chain_a = ph.sem("chain_dve"), ph.sem("chain_pool"), ph.sem("chain_act")
        tp = ph.ps2("tp", [P, P])
        n_loads = [0]
        with nc.Block() as block:
            @block.sync
            def _(sp):
                for j, n in enumerate(names):
                    sp.dma_start(raw[:, j, :], mats[n]).then_inc(loaded, 16)
                    n_loads[0] += 1
                for n, v in vecs.items():
                    sp.dma_start(C.v[n][:, :], v.rearrange("(a n) -> a n", a=1).partition_broadcast(P)
                                 if v.ndim == 1 else v).then_inc(loaded, 16)
                    n_loads[0] += 1
                with nc.allow_non_contiguous_dma(reason="small columns, once"):
                    for half in range(2):
                        sp.dma_start(C.acol[:, half * HEADS:(half + 1) * HEADS],
                                     w["L2_gnn_a"][:, half * P:(half + 1) * P].rearrange("h d -> d h")).then_inc(loaded, 16)
                        n_loads[0] += 1
                    sp.dma_start(C.bcol[:, :], w["L2_gnn_W_b"].rearrange("h d -> d h")).then_inc(loaded, 16)
                    n_loads[0] += 1
                sp.wait_ge(hwset, 1)
                full = HYPER // ROWS
                rest = (HYPER - full * ROWS) // GT
                sp.dma_start(C.hw[:, 0:full, :], w["L1_gnn_hyperedge_weight"][0:full * ROWS]
                             .rearrange("(g p k) -> p g k", p=P, k=GT)).then_inc(loaded, 16)
                sp.dma_start(C.hw[0:rest, full, :], w["L1_gnn_hyperedge_weight"][full * ROWS:HYPER]
                             .rearrange("(p k) -> p k", k=GT)).then_inc(loaded, 16)
                n_loads[0] += 2
                sp.wait_ge(loaded, 16 * n_loads[0])

            @block.gpsimd
            def _(pool):
                link = Chain(pool, chain_g)
                g = nc.gpsimd
                link(g.memset(C.ident[:, :], 0.0))
                link(g.affine_select(out=C.ident[:, :], in_=C.ident[:, :], compare_op=ALU.not_equal, fill=1.0,
                                     base=0, pattern=[[-1, P]], channel_multiplier=1))
                link(g.memset(C.upper[:, :], 1.0))
                link(g.affine_select(out=C.upper[:, :], in_=C.upper[:, :], compare_op=ALU.is_gt, fill=0.0,
                                     base=0, pattern=[[1, P]], channel_multiplier=-1))
                link(g.iota(C.digit_free[:, :], pattern=[[1, 256]], base=0, channel_multiplier=0,
                            allow_small_or_imprecise_dtypes=True))
                link(g.iota(C.digit_part[:, :], pattern=[[P, 2]], base=0, channel_multiplier=1,
                            allow_small_or_imprecise_dtypes=True))
                link.tell(made)

            @block.vector
            def _(dve):
                link = Chain(dve, chain_s)
                v = nc.vector
                link(v.memset(C.hw[:, :, :], 0.0))
                link.tell(hwset)
                v.memset(C.ones[:, :], 1.0)
                v.memset(C.zeros[:, :], 0.0)
                v.memset(C.ones_row[:, :], 1.0)
                v.memset(C.ones_bf[:, :], 1.0)
                link(v.memset(C.unit[:, :], 0.0))
                link(v.memset(C.unit[:, 0:1], 1.0))
                link(v.memset(C.eps[:, :], 1e-5))
                dve.wait_ge(made, 1)
                link(v.tensor_copy(C.lower[:, :], C.upper[:, :]))
                dve.wait_ge(loaded, 16 * n_loads[0])
                link(v.tensor_add(C.mean_b[:, :], C.v["Wb0"][:, :], C.v["Wb1"][:, :]))
                link(v.tensor_add(C.mean_b[:, :], C.mean_b[:, :], C.v["Wb2"][:, :]))
                link(v.tensor_add(C.mean_b[:, :], C.mean_b[:, :], C.v["Wb3"][:, :]))
                link(v.tensor_scalar(C.mean_b[:, :], C.mean_b[:, :], 1.0 / HEADS, None, ALU.mult))
                for h in range(HEADS):
                    link(v.tensor_scalar(C.bwide[:, h, :], C.ones[:, :], C.bcol[:, h:h + 1], None, ALU.mult))
                link.tell(made)

            jobs = []
            for j, n in enumerate(names):
                if n[:2] in ("Wq", "Wk"):
                    continue
                jobs.append((n, raw[:, j, :], C.ident[:, :], P))
            at = {n: j for j, n in enumerate(names)}
            for k in range(2):
                jobs.append((f"Wq{k}", raw[:, at[f"Wk{k}"], :], raw[:, at[f"Wq{k}"], :], P))
            for h in range(HEADS):
                for s in range(2):
                    c = s * HEADS + h
                    jobs.append((("w", c), raw[:, at[f"W{h}h"], :], C.acol[:, c:c + 1], 1))
                    jobs.append((("b", c), C.bwide[:, h, :], C.acol[:, c:c + 1], 1))

            @block.tensor
            def _(pe):
                pe.wait_ge(made, 2)
                pe.wait_ge(loaded, 16 * n_loads[0])
                for j, (n, left, right, width) in enumerate(jobs):
                    if j >= 2:
                        pe.wait_ge(moved, j - 1)
                    nc.tensor.matmul(tp[j % 2][:, 0:width], left, right, start=True, stop=True).then_inc(ready, 1)

            places = {"Wl": C.wlr[:, 0, :], "Wr": C.wlr[:, 1, :]}
            for h in range(HEADS):
                places[f"W{h}h"] = C.heads[:, h, :]
            for k in range(2):
                places[f"Wq{k}"] = C.ctxw[:, k, 0, :]
                places[f"Wctx{k}"] = C.ctxw[:, k, 1, :]
            for c in range(2 * HEADS):
                places["w", c] = C.score_w[:, c:c + 1]
                places["b", c] = C.score_b[:, c:c + 1]

            centred = [C.mean_b[:, :]] + [C.heads[:, h, :] for h in range(HEADS)]
            centred += [C.t[f"{n}{k}"][:, :] for n in ("Wa", "Wb", "Wlin") for k in range(2)]

            @block.scalar
            def _(act):
                for j, (n, _, _, width) in enumerate(jobs):
                    act.wait_ge(ready, j + 1)
                    to = places[n] if n in places else C.t[n][:, :]
                    nc.scalar.copy(to, tp[j % 2][:, 0:width]).then_inc(moved, 1)
                act.wait_ge(moved, len(jobs))
    with Phase(nc, "centre") as ph:
        chain = ph.sem("chain")
        with nc.Block() as block:
            @block.vector
            def _(dve):
                link = Chain(dve, chain)
                for m in centred:
                    link(nc.vector.tensor_reduce(C.row_mean[:, :], m, AX.X, ALU.add))
                    link(nc.vector.tensor_scalar(C.row_mean[:, :], C.row_mean[:, :], 1.0 / P, None, ALU.mult))
                    link(nc.vector.tensor_scalar(m, m, C.row_mean[:, :], None, ALU.subtract))
    return C


def load_edges(nc, A, keys, others, name):
    with Phase(nc, "edges_" + name) as ph:
        raw = [ph.sb("key", [P, TILES], I32), ph.sb("other", [P, TILES], I32)]
        loaded, padded, chain = ph.sem("loaded"), ph.sem("padded"), ph.sem("chain")
        with nc.Block() as block:
            @block.sync
            def _(sp):
                sp.wait_ge(padded, 1)
                for r, v in zip(raw, (keys, others)):
                    sp.dma_start(r[0:FULLP, :], v[0:FULLP * TILES].rearrange("(p t) -> p t", t=TILES)).then_inc(loaded, 16)
                    sp.dma_start(r[FULLP:FULLP + 1, 0:RESTT], v[FULLP * TILES:N].rearrange("(p t) -> p t", p=1)).then_inc(loaded, 16)
                sp.wait_ge(loaded, 64)

            @block.vector
            def _(dve):
                link = Chain(dve, chain)
                link(nc.vector.memset(raw[0][:, :], PAD_KEY))
                link(nc.vector.memset(raw[1][:, :], 0))
                link.tell(padded)
                dve.wait_ge(loaded, 64)
                link(nc.vector.tensor_copy(A[:, :, 0], raw[0][:, :]))
                link(nc.vector.tensor_copy(A[:, :, 1], raw[1][:, :]))


def sort_pass(nc, C, name, A, table, digit_rows, shift):
    with Phase(nc, name) as ph:
        digit_i = ph.sb("digit_i", [P, TILES], I32)
        digit = ph.sb("digit", [P, TILES])
        rows = ph.sb("rows", [P, GT, P], BF16)
        onehot = ph.sb2("onehot", [P, GT, 256], BF16)
        running = ph.sb("running", [P, 2, TILES])
        counts = ph.sb("counts", [P, 2, TILES])
        base = ph.sb("base", [P, 2])
        start_i = ph.sb("start_i", [P, 2, TILES], I32)
        part_i = ph.sb("part_i", [P, 2, TILES], I32)
        start = ph.sb("start", [P, 2, TILES, 2], BF16)
        wide = ph.sb2("wide", [P, ROWS], BF16)
        member = ph.sb2("member", [P, 2, ROWS], BF16)
        before = ph.sb2("before", [P, GT, P], BF16)
        parts = ph.sb2("parts", [P, GT, 2])
        pos = ph.sb2("pos", [P, GT], I32)
        pos_lo = ph.sb2("pos_lo", [P, GT], I32)
        pos_hi = ph.sb2("pos_hi", [P, GT], I32)
        where = ph.sb2("where", [P, GT], I32)
        pairs = ph.sb2("pairs", [P, GT, 2], I32)
        tp = ph.ps("tp", [P, 4, P])
        count_ps = [ph.ps(f"count{h}", [P, 512]) for h in range(2)]
        base_ps = ph.ps("base_ps", [P, 2])
        pos_ps = ph.ps2("pos_ps", [P, GT, 2])
        digits_ready, turned, rows_ready, rows_out = (ph.sem(x) for x in ("digits_ready", "turned", "rows_ready", "rows_out"))
        chain = ph.sem("chain")
        hot, counted = ph.sems2("hot"), ph.sems2("counted")
        totals_ready, base_ready, start_ready = (ph.sem(x) for x in ("totals_ready", "base_ready", "start_ready"))
        wide_in, wide_used = ph.sems2("wide_in"), ph.sems2("wide_used")
        member_ready, placed, taken = ph.sems2("member_ready"), ph.sems2("placed"), ph.sems2("taken")
        where_ready, scattered = ph.sems2("where_ready"), ph.sems2("scattered")
        went_on = ph.sem("went_on")
        tail = TILES - 3 * P
        digit_tiles = digit_rows.rearrange("(t c) -> t c", c=P)
        with nc.Block() as block:
            @block.sync
            def _(sp):
                for b in range(2):
                    sp.sem_inc(wide_used[b], 1)
                sp.wait_ge(rows_ready, 1)
                sp.dma_start(digit_tiles[0:3 * P, :].rearrange("(j p) c -> p j c", p=P), rows[:, 0:3, :]).then_inc(rows_out, 16)
                sp.dma_start(digit_tiles[3 * P:TILES, :], rows[0:tail, 3, :]).then_inc(rows_out, 16)
                sp.wait_ge(rows_out, 32)
                with nc.sync.Fori(0, STEPS) as i:
                    for b in range(2):
                        sp.wait_ge(wide_used[b], i + 1)
                        sp.dma_start(wide[b][:, :], digit_rows[ds((i * 2 + b) * ROWS, ROWS)]
                                     .rearrange("(a n) -> a n", a=1).partition_broadcast(P)).then_inc(wide_in[b], 16)

            @block.tensor
            def _(pe):
                pe.wait_ge(digits_ready, 1)
                for j in range(4):
                    w = P if j < 3 else tail
                    last = nc.tensor.transpose(tp[0:w, j, :], digit[:, j * P:j * P + w], C.ident[:, :])
                last.then_inc(turned, 1)
                with nc.tensor.Fori(0, STEPS) as i:
                    for b in range(2):
                        pe.wait_ge(hot[b], i + 1)
                        for k in range(GT):
                            for h in range(2):
                                last = nc.tensor.matmul(count_ps[h][:, ds(i * 8 + b * 4 + k, 1)],
                                                        onehot[b][:, k, h * P:(h + 1) * P], C.ones_bf[:, :],
                                                        start=True, stop=True)
                        last.then_inc(counted[b], 1)
                pe.wait_ge(totals_ready, 1)
                nc.tensor.matmul(base_ps[:, 0:1], C.upper[:, :], running[:, 0, TILES - 1:TILES], start=True, stop=True)
                nc.tensor.matmul(base_ps[:, 1:2], C.upper[:, :], running[:, 1, TILES - 1:TILES], start=True, stop=False)
                nc.tensor.matmul(base_ps[:, 1:2], C.ones[:, :], running[:, 0, TILES - 1:TILES], start=False, stop=True).then_inc(base_ready, 1)
                pe.wait_ge(start_ready, 1)
                with nc.tensor.Fori(0, STEPS) as i:
                    for b in range(2):
                        pe.wait_ge(member_ready[b], i + 1)
                        pe.wait_ge(taken[b], i + 1)
                        for k in range(GT):
                            t = i * 8 + b * 4 + k
                            o = pos_ps[b][:, k, :]
                            nc.tensor.matmul(o, before[b][:, k, :], C.unit[:, :], start=True, stop=False)
                            for h in range(2):
                                last = nc.tensor.matmul(o, member[b][:, h, k * P:(k + 1) * P],
                                                        start[:, h, ds(t, 1), :].rearrange("p o c -> p (o c)"),
                                                        start=False, stop=(h == 1))
                        last.then_inc(placed[b], 1)

            @block.scalar
            def _(act):
                act.wait_ge(turned, 1)
                nc.scalar.copy(rows[:, 0:3, :], tp[:, 0:3, :]).then_inc(went_on, 1)
                act.wait_ge(went_on, 1)
                nc.scalar.copy(rows[0:tail, 3, :], tp[0:tail, 3, :]).then_inc(rows_ready, 1)

            @block.vector
            def _(dve):
                v = nc.vector
                link = Chain(dve, chain)
                link(v.tensor_scalar(digit_i[:, :], A[:, :, 0], shift, 255, ALU.logical_shift_right, ALU.bitwise_and))
                link(v.tensor_copy(digit[:, :], digit_i[:, :]))
                link.tell(digits_ready)
                for b in range(2):
                    dve.sem_inc(counted[b], 1)
                    dve.sem_inc(taken[b], 1)
                link.restart()
                with v.Fori(0, STEPS) as i:
                    for b in range(2):
                        dve.wait_ge(counted[b], i + 1)
                        for k in range(GT):
                            last = v.tensor_scalar(onehot[b][:, k, :], C.digit_free[:, :],
                                                   digit[:, ds(i * 8 + b * 4 + k, 1)], None, ALU.is_equal)
                        last.then_inc(hot[b], 1)
                for b in range(2):
                    dve.wait_ge(counted[b], STEPS + 1)
                for h in range(2):
                    link(v.tensor_copy(counts[:, h, :], count_ps[h][:, 0:TILES]))
                    link(v.tensor_tensor_scan(running[:, h, :], counts[:, h, :], counts[:, h, :], 0.0,
                                              ALU.add, ALU.bypass))
                link.tell(totals_ready)
                dve.wait_ge(base_ready, 1)
                link(v.tensor_copy(base[:, :], base_ps[:, :]))
                for h in range(2):
                    link(v.tensor_sub(running[:, h, :], running[:, h, :], counts[:, h, :]))
                    link(v.tensor_scalar(start_i[:, h, :], running[:, h, :], base[:, h:h + 1], None, ALU.add))
                link(v.tensor_scalar(part_i[:, :, :], start_i[:, :, :], 255, None, ALU.bitwise_and))
                link(v.tensor_copy(start[:, :, :, 0], part_i[:, :, :]))
                link(v.tensor_scalar(part_i[:, :, :], start_i[:, :, :], 8, None, ALU.logical_shift_right))
                link(v.tensor_copy(start[:, :, :, 1], part_i[:, :, :]))
                link.tell(start_ready)
                link.restart()
                with v.Fori(0, STEPS) as i:
                    for b in range(2):
                        dve.wait_ge(wide_in[b], i * 16 + 16)
                        for h in range(2):
                            v.tensor_scalar(member[b][:, h, :], wide[b][:, :], C.digit_part[:, h:h + 1], None, ALU.is_equal)
                        for k in range(GT):
                            last = v.scalar_tensor_tensor(before[b][:, k, :], wide[b][:, k * P:(k + 1) * P],
                                                          digit[:, ds(i * 8 + b * 4 + k, 1)], C.lower[:, :],
                                                          ALU.is_equal, ALU.mult)
                        link(last)
                        link.tell(wide_used[b])
                        link.tell(member_ready[b])
                    for b in range(2):
                        dve.wait_ge(placed[b], i + 1)
                        link(v.tensor_copy(parts[b][:, :, :], pos_ps[b][:, :, :]))
                        link.tell(taken[b])
                        dve.wait_ge(scattered[b], i * 64 + 64)
                        link(v.scalar_tensor_tensor(pos[b][:, :], parts[b][:, :, 1], 256.0, parts[b][:, :, 0], ALU.mult, ALU.add))
                        v.tensor_scalar(pos_lo[b][:, :], pos[b][:, :], P - 1, None, ALU.bitwise_and)
                        v.tensor_copy(pairs[b][:, :, :], A[:, ds(i * 8 + b * 4, GT), :])
                        link(v.tensor_scalar(pos_hi[b][:, :], pos[b][:, :], 7, None, ALU.logical_shift_right))
                        link(v.scalar_tensor_tensor(where[b][:, :], pos_lo[b][:, :], float(TILES), pos_hi[b][:, :], ALU.mult, ALU.add))
                        link.tell(where_ready[b])
                    link.restart()

            @block.gpsimd
            def _(pool):
                for b in range(2):
                    first_credit(nc, C, b, scattered[b])
                with nc.gpsimd.Fori(0, STEPS) as i:
                    for b in range(2):
                        pool_wait(pool, where_ready[b], i + 1, went_on)
                        for k in range(GT):
                            nc.gpsimd.indirect_dma_start(
                                out=table, out_offset=bass.IndirectOffsetOnAxis(ap=where[b][:, k:k + 1], axis=0),
                                in_=pairs[b][:, k, :], in_offset=None, bounds_check=NP - 1,
                                oob_is_err=False).then_inc(scattered[b], 16)
                for b in range(2):
                    pool.wait_ge(scattered[b], 64 * (STEPS + 1))


def reload_pairs(nc, A, table, name):
    with Phase(nc, name) as ph:
        loaded = ph.sem("loaded")
        with nc.Block() as block:
            @block.sync
            def _(sp):
                sp.dma_start(A[:, :, :], table.rearrange("(p t) c -> p t c", t=TILES)).then_inc(loaded, 16)
                sp.wait_ge(loaded, 16)


class Order:

    KEY, OTHER, CLAMPED, TARGET = range(4)

    def __init__(self, nc, ctx, name):
        self.name = name
        self.index = nc.dram_tensor(f"{name}_index", (P, GROUPS * 4 * GT), I32, kind="Internal").ap()
        self.same = nc.dram_tensor(f"{name}_same", (NP,), BF16, kind="Internal").ap()
        self.pad_bias = ctx.enter_context(nc.sbuf_tensor(f"{name}_pad_bias", [P, TILES], FP32))

    def index_of(self, g, slot, slots=1):
        at = self.index.rearrange("p (g s) -> p g s", s=4 * GT)
        return at[:, ds(g, 1), slot * GT:(slot + slots) * GT].rearrange("p o s -> p (o s)")


def describe_order(nc, C, A, table, order, limit):
    with Phase(nc, "order_" + order.name) as ph:
        later = ph.sb("later", [P, TILES, 2], I32)
        earlier = ph.sb("earlier", [P, TILES, 2], I32)
        key, nxt, prv = ph.sb("key", [P, TILES]), ph.sb("nxt", [P, TILES]), ph.sb("prv", [P, TILES])
        same, more = ph.sb("same", [P, TILES]), ph.sb("more", [P, TILES])
        packed = ph.sb("packed", [P, GROUPS, 4, GT], I32)
        rows = ph.sb("rows", [P, 4, P], BF16)
        tp = ph.ps("tp", [P, 4, P])
        loaded, cleared, same_ready, turned, rows_ready, packed_ready, stored, chain, chain_act = (ph.sem(x) for x in (
            "loaded", "cleared", "same_ready", "turned", "rows_ready", "packed_ready", "stored", "chain", "chain_act"))
        tail = TILES - 3 * P
        tv = table.rearrange("(p t) c -> p t c", t=TILES)
        same_tiles = order.same.rearrange("(t c) -> t c", c=P)
        with nc.Block() as block:
            @block.sync
            def _(sp):
                sp.dma_start(A[:, :, :], tv).then_inc(loaded, 16)
                sp.wait_ge(cleared, 1)
                sp.dma_start(later[0:P - 1, :, :], tv[1:P, :, :]).then_inc(loaded, 16)
                sp.dma_start(later[P - 1:P, 0:TILES - 1, :], tv[0:1, 1:TILES, :]).then_inc(loaded, 16)
                sp.dma_start(earlier[1:P, :, :], tv[0:P - 1, :, :]).then_inc(loaded, 16)
                sp.dma_start(earlier[0:1, 1:TILES, :], tv[P - 1:P, 0:TILES - 1, :]).then_inc(loaded, 16)
                sp.wait_ge(rows_ready, 1)
                sp.dma_start(same_tiles[0:3 * P, :].rearrange("(j p) c -> p j c", p=P), rows[:, 0:3, :]).then_inc(stored, 16)
                sp.dma_start(same_tiles[3 * P:TILES, :], rows[0:tail, 3, :]).then_inc(stored, 16)
                sp.wait_ge(packed_ready, 1)
                sp.dma_start(order.index, packed[:, :, :, :].rearrange("p g s k -> p (g s k)")).then_inc(stored, 16)
                sp.wait_ge(stored, 48)

            @block.vector
            def _(dve):
                v = nc.vector
                link = Chain(dve, chain)
                v.memset(later[:, :, :], -1)
                link(v.memset(earlier[:, :, :], -1))
                link.tell(cleared)
                dve.wait_ge(loaded, 80)
                v.tensor_copy(key[:, :], A[:, :, 0])
                v.tensor_copy(nxt[:, :], later[:, :, 0])
                link(v.tensor_copy(prv[:, :], earlier[:, :, 0]))
                link(v.tensor_tensor(same[:, :], key[:, :], prv[:, :], ALU.is_equal))
                link.tell(same_ready)
                link(v.tensor_tensor(more[:, :], key[:, :], nxt[:, :], ALU.is_equal))
                link(v.scalar_tensor_tensor(more[:, :], more[:, :], float(PAD_KEY), key[:, :], ALU.mult, ALU.max))
                grouped = [x.rearrange("p (g k) -> p g k", k=GT) for x in (key[:, :], more[:, :])]
                other = A[:, :, 1].rearrange("p (g k) -> p g k", k=GT)
                v.tensor_scalar(packed[:, :, Order.KEY, :], grouped[0], float(NP - 1), None, ALU.min)
                v.tensor_copy(packed[:, :, Order.OTHER, :], other)
                v.tensor_scalar(packed[:, :, Order.CLAMPED, :], other, float(limit - 1), None, ALU.min)
                v.tensor_scalar(order.pad_bias[:, :], key[:, :], float(N), -1e30, ALU.is_ge, ALU.mult)
                link(v.tensor_copy(packed[:, :, Order.TARGET, :], grouped[1]))
                link.tell(packed_ready)

            @block.tensor
            def _(pe):
                pe.wait_ge(same_ready, 1)
                for j in range(4):
                    w = P if j < 3 else tail
                    last = nc.tensor.transpose(tp[0:w, j, :], same[:, j * P:j * P + w], C.ident[:, :])
                last.then_inc(turned, 1)

            @block.scalar
            def _(act):
                link = Chain(act, chain_act)
                act.wait_ge(turned, 1)
                link(nc.scalar.copy(rows[:, 0:3, :], tp[:, 0:3, :]))
                nc.scalar.copy(rows[0:tail, 3, :], tp[0:tail, 3, :]).then_inc(rows_ready, 1)


def fill_zero(nc, C, tables):
    with Phase(nc, "zero") as ph:
        z = ph.sb("z", [P, 16 * SW])
        cleared, stored = ph.sem("cleared"), ph.sem("stored")
        count = NODE_ROWS // (P * 16)
        with nc.Block() as block:
            @block.vector
            def _(dve):
                nc.vector.memset(z[:, :], 0.0).then_inc(cleared, 1)

            @block.sync
            def _(sp):
                sp.wait_ge(cleared, 1)
                for t in tables:
                    v = t.rearrange("(c p r) w -> c p (r w)", p=P, r=16)
                    for c in range(count):
                        sp.dma_start(v[c], z[:, :]).then_inc(stored, 16)
                sp.wait_ge(stored, 16 * count * len(tables))


def gather(nc, to, table, index, sem, rows):
    nc.gpsimd.indirect_dma_start(out=to, out_offset=None, in_=table,
                                 in_offset=bass.IndirectOffsetOnAxis(ap=index, axis=0),
                                 bounds_check=rows - 1, oob_is_err=False).then_inc(sem, 16)


def load_targets(act, order, i, b, target, target_in, scattered):
    act.wait_ge(scattered[b], i * 64 + 64)
    act.dma_start(target[b][:, :], order.index_of(i * 2 + b, Order.TARGET)).then_inc(target_in[b], 16)


def edge_loaders(nc, order, block, slot, slots, gather_index, same, gather_index_in, same_in, gathered, same_used, unit):
    @block.sync
    def _(sp):
        for b in range(2):
            sp.sem_inc(same_used[b], 1)
        with nc.sync.Fori(0, STEPS) as i:
            for b in range(2):
                g = i * 2 + b
                sp.wait_ge(gathered[b], i * unit + unit)
                sp.dma_start(gather_index[b][:, :], order.index_of(g, slot, slots)).then_inc(gather_index_in[b], 16)
                sp.wait_ge(same_used[b], i + 1)
                sp.dma_start(same[b][:, :], order.same[ds(g * ROWS, ROWS)]
                             .rearrange("(a n) -> a n", a=1).partition_broadcast(P)).then_inc(same_in[b], 16)


def edge_pool(nc, C, block, gathers, sums, rows_out, target, target_in, rows_ready, gathered, scattered,
              gather_index_in, gathers_free, went_on, unit):
    @block.gpsimd
    def _(pool):
        for b in range(2):
            nc.gpsimd.dma_start(C.credit[b:b + 1, :], C.eps[0:1, :]).then_inc(gathered[b], unit)
            nc.gpsimd.dma_start(C.credit[2 + b:3 + b, :], C.eps[0:1, :]).then_inc(scattered[b], 64)

        def take(i, b):
            pool_wait(pool, gather_index_in[b], i * 16 + 16, went_on)
            pool_wait(pool, gathers_free[b], i + 1, went_on)
            gathers(b)

        def put(i, b):
            pool_wait(pool, target_in[b], i * 16 + 16, went_on)
            pool_wait(pool, rows_ready[b], i + 1, went_on)
            for k in range(GT):
                nc.gpsimd.indirect_dma_start(
                    out=sums, out_offset=bass.IndirectOffsetOnAxis(ap=target[b][:, k:k + 1], axis=0),
                    in_=rows_out[b][:, k, :], in_offset=None, bounds_check=NP - 1,
                    oob_is_err=False).then_inc(scattered[b], 16)

        take(0, 0)
        take(0, 1)
        with nc.gpsimd.Fori(0, STEPS - 1) as i:
            take(i + 1, 0)
            put(i, 0)
            take(i + 1, 1)
            put(i, 1)
        put(STEPS - 1, 0)
        put(STEPS - 1, 1)
        for b in range(2):
            pool.wait_ge(scattered[b], 64 * (STEPS + 1))


def plain_pass(nc, C, name, order, table, width, slot, weight, sums):
    counts = width == P
    with Phase(nc, name) as ph:
        rows = ph.sb2("rows", [P, GT, width])
        gather_index, target = ph.sb2("gather_index", [P, GT], I32), ph.sb2("target", [P, GT], I32)
        same = ph.sb2("same", [P, ROWS], BF16)
        total, scalar_total = ph.sb2("total", [P, ROWS]), ph.sb2("scalar_total", [1, ROWS])
        out_rows = ph.sb2("out_rows", [P, GT, SW])
        turned_ps, product = ph.ps2("turned_ps", [P, ROWS]), ph.ps2("product", [P, GT, P])
        scalar_ps, scalar_back = ph.ps2("scalar_ps", [1, ROWS]), ph.ps2("scalar_back", [P, GT])
        names = ("gather_index_in", "target_in", "same_in", "gathered", "scattered", "same_used",
                 "turned", "scanned", "projected", "copied", "rows_ready")
        (gather_index_in, target_in, same_in, gathered, scattered, same_used,
         turned, scanned, projected, copied, rows_ready) = (ph.sems2(x) for x in names)
        went_on, chain, chain_act, cleared = ph.sem("went_on"), ph.sem("chain"), ph.sem("chain_act"), ph.sem("cleared")
        unit = 64
        with nc.Block() as block:
            edge_loaders(nc, order, block, slot, 1, gather_index, same, gather_index_in, same_in, gathered,
                         same_used, unit)

            def gathers(b):
                for k in range(GT):
                    gather(nc, rows[b][:, k, :], table, gather_index[b][:, k:k + 1], gathered[b], table.shape[0])

            edge_pool(nc, C, block, gathers, sums, out_rows, target, target_in, rows_ready, gathered, scattered,
                      gather_index_in, turned, went_on, unit)

            @block.tensor
            def _(pe):
                for b in range(2):
                    pe.sem_inc(turned[b], 1)
                    pe.sem_inc(projected[b], 1)
                with nc.tensor.Fori(0, STEPS) as i:
                    for b in range(2):
                        pe.wait_ge(gathered[b], i * unit + 2 * unit)
                        pe.wait_ge(scanned[b], i + 1)
                        for k in range(GT):
                            if not counts:
                                nc.tensor.transpose(scalar_ps[b][:, k * P:(k + 1) * P], rows[b][:, k, P:P + 1], C.ident[:, :])
                            last = nc.tensor.transpose(turned_ps[b][:, k * P:(k + 1) * P], rows[b][:, k, 0:P], C.ident[:, :])
                        last.then_inc(turned[b], 1)
                        pe.wait_ge(scanned[b], i + 2)
                        pe.wait_ge(copied[b], i + 1)
                        for k in range(GT):
                            nc.tensor.matmul(product[b][:, k, :], total[b][:, k * P:(k + 1) * P], weight,
                                             start=True, stop=True)
                            last = nc.tensor.matmul(scalar_back[b][:, k:k + 1], scalar_total[b][:, k * P:(k + 1) * P],
                                                    C.ones[0:1, 0:1], start=True, stop=True)
                        last.then_inc(projected[b], 1)

            @block.vector
            def _(dve):
                v = nc.vector
                link = Chain(dve, chain)
                v.memset(total[1][:, ROWS - 1:ROWS], 0.0)
                link(v.memset(scalar_total[1][:, ROWS - 1:ROWS], 0.0))
                for b in range(2):
                    dve.sem_inc(scanned[b], 1)
                link.restart()
                with v.Fori(0, STEPS) as i:
                    for b in range(2):
                        dve.wait_ge(turned[b], i + 2)
                        dve.wait_ge(same_in[b], i * 16 + 16)
                        dve.wait_ge(projected[b], i + 1)
                        source = C.ones_row[0:1, :] if counts else scalar_ps[b][:, :]
                        v.tensor_tensor_scan(scalar_total[b][:, :], same[b][0:1, :], source,
                                             scalar_total[1 - b][:, ROWS - 1:ROWS], ALU.mult, ALU.add)
                        link(v.tensor_tensor_scan(total[b][:, :], same[b][:, :], turned_ps[b][:, :],
                                                  total[1 - b][:, ROWS - 1:ROWS], ALU.mult, ALU.add))
                        link.tell(scanned[b])
                        link.tell(same_used[b])
                    link.restart()

            @block.scalar
            def _(act):
                link = Chain(act, chain_act)
                for b in range(2):
                    act.sem_inc(copied[b], 1)
                for b in range(2):
                    last = nc.scalar.copy(out_rows[b][:, :, P:SW], C.zeros[:, 0:GT * (SW - P)].rearrange("p (k c) -> p k c", k=GT))
                link(last)
                link.restart()
                with nc.scalar.Fori(0, STEPS) as i:
                    for b in range(2):
                        load_targets(act, order, i, b, target, target_in, scattered)
                        act.wait_ge(projected[b], i + 2)
                        nc.scalar.copy(out_rows[b][:, :, P], scalar_back[b][:, :])
                        link(nc.scalar.copy(out_rows[b][:, :, 0:P], product[b][:, :, :]))
                        link.tell(copied[b])
                        link.tell(rows_ready[b])
                    link.restart()


def attention_pass(nc, C, order, table, scores, sums):
    scale = float((P * HEADS) ** -0.5)
    with Phase(nc, "gat") as ph:
        rows, mine = ph.sb2("rows", [P, GT, P + HEADS]), ph.sb2("mine", [P, GT, HEADS])
        gather_index, target = ph.sb2("gather_index", [P, 2 * GT], I32), ph.sb2("target", [P, GT], I32)
        same = ph.sb2("same", [P, ROWS], BF16)
        e, ee, t1 = ph.sb2("e", [P, GT, HEADS]), ph.sb2("ee", [P, GT, HEADS]), ph.sb("t1", [P, GT, HEADS])
        weighted = ph.sb2("weighted", [P, HEADS, GT, P])
        total, scalar_total = ph.sb2("total", [P, HEADS, ROWS]), ph.sb2("scalar_total", [HEADS, ROWS])
        out_rows = ph.sb2("out_rows", [P, GT, SW])
        wsum, empty, winv = ph.sb("wsum", [P, GT, HEADS]), ph.sb("empty", [P, GT, HEADS]), ph.sb("winv", [P, GT, HEADS])
        turned_ps = [ph.ps(f"turned_ps{h}", [P, ROWS]) for h in range(HEADS)]
        product = ph.ps2("product", [P, HEADS, P])
        scalar_ps, scalar_back = ph.ps("scalar_ps", [HEADS, ROWS]), ph.ps("scalar_back", [P, GT, HEADS])
        names = ("gather_index_in", "target_in", "same_in", "gathered", "scattered", "same_used", "scores_ready",
                 "weighted_ready", "turned", "scanned", "product_ready", "product_used", "rows_ready")
        (gather_index_in, target_in, same_in, gathered, scattered, same_used, scores_ready,
         weighted_ready, turned, scanned, product_ready, product_used, rows_ready) = (ph.sems2(x) for x in names)
        sums_back, sums_used = ph.sem("sums_back"), ph.sem("sums_used")
        went_on, chain, chain_act = ph.sem("went_on"), ph.sem("chain"), ph.sem("chain_act")
        unit = 128
        with nc.Block() as block:
            edge_loaders(nc, order, block, Order.KEY, 2, gather_index, same, gather_index_in, same_in, gathered,
                         same_used, unit)

            def gathers(b):
                for k in range(GT):
                    gather(nc, rows[b][:, k, :], table, gather_index[b][:, GT + k:GT + k + 1], gathered[b], NP)
                    gather(nc, mine[b][:, k, :], scores, gather_index[b][:, k:k + 1], gathered[b], NP)

            edge_pool(nc, C, block, gathers, sums, out_rows, target, target_in, rows_ready, gathered, scattered,
                      gather_index_in, weighted_ready, went_on, unit)

            @block.scalar
            def _(act):
                link = Chain(act, chain_act)
                for b in range(2):
                    act.sem_inc(weighted_ready[b], 1)
                with nc.scalar.Fori(0, STEPS) as i:
                    for b in range(2):
                        act.wait_ge(scores_ready[b], i + 1)
                        act.wait_ge(turned[b], i + 1)
                        link(nc.scalar.activation(ee[b][:, :, :], e[b][:, :, :], ACT.Exp, scale=scale))
                        for h in range(HEADS):
                            for k in range(GT):
                                last = nc.scalar.activation(weighted[b][:, h, k, :], rows[b][:, k, 0:P], ACT.Copy,
                                                            scale=ee[b][:, k, h:h + 1])
                        link(last)
                        link.tell(weighted_ready[b])
                        load_targets(act, order, i, b, target, target_in, scattered)
                    link.restart()

            @block.tensor
            def _(pe):
                for b in range(2):
                    pe.sem_inc(turned[b], 1)
                pe.sem_inc(sums_back, 1)
                with nc.tensor.Fori(0, STEPS) as i:
                    for b in range(2):
                        pe.wait_ge(weighted_ready[b], i + 2)
                        pe.wait_ge(scanned[1 - b], i + 1 + b)
                        for k in range(GT):
                            nc.tensor.transpose(scalar_ps[:, k * P:(k + 1) * P], ee[b][:, k, :], C.ident[:, :])
                            for h in range(HEADS):
                                last = nc.tensor.transpose(turned_ps[h][:, k * P:(k + 1) * P], weighted[b][:, h, k, :], C.ident[:, :])
                        last.then_inc(turned[b], 1)
                        pe.wait_ge(scanned[b], i + 1 + 1)
                        pe.wait_ge(sums_used, i * 2 + b + 1)
                        for k in range(GT):
                            last = nc.tensor.matmul(scalar_back[:, k, :], scalar_total[b][:, k * P:(k + 1) * P],
                                                    C.ident[0:HEADS, 0:HEADS], start=True, stop=True)
                        last.then_inc(sums_back, 1)
                        for k in range(GT):
                            pe.wait_ge(product_used[k % 2], i * 4 + b * 2 + k // 2 + 1)
                            for h in range(HEADS):
                                last = nc.tensor.matmul(product[k % 2][:, h, :], total[b][:, h, k * P:(k + 1) * P],
                                                        C.heads[:, h, :], start=True, stop=True)
                            last.then_inc(product_ready[k % 2], 1)

            @block.vector
            def _(dve):
                v = nc.vector
                link = Chain(dve, chain)
                v.memset(total[1][:, :, ROWS - 1:ROWS], 0.0)
                link(v.memset(scalar_total[1][:, ROWS - 1:ROWS], 0.0))
                link.restart()
                for b in range(2):
                    dve.sem_inc(scanned[b], 1)
                    dve.sem_inc(product_used[b], 1)
                dve.sem_inc(sums_used, 1)

                def score(i, b):
                    dve.wait_ge(gathered[b], i * unit + 2 * unit)
                    dve.wait_ge(weighted_ready[b], i + 1)
                    link(v.tensor_add(t1[:, :, :], rows[b][:, :, P:P + HEADS], mine[b][:, :, :]))
                    link(v.scalar_tensor_tensor(e[b][:, :, :], t1[:, :, :], 0.2, t1[:, :, :], ALU.mult, ALU.max))
                    link.tell(scores_ready[b])

                def scan(i, b):
                    dve.wait_ge(turned[b], i + 2)
                    dve.wait_ge(same_in[b], i * 16 + 16)
                    v.tensor_tensor_scan(scalar_total[b][:, :], same[b][0:HEADS, :], scalar_ps[:, :],
                                         scalar_total[1 - b][:, ROWS - 1:ROWS], ALU.mult, ALU.add)
                    for h in range(HEADS):
                        last = v.tensor_tensor_scan(total[b][:, h, :], same[b][:, :], turned_ps[h][:, :],
                                                    total[1 - b][:, h, ROWS - 1:ROWS], ALU.mult, ALU.add)
                    link(last)
                    link.tell(scanned[b])
                    link.tell(same_used[b])

                def combine(i, b):
                    dve.wait_ge(sums_back, i * 2 + b + 2)
                    link(v.tensor_copy(wsum[:, :, :], scalar_back[:, :, :]))
                    link.tell(sums_used)
                    link(v.tensor_scalar(empty[:, :, :], wsum[:, :, :], 0.0, None, ALU.is_equal))
                    link(v.tensor_add(wsum[:, :, :], wsum[:, :, :], empty[:, :, :]))
                    link(v.reciprocal(winv[:, :, :], wsum[:, :, :]))
                    dve.wait_ge(scattered[b], i * 64 + 64)
                    v.tensor_scalar(out_rows[b][:, :, P:P + HEADS], empty[:, :, :], -1.0, 1.0, ALU.mult, ALU.add)
                    link(v.tensor_scalar(winv[:, :, :], winv[:, :, :], 1.0 / HEADS, None, ALU.mult))
                    for k in range(GT):
                        dve.wait_ge(product_ready[k % 2], i * 4 + b * 2 + k // 2 + 1)
                        o = out_rows[b][:, k, 0:P]
                        link(v.tensor_scalar(o, product[k % 2][:, 0, :], winv[:, k, 0:1], None, ALU.mult))
                        for h in range(1, HEADS):
                            link(v.scalar_tensor_tensor(o, product[k % 2][:, h, :], winv[:, k, h:h + 1], o, ALU.mult, ALU.add))
                        link.tell(product_used[k % 2])
                    link.tell(rows_ready[b])

                score(0, 0)
                link.restart()
                with v.Fori(0, STEPS - 1) as i:
                    scan(i, 0)
                    score(i, 1)
                    combine(i, 0)
                    scan(i, 1)
                    score(i + 1, 0)
                    combine(i, 1)
                    link.restart()
                scan(STEPS - 1, 0)
                score(STEPS - 1, 1)
                combine(STEPS - 1, 0)
                scan(STEPS - 1, 1)
                combine(STEPS - 1, 1)


def context_pass(nc, C, block_no, order, ctx_table, agents, sums, last_max):
    with Phase(nc, f"ctx{block_no}") as ph:
        rows, mine = ph.sb2("rows", [P, GT, 2 * P]), ph.sb2("mine", [P, GT, P])
        gather_index, target = ph.sb2("gather_index", [P, 3 * GT], I32), ph.sb2("target", [P, GT], I32)
        same = ph.sb2("same", [P, ROWS], BF16)
        prod = ph.sb("prod", [P, GT, P])
        c, ee = ph.sb2("c", [P, GT]), ph.sb2("ee", [P, GT])
        part_max, all_max, running = ph.sb("part_max", [P, 1]), ph.sb("all_max", [1, 1]), ph.sb("running", [1, 1])
        shift, neg_shift, fade = ph.sb2("shift", [P, 1]), ph.sb2("neg_shift", [P, 1]), ph.sb2("fade", [P, 1])
        begin, scalar_begin = ph.sb("begin", [P, 1]), ph.sb("scalar_begin", [1, 1])
        weighted = ph.sb2("weighted", [P, GT, P])
        total, scalar_total = ph.sb2("total", [P, ROWS]), ph.sb2("scalar_total", [1, ROWS])
        out_rows = ph.sb2("out_rows", [P, GT, SW])
        turned_ps, product = ph.ps2("turned_ps", [P, ROWS]), ph.ps2("product", [P, GT, P])
        scalar_ps, scalar_back = ph.ps("scalar_ps", [1, ROWS]), ph.ps("scalar_back", [P, GT])
        max_row, max_wide = ph.ps("max_row", [1, P]), ph.ps("max_wide", [P, 1])
        names = ("gather_index_in", "target_in", "same_in", "gathered", "scattered", "same_used", "shift_ready",
                 "weighted_ready", "turned", "scanned", "projected", "copied", "rows_ready")
        (gather_index_in, target_in, same_in, gathered, scattered, same_used, shift_ready,
         weighted_ready, turned, scanned, projected, copied, rows_ready) = (ph.sems2(x) for x in names)
        parts_ready, row_ready, max_ready, wide_ready = (ph.sem(x) for x in ("parts_ready", "row_ready", "max_ready", "wide_ready"))
        went_on, chain, chain_act = ph.sem("went_on"), ph.sem("chain"), ph.sem("chain_act")
        unit = 128
        with nc.Block() as block:
            edge_loaders(nc, order, block, Order.KEY, 3, gather_index, same, gather_index_in, same_in, gathered,
                         same_used, unit)

            def gathers(b):
                for k in range(GT):
                    gather(nc, rows[b][:, k, :], ctx_table, gather_index[b][:, 2 * GT + k:2 * GT + k + 1], gathered[b], CTX)
                    gather(nc, mine[b][:, k, :], agents, gather_index[b][:, k:k + 1], gathered[b], NP)

            edge_pool(nc, C, block, gathers, sums, out_rows, target, target_in, rows_ready, gathered, scattered,
                      gather_index_in, weighted_ready, went_on, unit)

            @block.vector
            def _(dve):
                v = nc.vector
                link = Chain(dve, chain)
                v.memset(total[1][:, ROWS - 1:ROWS], 0.0)
                v.memset(scalar_total[1][:, ROWS - 1:ROWS], 0.0)
                v.memset(running[:, :], -1e30)
                link(v.memset(shift[1][:, :], -1e30))
                link.restart()
                for b in range(2):
                    dve.sem_inc(scanned[b], 1)

                def score(i, b):
                    g = i * 2 + b
                    dve.wait_ge(gathered[b], i * unit + 2 * unit)
                    dve.wait_ge(copied[b], i + 1)
                    link(v.tensor_mul(prod[:, :, :], rows[b][:, :, 0:P], mine[b][:, :, :]))
                    link(v.tensor_reduce(c[b][:, :], prod[:, :, :], AX.X, ALU.add))
                    link(v.scalar_tensor_tensor(c[b][:, :], c[b][:, :], 0.1, c[b][:, :], ALU.mult, ALU.max))
                    link(v.tensor_add(c[b][:, :], c[b][:, :], order.pad_bias[:, ds(g * GT, GT)]))
                    link(v.tensor_reduce(part_max[:, :], c[b][:, :], AX.X, ALU.max))
                    link.tell(parts_ready)
                    dve.wait_ge(row_ready, g + 1)
                    link(v.tensor_reduce(all_max[:, :], max_row[:, :], AX.X, ALU.max))
                    link(v.tensor_tensor(running[:, :], running[:, :], all_max[:, :], ALU.max))
                    link.tell(max_ready)
                    dve.wait_ge(wide_ready, g + 1)
                    link(v.tensor_copy(shift[b][:, :], max_wide[:, :]))
                    link(v.tensor_scalar(neg_shift[b][:, :], shift[b][:, :], -1.0, None, ALU.mult))
                    link.tell(shift_ready[b])

                def scan(i, b):
                    dve.wait_ge(turned[b], i + 2)
                    dve.wait_ge(same_in[b], i * 16 + 16)
                    dve.wait_ge(projected[b], i + 1)
                    v.tensor_tensor(scalar_begin[:, :], scalar_total[1 - b][:, ROWS - 1:ROWS], fade[b][0:1, :], ALU.mult)
                    link(v.tensor_tensor(begin[:, :], total[1 - b][:, ROWS - 1:ROWS], fade[b][:, :], ALU.mult))
                    v.tensor_tensor_scan(scalar_total[b][:, :], same[b][0:1, :], scalar_ps[:, :], scalar_begin[:, :],
                                         ALU.mult, ALU.add)
                    link(v.tensor_tensor_scan(total[b][:, :], same[b][:, :], turned_ps[b][:, :], begin[:, :],
                                              ALU.mult, ALU.add))
                    link.tell(scanned[b])
                    link.tell(same_used[b])

                score(0, 0)
                link.restart()
                with v.Fori(0, STEPS - 1) as i:
                    scan(i, 0)
                    score(i, 1)
                    scan(i, 1)
                    score(i + 1, 0)
                    link.restart()
                scan(STEPS - 1, 0)
                score(STEPS - 1, 1)
                scan(STEPS - 1, 1)
                link(v.tensor_copy(last_max[:, :], shift[1][:, :]))

            @block.scalar
            def _(act):
                link = Chain(act, chain_act)
                for b in range(2):
                    act.sem_inc(weighted_ready[b], 1)
                    act.sem_inc(copied[b], 1)
                for b in range(2):
                    last = nc.scalar.copy(out_rows[b][:, :, P:SW], C.zeros[:, 0:GT * (SW - P)].rearrange("p (k c) -> p k c", k=GT))
                link(last)
                link.restart()

                def weigh(i, b):
                    act.wait_ge(shift_ready[b], i + 1)
                    act.wait_ge(turned[b], i + 1)
                    act.wait_ge(scanned[b], i + 1)
                    nc.scalar.activation(fade[b][:, :], shift[1 - b][:, :], ACT.Exp, bias=neg_shift[b][:, :])
                    link(nc.scalar.activation(ee[b][:, :], c[b][:, :], ACT.Exp, bias=neg_shift[b][:, :]))
                    for k in range(GT):
                        last = nc.scalar.activation(weighted[b][:, k, :], rows[b][:, k, P:2 * P], ACT.Copy,
                                                    scale=ee[b][:, k:k + 1])
                    link(last)
                    link.tell(weighted_ready[b])

                def copy_out(i, b):
                    load_targets(act, order, i, b, target, target_in, scattered)
                    act.wait_ge(projected[b], i + 2)
                    nc.scalar.activation(out_rows[b][:, :, P + 1], C.zeros[:, 0:GT], ACT.Identity, bias=shift[b][:, :])
                    nc.scalar.copy(out_rows[b][:, :, P], scalar_back[:, :])
                    link(nc.scalar.copy(out_rows[b][:, :, 0:P], product[b][:, :, :]))
                    link.tell(copied[b])
                    link.tell(rows_ready[b])

                weigh(0, 0)
                link.restart()
                with nc.scalar.Fori(0, STEPS - 1) as i:
                    copy_out(i, 0)
                    weigh(i, 1)
                    copy_out(i, 1)
                    weigh(i + 1, 0)
                    link.restart()
                copy_out(STEPS - 1, 0)
                weigh(STEPS - 1, 1)
                copy_out(STEPS - 1, 1)

            @block.tensor
            def _(pe):
                for b in range(2):
                    pe.sem_inc(turned[b], 1)
                    pe.sem_inc(projected[b], 1)

                def maxima(i, b):
                    g = i * 2 + b
                    pe.wait_ge(parts_ready, g + 1)
                    nc.tensor.transpose(max_row[:, :], part_max[:, :], C.ident[:, :]).then_inc(row_ready, 1)
                    pe.wait_ge(max_ready, g + 1)
                    nc.tensor.matmul(max_wide[:, :], C.ones[0:1, :], running[:, :], start=True, stop=True).then_inc(wide_ready, 1)

                def turn(i, b):
                    pe.wait_ge(weighted_ready[b], i + 2)
                    pe.wait_ge(scanned[b], i + 1)
                    pe.wait_ge(scanned[1 - b], i + 1 + b)
                    for k in range(GT):
                        nc.tensor.transpose(scalar_ps[:, k * P:(k + 1) * P], ee[b][:, k:k + 1], C.ident[:, :])
                        last = nc.tensor.transpose(turned_ps[b][:, k * P:(k + 1) * P], weighted[b][:, k, :], C.ident[:, :])
                    last.then_inc(turned[b], 1)

                def project(i, b):
                    pe.wait_ge(scanned[b], i + 2)
                    pe.wait_ge(copied[b], i + 1)
                    pe.wait_ge(copied[1 - b], i + 1 + b)
                    for k in range(GT):
                        nc.tensor.matmul(product[b][:, k, :], total[b][:, k * P:(k + 1) * P], C.t[f"Wb{block_no}"][:, :],
                                         start=True, stop=True)
                        last = nc.tensor.matmul(scalar_back[:, k:k + 1], scalar_total[b][:, k * P:(k + 1) * P],
                                                C.ones[0:1, 0:1], start=True, stop=True)
                    last.then_inc(projected[b], 1)

                maxima(0, 0)
                with nc.tensor.Fori(0, STEPS - 1) as i:
                    turn(i, 0)
                    project(i, 0)
                    maxima(i, 1)
                    turn(i, 1)
                    project(i, 1)
                    maxima(i + 1, 0)
                turn(STEPS - 1, 0)
                project(STEPS - 1, 0)
                maxima(STEPS - 1, 1)
                turn(STEPS - 1, 1)
                project(STEPS - 1, 1)


def spread(vec):
    return vec[:, :].rearrange("p (o d) -> p o d", o=1).to_broadcast([P, GT, P])


class NodePhase(Phase):

    def __init__(self, nc, C, name, loads, stores):
        super().__init__(nc, name)
        self.C, self.loads, self.stores = C, loads, stores
        self.loaded, self.used, self.done, self.stored = self.ways_sem("loaded", "used", "done", "stored")
        self.chain, self.chain_act, self.chain_pool = self.sem("chain"), self.sem("chain_act"), self.sem("chain_pool")
        self.went_on = self.sem("went_on")

    def mover(self, block, load, store, peel_load=False, peel_store=False):
        nc = self.nc

        @block.sync
        def _(sp):
            def loads(i, b, last=False):
                pairs = load(i, b, last)
                for to, of in pairs:
                    sp.dma_start(to, of).then_inc(self.loaded[b], 16)
                if len(pairs) < self.loads:
                    sp.sem_inc(self.loaded[b], 16 * (self.loads - len(pairs)))

            def stores(i, b, last=False):
                for to, of in store(i, b, last):
                    sp.dma_start(to, of).then_inc(self.stored[b], 16)

            def step(i, last_load=False):
                for b in range(WAYS):
                    sp.wait_ge(self.used[b], i + 1)
                    loads(i + 1, b, last_load)
                for b in range(WAYS):
                    sp.wait_ge(self.done[b], i + 1)
                    stores(i, b)

            for b in range(WAYS):
                sp.sem_inc(self.stored[b], 16 * self.stores)
                loads(0, b)
            with nc.sync.Fori(0, NODE_STEPS - 2) as i:
                step(i)
            step(NODE_STEPS - 2, peel_load)
            skipped = [0] * WAYS
            for b in range(WAYS):
                sp.wait_ge(self.done[b], NODE_STEPS)
                pairs = store(NODE_STEPS - 1, b, peel_store)
                skipped[b] = self.stores - len(pairs)
                for to, of in pairs:
                    sp.dma_start(to, of).then_inc(self.stored[b], 16)
            for b in range(WAYS):
                sp.wait_ge(self.stored[b], 16 * (self.stores * (NODE_STEPS + 1) - skipped[b]))

    def before_load(self, b, i):
        return i * 16 * self.loads + 16 * self.loads

    def before_store(self, i):
        return i * 16 * self.stores + 16 * self.stores


class Norm:

    def __init__(self, nc, C, ph, per_step):
        self.nc, self.C, self.per_step = nc, C, per_step
        self.stats, = ph.ways_sb([P, GT, 6], "stats")
        self.mean_var, = ph.ways_sb([P, GT, 2], "mean_var")
        self.squares, self.root, self.inv, self.bias = ph.ways_sb([P, GT], "squares", "root", "inv", "bias")
        self.junk = ph.sb("junk", [P, P])
        self.var_ready, self.root_ready = ph.ways_sem("var_ready", "root_ready")

    def stats_dve(self, link, b, x):
        v = self.nc.vector
        for k in range(GT):
            last = v.bn_stats(self.stats[b][:, k, :], x[:, k, :])
        link(last)
        for k in range(GT):
            last = v.bn_aggr(self.mean_var[b][:, k, :], self.stats[b][:, k, :])
        link(last)
        link.tell(self.var_ready[b])

    def root_act(self, act, i, b):
        act.wait_ge(self.var_ready[b], i + 1)
        self.nc.scalar.activation(self.root[b][:, :], self.mean_var[b][:, :, 1], ACT.Sqrt,
                                  bias=self.C.eps[:, :]).then_inc(self.root_ready[b], 1)

    def squares_act(self, link, b, x, divisor, eps=True):
        s = self.nc.scalar
        for k in range(GT):
            link(s.activation(self.junk[:, :], x[:, k, :], ACT.Square, accum_out=self.squares[b][:, k:k + 1]))
        kw = {"bias": self.C.eps[:, :]} if eps else {}
        link(s.activation(self.root[b][:, :], self.squares[b][:, :], ACT.Sqrt, scale=1.0 / divisor, **kw))
        link.tell(self.root_ready[b])

    def inverse_dve(self, dve, link, i, b, n, add=0.0, bias=False):
        v = self.nc.vector
        dve.wait_ge(self.root_ready[b], i * self.per_step + n + 1)
        if add:
            link(v.tensor_scalar(self.root[b][:, :], self.root[b][:, :], add, None, ALU.add))
        link(v.reciprocal(self.inv[b][:, :], self.root[b][:, :]))
        if bias:
            link(v.scalar_tensor_tensor(self.bias[b][:, :], self.mean_var[b][:, :, 0], -1.0, self.inv[b][:, :],
                                        ALU.mult, ALU.mult))

    def apply_act(self, b, x, y, func):
        for k in range(GT):
            last = self.nc.scalar.activation(y[:, k, :], x[:, k, :], func, scale=self.inv[b][:, k:k + 1],
                                             bias=self.bias[b][:, k:k + 1])
        return last


def scale_rows(v, link, out, x, scalars, other, op=ALU.add):
    for k in range(GT):
        last = v.scalar_tensor_tensor(out[:, k, :], x(k), scalars[:, k:k + 1], other(k), ALU.mult, op)
    link(last)


def input_rows(x, buf, i, b, last):
    if not last or b == 0:
        v = x[0:LASTG * ROWS, :].rearrange("(g p k) d -> p g k d", p=P, k=GT)
        return ((buf[:, :, :], v[:, ds(i * WAYS + b, 1), :, :].rearrange("p o k d -> p (o k) d")),)
    if b == 1:
        return ((buf[0:LASTP, :, :], x[LASTG * ROWS:N, :].rearrange("(p k) d -> p k d", k=GT)),)
    return ()


def norm_input(nc, C, x, h_out):
    with NodePhase(nc, C, "n0", 1, 1) as ph:
        X, H = ph.ways_sb([P, GT, P], "X", "H")
        norm = Norm(nc, C, ph, 1)
        ready, = ph.ways_sem("ready")
        with nc.Block() as block:
            ph.mover(block, lambda i, b, last: input_rows(x, X[b], i, b, last),
                     lambda i, b, last: ((group_rows(h_out, i * WAYS + b), H[b][:, :, :]),), peel_load=True)

            @block.vector
            def _(dve):
                link = Chain(dve, ph.chain)
                with nc.vector.Fori(0, NODE_STEPS) as i:
                    for b in range(WAYS):
                        dve.wait_ge(ph.loaded[b], ph.before_load(b, i))
                        norm.stats_dve(link, b, X[b])
                    for b in range(WAYS):
                        norm.inverse_dve(dve, link, i, b, 0, bias=True)
                        link.tell(ready[b])
                    link.restart()

            @block.scalar
            def _(act):
                link = Chain(act, ph.chain_act)
                with nc.scalar.Fori(0, NODE_STEPS) as i:
                    for b in range(WAYS):
                        norm.root_act(act, i, b)
                    for b in range(WAYS):
                        act.wait_ge(ready[b], i + 1)
                        act.wait_ge(ph.stored[b], ph.before_store(i))
                        link(norm.apply_act(b, X[b], H[b], ACT.Relu))
                        link.tell(ph.used[b])
                        link.tell(ph.done[b])
                    link.restart()


def sage_nodes(nc, C, x, h, sums, x_out, h_out):
    with NodePhase(nc, C, "n1", 3, 2) as ph:
        X, X1, H, HT, H1 = ph.ways_sb([P, GT, P], "X", "X1", "H", "HT", "H1")
        S, = ph.ways_sb([P, GT, SW], "S")
        inv, own = ph.ways_sb([P, GT], "count_inv", "own")
        tp, po = ph.ps2("tp", [P, GT, P]), ph.ps2("po", [P, GT, 2, P])
        norm = Norm(nc, C, ph, 1)
        turned, moved, product, added, biased, ready = ph.ways_sem("turned", "moved", "product", "added", "biased", "ready")
        with nc.Block() as block:
            ph.mover(block, lambda i, b, last: input_rows(x, X[b], i, b, last) + (
                (S[b][:, :, :], group_rows(sums, i * WAYS + b)), (H[b][:, :, :], group_rows(h, i * WAYS + b))),
                lambda i, b, last: ((group_rows(x_out, i * WAYS + b), X1[b][:, :, :]),
                                    (group_rows(h_out, i * WAYS + b), H1[b][:, :, :])), peel_load=True)

            @block.gpsimd
            def _(pool):
                link = Chain(pool, ph.chain_pool)
                with nc.gpsimd.Fori(0, NODE_STEPS) as i:
                    for b in range(WAYS):
                        pool_wait(pool, ph.loaded[b], ph.before_load(b, i), ph.went_on)
                        link(nc.gpsimd.tensor_add(X[b][:, :, :], X[b][:, :, :], spread(C.v["bl"])))
                        link.tell(biased[b])
                    link.restart()

            @block.tensor
            def _(pe):
                for b in range(WAYS):
                    pe.sem_inc(added[b], 1)
                with nc.tensor.Fori(0, NODE_STEPS) as i:
                    for b in range(WAYS):
                        pe.wait_ge(ph.loaded[b], ph.before_load(b, i))
                        if b >= 2:
                            pe.wait_ge(moved[b - 2], i + 1)
                        for k in range(GT):
                            last = nc.tensor.transpose(tp[b % 2][:, k, :], H[b][:, k, :], C.ident[:, :])
                        last.then_inc(turned[b], 1)
                    for b in range(WAYS):
                        pe.wait_ge(moved[b], i + 1)
                        pe.wait_ge(added[(b + 2) % WAYS], i + 1 + (b >= 2))
                        for k in range(GT):
                            last = nc.tensor.matmul(po[b % 2][:, k, :, :].rearrange("p a d -> p (a d)"), HT[b][:, k, :],
                                                    C.wlr[:, :, :].rearrange("p a d -> p (a d)"), start=True, stop=True)
                        last.then_inc(product[b], 1)

            @block.vector
            def _(dve):
                v = nc.vector
                link = Chain(dve, ph.chain)
                with v.Fori(0, NODE_STEPS) as i:
                    for b in range(WAYS):
                        dve.wait_ge(ph.loaded[b], ph.before_load(b, i))
                        link(v.tensor_scalar(inv[b][:, :], S[b][:, :, P], 1.0, None, ALU.max))
                        link(v.reciprocal(inv[b][:, :], inv[b][:, :]))
                        v.tensor_scalar(own[b][:, :], S[b][:, :, P], 0.0, -1.0, ALU.is_gt, ALU.mult)
                        dve.wait_ge(ph.stored[b], ph.before_store(i))
                        dve.wait_ge(biased[b], i + 1)
                        scale_rows(v, link, X1[b], lambda k: S[b][:, k, 0:P], inv[b], lambda k: X[b][:, k, :])
                    for b in range(WAYS):
                        dve.wait_ge(product[b], i + 1)
                        link.tell(ph.used[b])
                        scale_rows(v, link, X1[b], lambda k: po[b % 2][:, k, 0, :], own[b], lambda k: X1[b][:, k, :])
                        link(v.tensor_add(X1[b][:, :, :], X1[b][:, :, :], po[b % 2][:, :, 1, :]))
                        link.tell(added[b])
                        norm.stats_dve(link, b, X1[b])
                    for b in range(WAYS):
                        norm.inverse_dve(dve, link, i, b, 0, bias=True)
                        link.tell(ready[b])
                    link.restart()

            @block.scalar
            def _(act):
                link = Chain(act, ph.chain_act)
                with nc.scalar.Fori(0, NODE_STEPS) as i:
                    for b in range(WAYS):
                        act.wait_ge(turned[b], i + 1)
                        link(nc.scalar.copy(HT[b][:, :, :], tp[b % 2][:, :, :]))
                        link.tell(moved[b])
                    for b in range(WAYS):
                        norm.root_act(act, i, b)
                    for b in range(WAYS):
                        act.wait_ge(ready[b], i + 1)
                        link(norm.apply_act(b, X1[b], H1[b], ACT.Relu))
                        link.tell(ph.done[b])
                    link.restart()


def hyper_rows(nc, C, name, sums, e_out, affine):
    steps = HGROUPS // 2
    with Phase(nc, name) as ph:
        ph.loaded, ph.used, ph.done, ph.stored = (ph.sems2(n) for n in ("loaded", "used", "done", "stored"))
        ph.chain, ph.went_on = ph.sem("chain"), ph.sem("went_on")
        S, E = ph.sb2("S", [P, GT, SW]), ph.sb2("E", [P, GT, P + 1])
        inv, has = ph.sb2("inv", [P, GT]), ph.sb2("has", [P, GT])
        with nc.Block() as block:
            @block.sync
            def _(sp):
                for b in range(2):
                    sp.sem_inc(ph.used[b], 1)
                with nc.sync.Fori(0, steps) as i:
                    for b in range(2):
                        sp.wait_ge(ph.used[b], i + 1)
                        sp.dma_start(S[b][:, :, :], group_rows(sums, i * 2 + b)).then_inc(ph.loaded[b], 16)

            @block.vector
            def _(dve):
                v = nc.vector
                link = Chain(dve, ph.chain)
                with v.Fori(0, steps) as i:
                    for b in range(2):
                        dve.wait_ge(ph.loaded[b], i * 16 + 16)
                        v.tensor_scalar(has[b][:, :], S[b][:, :, P], 0.0, None, ALU.is_gt)
                        link(v.tensor_scalar(inv[b][:, :], S[b][:, :, P], 1.0, None, ALU.max))
                        link(v.reciprocal(inv[b][:, :], inv[b][:, :]))
                        dve.wait_ge(ph.stored[b], i * 16 + 16)
                        v.tensor_copy(E[b][:, :, P], C.hw[:, ds(i * 2 + b, 1), :].rearrange("p o k -> p (o k)"))
                        for k in range(GT):
                            last = v.tensor_scalar(E[b][:, k, 0:P], S[b][:, k, 0:P], inv[b][:, k:k + 1], None, ALU.mult)
                        link(last)
                        if affine:
                            link(v.tensor_mul(E[b][:, :, 0:P], E[b][:, :, 0:P], spread(C.bn_scale)))
                            for k in range(GT):
                                last = v.scalar_tensor_tensor(E[b][:, k, 0:P], C.bn_bias[:, :], has[b][:, k:k + 1],
                                                              E[b][:, k, 0:P], ALU.mult, ALU.add)
                            link(last)
                        link.tell(ph.used[b])
                        link.tell(ph.done[b])
                    link.restart()

            @block.gpsimd
            def _(pool):
                for b in range(2):
                    nc.gpsimd.dma_start(C.credit[b:b + 1, :], C.eps[0:1, :]).then_inc(ph.stored[b], 16)
                with nc.gpsimd.Fori(0, steps) as i:
                    for b in range(2):
                        pool_wait(pool, ph.done[b], i + 1, ph.went_on)
                        nc.gpsimd.dma_start(group_rows(e_out, i * 2 + b), E[b][:, :, :]).then_inc(ph.stored[b], 16)
                for b in range(2):
                    pool.wait_ge(ph.stored[b], 16 * (steps + 1))


def inverse_degree(link, v, d, one, inv):
    link(v.tensor_scalar(one, d, 0.0, None, ALU.is_gt))
    link(v.tensor_tensor(inv, d, one, ALU.mult))
    link(v.scalar_tensor_tensor(inv, one, -1.0, inv, ALU.mult, ALU.add))
    link(v.tensor_scalar(inv, inv, 1.0, None, ALU.add))
    link(v.reciprocal(inv, inv))
    link(v.tensor_tensor(inv, inv, one, ALU.mult))


def hyper_nodes1(nc, C, sums, g_out):
    with NodePhase(nc, C, "n3", 1, 1) as ph:
        S, = ph.ways_sb([P, GT, SW], "S")
        G, Q = ph.ways_sb([P, GT, P], "G", "Q")
        one, inv = ph.ways_sb([P, GT], "one", "inv")
        sum_ps, square_ps = ph.ps("sum_ps", [1, ROWS]), ph.ps("square_ps", [1, ROWS])
        wide_ps = ph.ps("wide_ps", [P, 2, P])
        part = ph.sb("part", [1, 2, ROWS])
        mean, second, var, row = ph.sb("mean", [1, P]), ph.sb("second", [1, P]), ph.sb("var", [1, P]), ph.sb("row", [1, 2, P])
        summed, squared = ph.ways_sem("summed", "squared")
        all_summed, var_ready, root_ready, row_ready, wide_ready = (ph.sem(n) for n in (
            "all_summed", "var_ready", "root_ready", "row_ready", "wide_ready"))
        with nc.Block() as block:
            ph.mover(block, lambda i, b, last: ((S[b][:, :, :], group_rows(sums, i * WAYS + b)),),
                     lambda i, b, last: ((group_rows(g_out, i * WAYS + b), G[b][:, :, :]),))

            @block.vector
            def _(dve):
                v = nc.vector
                link = Chain(dve, ph.chain)
                with v.Fori(0, NODE_STEPS) as i:
                    for b in range(WAYS):
                        dve.wait_ge(ph.loaded[b], ph.before_load(b, i))
                        inverse_degree(link, v, S[b][:, :, P], one[b][:, :], inv[b][:, :])
                        dve.wait_ge(ph.stored[b], ph.before_store(i))
                        dve.wait_ge(summed[b], i + 1)
                        for k in range(GT):
                            last = v.tensor_scalar(G[b][:, k, :], S[b][:, k, 0:P], inv[b][:, k:k + 1], None, ALU.mult)
                        link(last)
                        link.tell(ph.used[b])
                        link.tell(ph.done[b])
                    link.restart()
                dve.wait_ge(all_summed, 1)
                v.tensor_copy(part[:, 0, :], sum_ps[:, :])
                link(v.tensor_copy(part[:, 1, :], square_ps[:, :]))
                for j, to in enumerate((mean, second)):
                    link(v.tensor_add(part[:, j, 0:2 * P], part[:, j, 0:2 * P], part[:, j, 2 * P:4 * P]))
                    link(v.tensor_add(part[:, j, 0:P], part[:, j, 0:P], part[:, j, P:2 * P]))
                    link(v.tensor_scalar(to[:, :], part[:, j, 0:P], 1.0 / N, None, ALU.mult))
                link(v.tensor_mul(var[:, :], mean[:, :], mean[:, :]))
                link(v.tensor_sub(var[:, :], second[:, :], var[:, :]))
                link(v.tensor_scalar(var[:, :], var[:, :], 0.0, None, ALU.max))
                link.tell(var_ready)
                dve.wait_ge(root_ready, 1)
                link(v.reciprocal(var[:, :], var[:, :]))
                link(v.tensor_mul(row[:, 0, :], var[:, :], C.v["gamma"][0:1, :]))
                link(v.tensor_mul(mean[:, :], mean[:, :], row[:, 0, :]))
                link(v.tensor_sub(row[:, 1, :], C.v["beta"][0:1, :], mean[:, :]))
                link.tell(row_ready)
                dve.wait_ge(wide_ready, 1)
                v.tensor_copy(C.bn_scale[:, :], wide_ps[:, 0, :])
                link(v.tensor_copy(C.bn_bias[:, :], wide_ps[:, 1, :]))

            @block.scalar
            def _(act):
                with nc.scalar.Fori(0, NODE_STEPS) as i:
                    for b in range(WAYS):
                        act.wait_ge(ph.done[b], i + 1)
                        nc.scalar.activation(Q[b][:, :, :], G[b][:, :, :], ACT.Square).then_inc(squared[b], 1)
                act.wait_ge(var_ready, 1)
                nc.scalar.activation(var[:, :], var[:, :], ACT.Sqrt, bias=C.eps[0:1, :]).then_inc(root_ready, 1)

            @block.tensor
            def _(pe):
                for b in range(WAYS):
                    pe.sem_inc(summed[b], 1)
                z = C.zeros[:, 0:1]
                for o in (sum_ps, square_ps):
                    for k in range(GT):
                        nc.tensor.matmul(o[:, k * P:(k + 1) * P], z, C.zeros[:, :], start=(k == 0), stop=False,
                                         skip_group_check=True)
                with nc.tensor.Fori(0, NODE_STEPS) as i:
                    for b in range(WAYS):
                        pe.wait_ge(squared[b], i + 1)
                        nc.tensor.matmul(sum_ps[:, :], C.ones[:, 0:1], G[b][:, :, :].rearrange("p k d -> p (k d)"),
                                         start=False, stop=False, skip_group_check=True)
                        nc.tensor.matmul(square_ps[:, :], C.ones[:, 0:1], Q[b][:, :, :].rearrange("p k d -> p (k d)"),
                                         start=False, stop=False, skip_group_check=True).then_inc(summed[b], 1)
                for o in (sum_ps, square_ps):
                    last = nc.tensor.matmul(o[:, 0:P], z, C.zeros[:, :], start=False, stop=True, skip_group_check=True)
                last.then_inc(all_summed, 1)
                pe.wait_ge(row_ready, 1)
                nc.tensor.matmul(wide_ps[:, :, :].rearrange("p a d -> p (a d)"), C.ones[0:1, :],
                                 row[:, :, :].rearrange("p a d -> p (a d)"), start=True, stop=True).then_inc(wide_ready, 1)


def hyper_nodes2(nc, C, x, sums, x_out, h_out, score_out):
    with NodePhase(nc, C, "n4", 2, 3) as ph:
        X, X2, HT = ph.ways_sb([P, GT, P], "X", "X2", "HT")
        S, = ph.ways_sb([P, GT, SW], "S")
        H, = ph.ways_sb([P, GT, P + HEADS], "H")
        scores, = ph.ways_sb([P, GT, HEADS], "scores")
        one, inv = ph.ways_sb([P, GT], "one", "inv_degree")
        tp, scores_ps = ph.ps2("tp", [P, GT, P]), [ph.ps(f"scores_ps{b}", [P, GT, 2 * HEADS]) for b in range(WAYS)]
        norm = Norm(nc, C, ph, 1)
        turned, moved, product, biased, ready, relued = ph.ways_sem("turned", "moved", "product", "biased", "ready", "relued")

        def score_bias(at):
            return C.score_b[:, at:at + HEADS].rearrange("p (o d) -> p o d", o=1).to_broadcast([P, GT, HEADS])

        with nc.Block() as block:
            ph.mover(block, lambda i, b, last: ((X[b][:, :, :], group_rows(x, i * WAYS + b)),
                                                (S[b][:, :, :], group_rows(sums, i * WAYS + b))),
                     lambda i, b, last: ((group_rows(x_out, i * WAYS + b), X2[b][:, :, :]),
                                         (group_rows(h_out, i * WAYS + b), H[b][:, :, :]),
                                         (group_rows(score_out, i * WAYS + b), scores[b][:, :, :])))

            @block.gpsimd
            def _(pool):
                link = Chain(pool, ph.chain_pool)
                with nc.gpsimd.Fori(0, NODE_STEPS) as i:
                    for b in range(WAYS):
                        pool_wait(pool, ph.loaded[b], ph.before_load(b, i), ph.went_on)
                        link(nc.gpsimd.tensor_add(X[b][:, :, :], X[b][:, :, :], spread(C.v["b2"])))
                        link.tell(biased[b])
                    link.restart()

            @block.vector
            def _(dve):
                v = nc.vector
                link = Chain(dve, ph.chain)
                with v.Fori(0, NODE_STEPS) as i:
                    for b in range(WAYS):
                        dve.wait_ge(ph.loaded[b], ph.before_load(b, i))
                        inverse_degree(link, v, S[b][:, :, P], one[b][:, :], inv[b][:, :])
                        dve.wait_ge(ph.stored[b], ph.before_store(i))
                        dve.wait_ge(biased[b], i + 1)
                        scale_rows(v, link, X2[b], lambda k: S[b][:, k, 0:P], inv[b], lambda k: X[b][:, k, :])
                        link.tell(ph.used[b])
                        norm.stats_dve(link, b, X2[b])
                    for b in range(WAYS):
                        norm.inverse_dve(dve, link, i, b, 0, bias=True)
                        link.tell(ready[b])
                    for b in range(WAYS):
                        dve.wait_ge(product[b], i + 1)
                        v.tensor_add(scores[b][:, :, :], scores_ps[b][:, :, 0:HEADS], score_bias(0))
                        link(v.tensor_add(H[b][:, :, P:P + HEADS], scores_ps[b][:, :, HEADS:2 * HEADS], score_bias(HEADS)))
                        link.tell(ph.done[b])
                    link.restart()

            @block.scalar
            def _(act):
                link = Chain(act, ph.chain_act)
                with nc.scalar.Fori(0, NODE_STEPS) as i:
                    for b in range(WAYS):
                        norm.root_act(act, i, b)
                    for b in range(WAYS):
                        act.wait_ge(ready[b], i + 1)
                        link(norm.apply_act(b, X2[b], H[b][:, :, 0:P], ACT.Relu))
                        link.tell(relued[b])
                    for b in range(WAYS):
                        act.wait_ge(turned[b], i + 1)
                        link(nc.scalar.copy(HT[b][:, :, :], tp[b % 2][:, :, :]))
                        link.tell(moved[b])
                    link.restart()

            @block.tensor
            def _(pe):
                with nc.tensor.Fori(0, NODE_STEPS) as i:
                    for b in range(WAYS):
                        pe.wait_ge(relued[b], i + 1)
                        if b >= 2:
                            pe.wait_ge(moved[b - 2], i + 1)
                        for k in range(GT):
                            last = nc.tensor.transpose(tp[b % 2][:, k, :], H[b][:, k, 0:P], C.ident[:, :])
                        last.then_inc(turned[b], 1)
                    for b in range(WAYS):
                        pe.wait_ge(moved[b], i + 1)
                        for k in range(GT):
                            last = nc.tensor.matmul(scores_ps[b][:, k, :], HT[b][:, k, :], C.score_w[:, :], start=True, stop=True)
                        last.then_inc(product[b], 1)


def attention_nodes(nc, C, x, h, sums, x_out, h_out):
    with NodePhase(nc, C, "n5", 3, 2) as ph:
        X, X3, H, HT, A, T, Y, R, H3 = ph.ways_sb([P, GT, P], "X", "X3", "H", "HT", "A", "T", "Y", "R", "H3")
        S, = ph.ways_sb([P, GT, SW], "S")
        empty, = ph.ways_sb([P, GT, HEADS], "empty")
        tp, out_ps = ph.ps2("tp", [P, GT, P]), ph.ps2("out_ps", [P, GT, P])
        heads_ps = [ph.ps(f"heads_ps{k}", [P, HEADS, P]) for k in range(GT)]
        norm = Norm(nc, C, ph, 2)
        (turned, moved, product, empty_ready, based, summed, scaled, biased, relued, ready, xbiased, added) = ph.ways_sem(
            "turned", "moved", "product", "empty_ready", "based", "summed", "scaled", "biased", "relued", "ready", "xbiased", "added")
        fourth = ph.ways_sem("fourth")[0]
        heads_ready = [ph.sem(f"heads_ready{k}") for k in range(GT)]
        heads_used = [ph.sem(f"heads_used{k}") for k in range(GT)]
        heads_added = [ph.sem(f"heads_added{k}") for k in range(GT)]
        with nc.Block() as block:
            ph.mover(block, lambda i, b, last: ((X[b][:, :, :], group_rows(x, i * WAYS + b)),
                                                (S[b][:, :, :], group_rows(sums, i * WAYS + b)),
                                                (H[b][:, :, :], group_rows(h, i * WAYS + b, 0, P))),
                     lambda i, b, last: ((group_rows(x_out, i * WAYS + b), X3[b][:, :, :]),
                                         (group_rows(h_out, i * WAYS + b), H3[b][:, :, :])))

            def project_rows(pe, i, b):
                pe.wait_ge(moved[b], i * 2 + 2)
                if b >= 2:
                    pe.wait_ge(added[b - 2], i + 1)
                for k in range(GT):
                    last = nc.tensor.matmul(out_ps[b % 2][:, k, :], HT[b][:, k, :], C.t["V"][:, :], start=True, stop=True)
                last.then_inc(product[b], 1)

            @block.tensor
            def _(pe):
                for k in range(GT):
                    pe.sem_inc(heads_used[k], 1)
                with nc.tensor.Fori(0, NODE_STEPS) as i:
                    for b in range(WAYS):
                        pe.wait_ge(ph.loaded[b], ph.before_load(b, i))
                        if b >= 2:
                            pe.wait_ge(moved[b - 2], i * 2 + 1)
                        for k in range(GT):
                            last = nc.tensor.transpose(tp[b % 2][:, k, :], H[b][:, k, :], C.ident[:, :])
                        last.then_inc(turned[b], 1)
                    for b in range(WAYS):
                        pe.wait_ge(moved[b], i * 2 + 1)
                        for k in range(GT):
                            pe.wait_ge(heads_used[k], i * WAYS + b + 1)
                            nc.tensor.matmul(heads_ps[k][:, :, :].rearrange("p a d -> p (a d)"), HT[b][:, k, :],
                                             C.heads[:, :, :].rearrange("p a d -> p (a d)"), start=True,
                                             stop=True).then_inc(heads_ready[k], 1)
                    for b in range(WAYS):
                        pe.wait_ge(relued[b], i + 1)
                        if b >= 2:
                            pe.wait_ge(moved[b - 2], i * 2 + 2)
                        for k in range(GT):
                            last = nc.tensor.transpose(tp[b % 2][:, k, :], R[b][:, k, :], C.ident[:, :])
                        last.then_inc(turned[b], 1)
                        if b >= 1:
                            project_rows(pe, i, b - 1)
                    project_rows(pe, i, WAYS - 1)

            @block.gpsimd
            def _(pool):
                g = nc.gpsimd
                link = Chain(pool, ph.chain_pool)
                with g.Fori(0, NODE_STEPS) as i:
                    for b in range(WAYS):
                        pool_wait(pool, ph.loaded[b], ph.before_load(b, i), ph.went_on)
                        link(g.tensor_add(X[b][:, :, :], X[b][:, :, :], spread(C.v["Vb"])))
                        link.tell(xbiased[b])
                    for b in range(WAYS):
                        pool_wait(pool, fourth[b], i + 1, ph.went_on)
                        link(g.tensor_add(T[b][:, :, :], T[b][:, :, :], spread(C.mean_b)))
                        link.tell(based[b])
                    for b in range(WAYS):
                        pool_wait(pool, scaled[b], i + 1, ph.went_on)
                        link(g.tensor_add(Y[b][:, :, :], Y[b][:, :, :], spread(C.v["ln_b"])))
                        link.tell(biased[b])
                    link.restart()

            def add_fourth(dve, link, i, b):
                dve.wait_ge(based[b], i + 1)
                link(nc.vector.tensor_add(A[b][:, :, :], A[b][:, :, :], T[b][:, :, :]))
                link.tell(summed[b])

            @block.vector
            def _(dve):
                v = nc.vector
                link = Chain(dve, ph.chain)
                with v.Fori(0, NODE_STEPS) as i:
                    for b in range(WAYS):
                        dve.wait_ge(ph.loaded[b], ph.before_load(b, i))
                        link(v.tensor_scalar(empty[b][:, :, :], S[b][:, :, P:P + HEADS], -1.0 / HEADS, 1.0 / HEADS, ALU.mult, ALU.add))
                        link.tell(empty_ready[b])
                    for b in range(WAYS):
                        for k in range(GT):
                            dve.wait_ge(heads_ready[k], i * WAYS + b + 1)
                            for a in range(HEADS - 1):
                                link(v.scalar_tensor_tensor(A[b][:, k, :], heads_ps[k][:, a, :], empty[b][:, k, a:a + 1],
                                                            (A[b] if a else S[b])[:, k, 0:P], ALU.mult, ALU.add))
                            link.tell(heads_added[k])
                        if b >= 1:
                            add_fourth(dve, link, i, b - 1)
                    add_fourth(dve, link, i, WAYS - 1)
                    for b in range(WAYS):
                        norm.inverse_dve(dve, link, i, b, 0, add=1e-6)
                        scale_rows(v, link, Y[b], lambda k: A[b][:, k, :], norm.inv[b], lambda k: C.v["ln_g"][:, :], ALU.mult)
                        link.tell(scaled[b])
                    for b in range(WAYS):
                        dve.wait_ge(product[b], i + 1)
                        dve.wait_ge(xbiased[b], i + 1)
                        dve.wait_ge(ph.stored[b], ph.before_store(i))
                        link(v.tensor_add(X3[b][:, :, :], X[b][:, :, :], out_ps[b % 2][:, :, :]))
                        link.tell(ph.used[b])
                        link.tell(added[b])
                        norm.stats_dve(link, b, X3[b])
                    for b in range(WAYS):
                        norm.inverse_dve(dve, link, i, b, 1, bias=True)
                        link.tell(ready[b])
                    link.restart()

            def deviation(act, link, i, b):
                act.wait_ge(summed[b], i + 1)
                norm.squares_act(link, b, A[b], P - 1.0, eps=False)

            def move_back(act, link, i, b):
                act.wait_ge(turned[b], i * 2 + 2)
                link(nc.scalar.copy(HT[b][:, :, :], tp[b % 2][:, :, :]))
                link.tell(moved[b])

            @block.scalar
            def _(act):
                link = Chain(act, ph.chain_act)
                with nc.scalar.Fori(0, NODE_STEPS) as i:
                    for b in range(WAYS):
                        act.wait_ge(turned[b], i * 2 + 1)
                        link(nc.scalar.copy(HT[b][:, :, :], tp[b % 2][:, :, :]))
                        link.tell(moved[b])
                    for b in range(WAYS):
                        act.wait_ge(empty_ready[b], i + 1)
                        for k in range(GT):
                            act.wait_ge(heads_added[k], i * WAYS + b + 1)
                            link(nc.scalar.activation(T[b][:, k, :], heads_ps[k][:, HEADS - 1, :], ACT.Copy,
                                                      scale=empty[b][:, k, HEADS - 1:HEADS]))
                            link.tell(heads_used[k])
                        link.tell(fourth[b])
                        if b >= 2:
                            deviation(act, link, i, b - 2)
                    for b in range(WAYS - 2, WAYS):
                        deviation(act, link, i, b)
                    for b in range(WAYS):
                        act.wait_ge(biased[b], i + 1)
                        link(nc.scalar.activation(R[b][:, :, :], Y[b][:, :, :], ACT.Relu))
                        link.tell(relued[b])
                        if b >= 1:
                            move_back(act, link, i, b - 1)
                    move_back(act, link, i, WAYS - 1)
                    for b in range(WAYS):
                        norm.root_act(act, i, b)
                    for b in range(WAYS):
                        act.wait_ge(ready[b], i + 1)
                        link(norm.apply_act(b, X3[b], H3[b], ACT.Relu))
                        link.tell(ph.done[b])
                    link.restart()



def context_tables(nc, C, context, tables):
    full = CTX // P
    rest = CTX - full * P
    with Phase(nc, "ctxt") as ph:
        X = ph.sb("X", [P, CTILES, P])
        XC, XT = ph.sb("XC", [P, P]), ph.sb("XT", [P, P])
        T = ph.sb("T", [P, CTILES, 2, 2, P])
        stats, pair, work = ph.sb("stats", [P, 2, 6]), ph.sb("pair", [P, 2, 2]), ph.sb("work", [P, 2, P])
        mean_var, root = ph.sb("mean_var", [P, CTILES, 2, 2]), ph.sb("root", [P, CTILES, 2])
        tp, po = ph.ps("tp", [P, P]), ph.ps("po", [P, 2, 2, P])
        loaded, cleared, fetched, turned, moved, product, copied, var_ready, root_ready, done, stored, chain = (
            ph.sem(n) for n in ("loaded", "cleared", "fetched", "turned", "moved", "product", "copied", "var_ready",
                                "root_ready", "done", "stored", "chain"))
        with nc.Block() as block:
            @block.sync
            def _(sp):
                sp.wait_ge(cleared, 1)
                sp.dma_start(X[:, 0:full, :], context[0:full * P, :].rearrange("(t p) d -> p t d", p=P)).then_inc(loaded, 16)
                sp.dma_start(X[0:rest, full, :], context[full * P:CTX, :]).then_inc(loaded, 16)
                sp.wait_ge(done, 1)
                for k in range(2):
                    sp.dma_start(tables[k][0:full * P, :].rearrange("(t p) c -> p t c", p=P),
                                 T[:, 0:full, k, :, :].rearrange("p t a d -> p t (a d)")).then_inc(stored, 16)
                    sp.dma_start(tables[k][full * P:CTX, :], T[0:rest, full, k, :, :].rearrange("p a d -> p (a d)")).then_inc(stored, 16)
                sp.wait_ge(stored, 64)

            @block.tensor
            def _(pe):
                with nc.tensor.Fori(0, CTILES) as t:
                    pe.wait_ge(fetched, t + 1)
                    nc.tensor.transpose(tp[:, :], XC[:, :], C.ident[:, :]).then_inc(turned, 1)
                    pe.wait_ge(moved, t + 1)
                    nc.tensor.matmul(po[:, :, :, :].rearrange("p k a d -> p (k a d)"), XT[:, :],
                                     C.ctxw[:, :, :, :].rearrange("p k a d -> p (k a d)"), start=True, stop=True).then_inc(product, 1)

            @block.scalar
            def _(act):
                act.wait_ge(loaded, 32)
                with nc.scalar.Fori(0, CTILES) as t:
                    nc.scalar.copy(XC[:, :], X[:, ds(t, 1), :].rearrange("p o d -> p (o d)")).then_inc(fetched, 1)
                    act.wait_ge(turned, t + 1)
                    nc.scalar.copy(XT[:, :], tp[:, :]).then_inc(moved, 1)
                    act.wait_ge(product, t + 1)
                    nc.scalar.copy(T[:, ds(t, 1), :, :, :].rearrange("p o k a d -> p (o k a d)"),
                                   po[:, :, :, :].rearrange("p k a d -> p (k a d)")).then_inc(copied, 1)
                    act.wait_ge(copied, t + 1)
                act.wait_ge(var_ready, 1)
                nc.scalar.activation(root[:, :, :], mean_var[:, :, :, 1], ACT.Sqrt, bias=C.eps[:, :]).then_inc(root_ready, 1)

            @block.vector
            def _(dve):
                v = nc.vector
                link = Chain(dve, chain)
                link(v.memset(X[:, :, :], 0.0))
                link.tell(cleared)
                link.restart()

                def projected(t, k):
                    return T[:, ds(t, 1), k, 1, :].rearrange("p o d -> p (o d)")

                with v.Fori(0, CTILES) as t:
                    dve.wait_ge(copied, t + 1)
                    for k in range(2):
                        last = v.bn_stats(stats[:, k, :], projected(t, k))
                    link(last)
                    for k in range(2):
                        last = v.bn_aggr(pair[:, k, :], stats[:, k, :])
                    link(last)
                    link(v.tensor_copy(mean_var[:, ds(t, 1), :, :].rearrange("p o k c -> p (o k) c"), pair[:, :, :]))
                    link.restart()
                link.tell(var_ready)
                dve.wait_ge(root_ready, 1)
                link(v.reciprocal(root[:, :, :], root[:, :, :]))
                link.restart()
                with v.Fori(0, CTILES) as t:
                    link(v.tensor_copy(pair[:, :, 0], mean_var[:, ds(t, 1), :, 0].rearrange("p o k -> p (o k)")))
                    link(v.tensor_copy(pair[:, :, 1], root[:, ds(t, 1), :].rearrange("p o k -> p (o k)")))
                    for k in range(2):
                        link(v.tensor_scalar(work[:, k, :], projected(t, k), pair[:, k, 0:1], pair[:, k, 1:2],
                                             ALU.subtract, ALU.mult))
                        link(v.tensor_mul(work[:, k, :], work[:, k, :], C.v[f"gnc_w{k}"][:, :]))
                        link(v.tensor_add(projected(t, k), work[:, k, :], C.v[f"gnc_b{k}"][:, :]))
                    link.restart()
                link.tell(done)


def agent_nodes(nc, C, block_no, agents, sums, last_max, agents_out, x, out):
    final = out is not None
    with NodePhase(nc, C, f"n6{block_no}", 3 if final else 2, 1) as ph:
        A, AT, B, Y, Z, R, O = ph.ways_sb([P, GT, P], "A", "AT", "B", "Y", "Z", "R", "O")
        S, = ph.ways_sb([P, GT, SW], "S")
        X = ph.ways_sb([P, GT, P], "X")[0] if final else None
        low, fade, share = ph.ways_sb([P, GT], "low", "fade", "share")
        neg_max = ph.sb("neg_max", [P, 1])
        tp, out_ps = ph.ps2("tp", [P, GT, P]), [ph.ps(f"out_ps{b}", [P, GT, P]) for b in range(WAYS)]
        norm = Norm(nc, C, ph, 3)
        (turned, moved, product, faded, low_ready, summed, scaled, biased, ready, relued, abiased, whole) = ph.ways_sem(
            "turned", "moved", "product", "faded", "low_ready", "summed", "scaled", "biased", "ready", "relued", "abiased", "whole")

        def w(name):
            return C.v[f"{name}{block_no}"]

        def loads(i, b, last):
            g = i * WAYS + b
            pairs = ((A[b][:, :, :], group_rows(agents, g)), (S[b][:, :, :], group_rows(sums, g)))
            return pairs + (((X[b][:, :, :], group_rows(x, g)),) if final else ())

        def stores(i, b, last):
            g = i * WAYS + b
            if not final:
                return ((group_rows(agents_out, g), O[b][:, :, :]),)
            if not last or b == 0:
                o = out[0:LASTG * ROWS, :].rearrange("(g p k) d -> p g k d", p=P, k=GT)
                return ((o[:, ds(g, 1), :, :].rearrange("p o k d -> p (o k) d"), O[b][:, :, :]),)
            if b == 1:
                return ((out[LASTG * ROWS:N, :].rearrange("(p k) d -> p k d", k=GT), O[b][0:LASTP, :, :]),)
            return ()

        with nc.Block() as block:
            ph.mover(block, loads, stores, peel_store=final)

            @block.tensor
            def _(pe):
                def project(i, b, n, weight):
                    pe.wait_ge(moved[b], i * 2 + n + 1)
                    for k in range(GT):
                        last = nc.tensor.matmul(out_ps[b][:, k, :], AT[b][:, k, :], weight[:, :], start=True, stop=True)
                    last.then_inc(product[b], 1)

                for b in range(WAYS):
                    pe.sem_inc(whole[b], 1)
                with nc.tensor.Fori(0, NODE_STEPS) as i:
                    for b in range(WAYS):
                        pe.wait_ge(ph.loaded[b], ph.before_load(b, i))
                        if b >= 2:
                            pe.wait_ge(moved[b - 2], i * 2 + 1)
                        for k in range(GT):
                            last = nc.tensor.transpose(tp[b % 2][:, k, :], A[b][:, k, :], C.ident[:, :])
                        last.then_inc(turned[b], 1)
                        if b >= 1:
                            pe.wait_ge(whole[b - 1], i + 1)
                            project(i, b - 1, 0, C.t[f"Wa{block_no}"])
                    pe.wait_ge(whole[WAYS - 1], i + 1)
                    project(i, WAYS - 1, 0, C.t[f"Wa{block_no}"])
                    for b in range(WAYS):
                        pe.wait_ge(relued[b], i + 1)
                        if b >= 2:
                            pe.wait_ge(moved[b - 2], i * 2 + 2)
                        for k in range(GT):
                            last = nc.tensor.transpose(tp[b % 2][:, k, :], R[b][:, k, :], C.ident[:, :])
                        last.then_inc(turned[b], 1)
                        if b >= 1:
                            project(i, b - 1, 1, C.t[f"Wlin{block_no}"])
                    project(i, WAYS - 1, 1, C.t[f"Wlin{block_no}"])

            @block.gpsimd
            def _(pool):
                g = nc.gpsimd
                link = Chain(pool, ph.chain_pool)
                with g.Fori(0, NODE_STEPS) as i:
                    for b in range(WAYS):
                        pool_wait(pool, ph.loaded[b], ph.before_load(b, i), ph.went_on)
                        link(g.tensor_add(B[b][:, :, :], A[b][:, :, :], spread(w("gnl_b"))))
                        link.tell(abiased[b])
                    for n, name in enumerate(("gna_b", "norm_b")):
                        for b in range(WAYS):
                            pool_wait(pool, scaled[b], i * 2 + n + 1, ph.went_on)
                            link(g.tensor_add(Z[b][:, :, :], Z[b][:, :, :], spread(w(name))))
                            link.tell(biased[b])
                    link.restart()

            @block.vector
            def _(dve):
                v = nc.vector
                link = Chain(dve, ph.chain)
                link(v.tensor_scalar(neg_max[:, :], last_max[:, :], -1.0, None, ALU.mult))
                link.restart()
                with v.Fori(0, NODE_STEPS) as i:
                    for b in range(WAYS):
                        dve.wait_ge(ph.loaded[b], ph.before_load(b, i))
                        link(v.tensor_scalar(low[b][:, :], S[b][:, :, P + 1], neg_max[:, :], 0.0, ALU.add, ALU.min))
                        link.tell(low_ready[b])
                    for b in range(WAYS):
                        dve.wait_ge(faded[b], i + 1)
                        link(v.tensor_tensor(share[b][:, :], fade[b][:, :], S[b][:, :, P], ALU.mult))
                        link(v.tensor_scalar(share[b][:, :], share[b][:, :], 1e-16, None, ALU.add))
                        link(v.reciprocal(share[b][:, :], share[b][:, :]))
                        link(v.tensor_tensor(share[b][:, :], share[b][:, :], fade[b][:, :], ALU.mult))
                        dve.wait_ge(product[b], i * 2 + 1)
                        scale_rows(v, link, Y[b], lambda k: S[b][:, k, 0:P], share[b], lambda k: out_ps[b][:, k, :])
                        link.tell(summed[b])
                    for b in range(WAYS):
                        norm.inverse_dve(dve, link, i, b, 0)
                        scale_rows(v, link, Z[b], lambda k: Y[b][:, k, :], norm.inv[b], lambda k: w("gna_w")[:, :], ALU.mult)
                        link.tell(scaled[b])
                    for b in range(WAYS):
                        dve.wait_ge(biased[b], i * 2 + 1)
                        norm.stats_dve(link, b, Z[b])
                    for b in range(WAYS):
                        dve.wait_ge(norm.root_ready[b], i * 3 + 2)
                        link(v.reciprocal(norm.inv[b][:, :], norm.root[b][:, :]))
                        for k in range(GT):
                            last = v.tensor_scalar(Y[b][:, k, :], Z[b][:, k, :], norm.mean_var[b][:, k, 0:1],
                                                   norm.inv[b][:, k:k + 1], ALU.subtract, ALU.mult)
                        link(last)
                        link(v.tensor_mul(Z[b][:, :, :], Y[b][:, :, :], spread(w("norm_w"))))
                        link.tell(scaled[b])
                    for b in range(WAYS):
                        norm.inverse_dve(dve, link, i, b, 2)
                        scale_rows(v, link, Y[b], lambda k: out_ps[b][:, k, :], norm.inv[b], lambda k: w("gnl_w")[:, :], ALU.mult)
                        link.tell(whole[b])
                        dve.wait_ge(abiased[b], i + 1)
                        if final:
                            dve.wait_ge(ph.stored[b], ph.before_store(i))
                            link(v.tensor_add(Y[b][:, :, :], Y[b][:, :, :], B[b][:, :, :]))
                            link(v.scalar_tensor_tensor(O[b][:, :, :], Y[b][:, :, :], 0.0, X[b][:, :, :], ALU.max, ALU.add))
                            link.tell(ph.used[b])
                            link.tell(ph.done[b])
                        else:
                            link(v.tensor_add(Y[b][:, :, :], Y[b][:, :, :], B[b][:, :, :]))
                            link.tell(ph.used[b])
                            link.tell(ready[b])
                    link.restart()

            @block.scalar
            def _(act):
                link = Chain(act, ph.chain_act)
                with nc.scalar.Fori(0, NODE_STEPS) as i:
                    def move(b, n):
                        act.wait_ge(turned[b], i * 2 + n + 1)
                        link(nc.scalar.copy(AT[b][:, :, :], tp[b % 2][:, :, :]))
                        link.tell(moved[b])

                    for b in range(WAYS):
                        move(b, 0)
                        act.wait_ge(low_ready[b], i + 1)
                        link(nc.scalar.activation(fade[b][:, :], low[b][:, :], ACT.Exp))
                        link.tell(faded[b])
                    for b in range(WAYS):
                        act.wait_ge(summed[b], i + 1)
                        norm.squares_act(link, b, Y[b], float(P))
                    for b in range(WAYS):
                        norm.root_act(act, i, b)
                    for b in range(WAYS):
                        act.wait_ge(biased[b], i * 2 + 2)
                        link(nc.scalar.activation(R[b][:, :, :], Z[b][:, :, :], ACT.Relu))
                        link.tell(relued[b])
                        if b >= 1:
                            move(b - 1, 1)
                    move(WAYS - 1, 1)
                    for b in range(WAYS):
                        act.wait_ge(product[b], i * 2 + 2)
                        norm.squares_act(link, b, out_ps[b], float(P))
                    if not final:
                        for b in range(WAYS):
                            act.wait_ge(ready[b], i + 1)
                            act.wait_ge(ph.stored[b], ph.before_store(i))
                            link(nc.scalar.activation(O[b][:, :, :], Y[b][:, :, :], ACT.Relu))
                            link.tell(ph.done[b])
                    link.restart()


def gnn_layers(nc, w, out):
    with ExitStack() as ctx:
        def dram(name, shape, dt=FP32):
            return nc.dram_tensor(name, shape, dt, kind="Internal").ap()

        C = make_consts(nc, ctx, w)
        C.bn_scale = ctx.enter_context(nc.sbuf_tensor("bn_scale", [P, P], FP32))
        C.bn_bias = ctx.enter_context(nc.sbuf_tensor("bn_bias", [P, P], FP32))
        last_max = ctx.enter_context(nc.sbuf_tensor("last_max", [P, 1], FP32))
        by_dst_sums, by_src_sums = dram("by_dst_sums", (NODE_ROWS, SW)), dram("by_src_sums", (NODE_ROWS, SW))
        digit_rows = dram("digit_rows", (NP,), BF16)
        h0, h1, g, x1, x2, x3, a0, a1 = (dram(n, (NODE_ROWS, P)) for n in ("h0", "h1", "g", "x1", "x2", "x3", "a0", "a1"))
        h2, src_scores = dram("h2", (NODE_ROWS, P + HEADS)), dram("src_scores", (NODE_ROWS, HEADS))
        hyper = dram("hyper", (HGROUPS * ROWS, P + 1))
        ctx_tables = [dram(f"ctx_table{k}", (CTX, 2 * P)) for k in range(2)]

        fill_zero(nc, C, (by_dst_sums, by_src_sums))
        orders = {name: Order(nc, ctx, name) for name in ("by_src", "by_dst")}
        with ExitStack() as sorting:
            A = sorting.enter_context(nc.sbuf_tensor("pairs", [P, TILES, 2], I32))
            for name, key, other, limit in (("by_src", "src", "dst", HYPER), ("by_dst", "dst", "src", CTX)):
                once, twice = dram(f"{name}_once", (NP, 2), I32), dram(f"{name}_twice", (NP, 2), I32)
                load_edges(nc, A, w[key], w[other], name)
                sort_pass(nc, C, name + "_low", A, once, digit_rows, 0)
                reload_pairs(nc, A, once, name + "_reload")
                sort_pass(nc, C, name + "_high", A, twice, digit_rows, 8)
                describe_order(nc, C, A, twice, orders[name], limit)
        by_src, by_dst = orders["by_src"], orders["by_dst"]
        norm_input(nc, C, w["x"], h0)
        plain_pass(nc, C, "sage", by_dst, h0, P, Order.OTHER, C.wlr[:, 0, :], by_dst_sums)
        sage_nodes(nc, C, w["x"], h0, by_dst_sums, x1, h1)
        for step, (rows, weight) in enumerate(((h1, "W1"), (g, "W2"))):
            plain_pass(nc, C, f"hyper_in{step}", by_dst, rows, P, Order.OTHER, C.ident[:, :], by_dst_sums)
            hyper_rows(nc, C, f"hyper_rows{step}", by_dst_sums, hyper, affine=step == 1)
            plain_pass(nc, C, f"hyper_out{step}", by_src, hyper, P + 1, Order.CLAMPED, C.t[weight][:, :], by_src_sums)
            if step == 0:
                hyper_nodes1(nc, C, by_src_sums, g)
        hyper_nodes2(nc, C, x1, by_src_sums, x2, h2, src_scores)
        attention_pass(nc, C, by_src, h2, src_scores, by_src_sums)
        attention_nodes(nc, C, x2, h2, by_src_sums, x3, a0)
        context_tables(nc, C, w["L3_gnn_ctx"], ctx_tables)
        for k in range(2):
            agents = (a0, a1)[k]
            context_pass(nc, C, k, by_dst, ctx_tables[k], agents, by_dst_sums, last_max)
            agent_nodes(nc, C, k, agents, by_dst_sums, last_max, a1, x3, out if k == 1 else None)


_OUTS = [((50000, 128), "float32")]


def kernel(**inputs):
    import numpy as _np
    import concourse.bacc as _bacc
    from concourse import mybir as _mybir
    from concourse.bass_utils import run_bass_kernel_spmd as _run

    nc = _bacc.Bacc("TRN2", target_bir_lowering=False, num_devices=1)
    arrays, args = {}, {}
    for name, value in inputs.items():
        a = _np.ascontiguousarray(value)
        arrays[f"in_{name}_dram"] = a
        args[name] = nc.dram_tensor(f"in_{name}_dram", a.shape, _mybir.dt.from_np(a.dtype), kind="ExternalInput").ap()
    out = nc.dram_tensor("out_0_dram", _OUTS[0][0], _mybir.dt.float32, kind="ExternalOutput").ap()
    gnn_layers(nc, args, out)
    r = _run(nc, [arrays], core_ids=[0])
    return r.results[0]["out_0_dram"]
```

```python
import concourse.bass as bass
from concourse import mybir
from contextlib import ExitStack, contextmanager

FP32 = mybir.dt.float32
BF16 = mybir.dt.bfloat16
I32 = mybir.dt.int32
ALU = mybir.AluOpType
ACT = mybir.ActivationFunctionType
AX = mybir.AxisListType
ds = bass.ds

P = 128
N = 50000
GT = 4
ROWS = GT * P
GROUPS = -(-N // (2 * ROWS)) * 2
STEPS = GROUPS // 2
TILES = GROUPS * GT
NP = TILES * P
LASTG = N // ROWS
LASTP = (N - LASTG * ROWS) // GT
FULLP = N // TILES
RESTT = N - FULLP * TILES
PAD_KEY = 65535
HYPER = 10000
HGROUPS = 20
WAYS = 4
NODE_STEPS = 25
NODE_ROWS = NODE_STEPS * WAYS * ROWS
CTX = 3125
CTILES = 25
HEADS = 4
SW = 132


class Chain:

    def __init__(self, eng, sem):
        self.eng, self.sem, self.n = eng, sem, 0

    def __call__(self, ins):
        self.n += 1
        ins.then_inc(self.sem, 1)
        self.eng.wait_ge(self.sem, self.n)

    def tell(self, sem, by=1):
        self.eng.sem_inc(sem, by)

    def restart(self):
        self.eng.sem_clear(self.sem)
        self.n = 0


class Phase:

    def __init__(self, nc, name):
        self.nc, self.name, self.ctx, self.sems = nc, name, ExitStack(), []

    def sem(self, name):
        s = self.ctx.enter_context(self.nc.semaphore(f"{self.name}_{name}"))
        self.sems.append(s)
        return s

    def sems2(self, name):
        return [self.sem(f"{name}{b}") for b in range(2)]

    def ways_sem(self, *names):
        return [[self.sem(f"{n}{b}") for b in range(WAYS)] for n in names]

    def ways_sb(self, shape, *names):
        return [[self.sb(f"{n}{b}", shape) for b in range(WAYS)] for n in names]

    def sb(self, name, shape, dt=FP32):
        return self.ctx.enter_context(self.nc.sbuf_tensor(f"{self.name}_{name}", shape, dt))

    def sb2(self, name, shape, dt=FP32):
        return [self.sb(f"{name}{b}", shape, dt) for b in range(2)]

    def ps(self, name, shape, dt=FP32):
        return self.ctx.enter_context(self.nc.psum_tensor(f"{self.name}_{name}", shape, dt))

    def ps2(self, name, shape, dt=FP32):
        return [self.ps(f"{name}{b}", shape, dt) for b in range(2)]

    def __enter__(self):
        return self

    def __exit__(self, *exc):
        if exc[0] is None:
            with self.nc.Block() as block:
                @block.gpsimd
                def _(pool):
                    pool.dma_reset()
                    for s in self.sems:
                        pool.sem_clear(s)
        self.ctx.close()


def pool_wait(pool, sem, value, went_on):
    pool.wait_ge(sem, value)
    pool.sem_inc(went_on, 1)


def first_credit(nc, C, b, sem):
    nc.gpsimd.dma_start(C.credit[b:b + 1, :], C.eps[0:1, :]).then_inc(sem, 64)


def group_rows(table, g, lo=0, hi=None):
    v = table.rearrange("(g p k) d -> p g k d", p=P, k=GT)
    hi = table.shape[1] if hi is None else hi
    return v[:, ds(g, 1), :, lo:hi].rearrange("p o k d -> p (o k) d")


class Consts:
    pass


def make_consts(nc, ctx, w):
    C = Consts()

    def sb(name, shape, dt=FP32):
        return ctx.enter_context(nc.sbuf_tensor(name, shape, dt))

    C.ident = sb("ident", [P, P])
    C.ones = sb("ones", [P, P])
    C.zeros = sb("zeros", [P, P])
    C.ones_row = sb("ones_row", [1, ROWS])
    C.lower = sb("lower", [P, P], BF16)
    C.unit = sb("unit", [P, 2], BF16)
    C.ones_bf = sb("ones_bf", [P, 1], BF16)
    C.upper = sb("upper", [P, P])
    C.digit_free = sb("digit_free", [P, 256], BF16)
    C.digit_part = sb("digit_part", [P, 2])
    C.row_number = sb("row_number", [P, GT])
    C.eps = sb("eps", [P, 1])
    C.credit = nc.dram_tensor("credit", (4, 1), FP32, kind="Internal").ap()
    C.hw = sb("hw", [P, HGROUPS, GT])
    mats = {"Wl": w["L0_gnn_Wl"], "Wr": w["L0_gnn_Wr"], "W1": w["L1_gnn_W1"], "W2": w["L1_gnn_W2"],
            "V": w["L2_gnn_V_w"]}
    for h in range(HEADS):
        mats[f"W{h}h"] = w["L2_gnn_W_w"][h]
    for k in range(2):
        mats[f"Wctx{k}"] = w["L3_gnn_Wctx"][k]
        mats[f"Wlin{k}"] = w["L3_gnn_Wlin"][k]
        mats[f"Wa{k}"] = w["L3_gnn_Wagt"][k][:, 0:P]
        mats[f"Wb{k}"] = w["L3_gnn_Wagt"][k][:, P:2 * P]
        mats[f"Wq{k}"] = w["L3_gnn_Wq"][k]
        mats[f"Wk{k}"] = w["L3_gnn_Wk"][k]
    names = list(mats)
    raw = sb("raw_weights", [P, len(names), P])
    C.wlr = sb("wlr", [P, 2, P])
    C.heads = sb("heads", [P, HEADS, P])
    C.ctxw = sb("ctxw", [P, 2, 2, P])
    C.t = {}
    for n in names:
        C.t[n] = sb("T_" + n, [P, P])
    vecs = {"bl": w["L0_gnn_bl"], "b2": w["L1_gnn_b2"], "gamma": w["L1_gnn_gamma"], "beta": w["L1_gnn_beta"],
            "Vb": w["L2_gnn_V_b"], "ln_g": w["L2_gnn_ln_g"], "ln_b": w["L2_gnn_ln_b"]}
    for h in range(HEADS):
        vecs[f"Wb{h}"] = w["L2_gnn_W_b"][h]
    for k in range(2):
        for v in ("gnc_w", "gnc_b", "gna_w", "gna_b", "norm_w", "norm_b", "gnl_w", "gnl_b"):
            vecs[f"{v}{k}"] = w[f"L3_gnn_{v}"][k]
    C.v = {n: sb("V_" + n, [P, P]) for n in vecs}
    C.mean_b = sb("mean_b", [P, P])
    C.row_mean = sb("row_mean", [P, 1])
    C.acol = sb("acol", [P, 2 * HEADS])
    C.bcol = sb("bcol", [P, HEADS])
    C.bwide = sb("bwide", [P, HEADS, P])
    C.score_w = sb("score_w", [P, 2 * HEADS])
    C.score_b = sb("score_b", [P, 2 * HEADS])

    with Phase(nc, "setup") as ph:
        loaded, made, ready, moved = ph.sem("loaded"), ph.sem("made"), ph.sem("ready"), ph.sem("moved")
        hwset = ph.sem("hwset")
        chain_s, chain_g = ph.sem("chain_dve"), ph.sem("chain_pool")
        tp = ph.ps2("tp", [P, P])
        n_loads = [0]
        with nc.Block() as block:
            @block.sync
            def _(sp):
                for j, n in enumerate(names):
                    sp.dma_start(raw[:, j, :], mats[n]).then_inc(loaded, 16)
                    n_loads[0] += 1
                for n, v in vecs.items():
                    sp.dma_start(C.v[n][:, :], v.rearrange("(a n) -> a n", a=1).partition_broadcast(P)
                                 if v.ndim == 1 else v).then_inc(loaded, 16)
                    n_loads[0] += 1
                with nc.allow_non_contiguous_dma(reason="small columns, once"):
                    for half in range(2):
                        sp.dma_start(C.acol[:, half * HEADS:(half + 1) * HEADS],
                                     w["L2_gnn_a"][:, half * P:(half + 1) * P].rearrange("h d -> d h")).then_inc(loaded, 16)
                        n_loads[0] += 1
                    sp.dma_start(C.bcol[:, :], w["L2_gnn_W_b"].rearrange("h d -> d h")).then_inc(loaded, 16)
                    n_loads[0] += 1
                sp.wait_ge(hwset, 1)
                full = HYPER // ROWS
                rest = (HYPER - full * ROWS) // GT
                sp.dma_start(C.hw[:, 0:full, :], w["L1_gnn_hyperedge_weight"][0:full * ROWS]
                             .rearrange("(g p k) -> p g k", p=P, k=GT)).then_inc(loaded, 16)
                sp.dma_start(C.hw[0:rest, full, :], w["L1_gnn_hyperedge_weight"][full * ROWS:HYPER]
                             .rearrange("(p k) -> p k", k=GT)).then_inc(loaded, 16)
                n_loads[0] += 2
                sp.wait_ge(loaded, 16 * n_loads[0])

            @block.gpsimd
            def _(pool):
                link = Chain(pool, chain_g)
                g = nc.gpsimd
                link(g.memset(C.ident[:, :], 0.0))
                link(g.affine_select(out=C.ident[:, :], in_=C.ident[:, :], compare_op=ALU.not_equal, fill=1.0,
                                     base=0, pattern=[[-1, P]], channel_multiplier=1))
                link(g.memset(C.upper[:, :], 1.0))
                link(g.affine_select(out=C.upper[:, :], in_=C.upper[:, :], compare_op=ALU.is_gt, fill=0.0,
                                     base=0, pattern=[[1, P]], channel_multiplier=-1))
                link(g.iota(C.digit_free[:, :], pattern=[[1, 256]], base=0, channel_multiplier=0,
                            allow_small_or_imprecise_dtypes=True))
                link(g.iota(C.row_number[:, :], pattern=[[1, GT]], base=0, channel_multiplier=GT,
                            allow_small_or_imprecise_dtypes=True))
                link(g.iota(C.digit_part[:, :], pattern=[[P, 2]], base=0, channel_multiplier=1,
                            allow_small_or_imprecise_dtypes=True))
                link.tell(made)

            @block.vector
            def _(dve):
                link = Chain(dve, chain_s)
                v = nc.vector
                link(v.memset(C.hw[:, :, :], 0.0))
                link.tell(hwset)
                v.memset(C.ones[:, :], 1.0)
                v.memset(C.zeros[:, :], 0.0)
                v.memset(C.ones_row[:, :], 1.0)
                v.memset(C.ones_bf[:, :], 1.0)
                link(v.memset(C.unit[:, :], 0.0))
                link(v.memset(C.unit[:, 0:1], 1.0))
                link(v.memset(C.eps[:, :], 1e-5))
                dve.wait_ge(made, 1)
                link(v.tensor_copy(C.lower[:, :], C.upper[:, :]))
                dve.wait_ge(loaded, 16 * n_loads[0])
                link(v.tensor_add(C.mean_b[:, :], C.v["Wb0"][:, :], C.v["Wb1"][:, :]))
                link(v.tensor_add(C.mean_b[:, :], C.mean_b[:, :], C.v["Wb2"][:, :]))
                link(v.tensor_add(C.mean_b[:, :], C.mean_b[:, :], C.v["Wb3"][:, :]))
                link(v.tensor_scalar(C.mean_b[:, :], C.mean_b[:, :], 1.0 / HEADS, None, ALU.mult))
                for h in range(HEADS):
                    link(v.tensor_scalar(C.bwide[:, h, :], C.ones[:, :], C.bcol[:, h:h + 1], None, ALU.mult))
                link.tell(made)

            jobs = []
            for j, n in enumerate(names):
                if n[:2] in ("Wq", "Wk"):
                    continue
                jobs.append((n, raw[:, j, :], C.ident[:, :], P))
            at = {n: j for j, n in enumerate(names)}
            for k in range(2):
                jobs.append((f"Wq{k}", raw[:, at[f"Wk{k}"], :], raw[:, at[f"Wq{k}"], :], P))
            for h in range(HEADS):
                for s in range(2):
                    c = s * HEADS + h
                    jobs.append((("w", c), raw[:, at[f"W{h}h"], :], C.acol[:, c:c + 1], 1))
                    jobs.append((("b", c), C.bwide[:, h, :], C.acol[:, c:c + 1], 1))

            @block.tensor
            def _(pe):
                pe.wait_ge(made, 2)
                pe.wait_ge(loaded, 16 * n_loads[0])
                for j, (n, left, right, width) in enumerate(jobs):
                    if j >= 2:
                        pe.wait_ge(moved, j - 1)
                    nc.tensor.matmul(tp[j % 2][:, 0:width], left, right, start=True, stop=True).then_inc(ready, 1)

            places = {"Wl": C.wlr[:, 0, :], "Wr": C.wlr[:, 1, :]}
            for h in range(HEADS):
                places[f"W{h}h"] = C.heads[:, h, :]
            for k in range(2):
                places[f"Wq{k}"] = C.ctxw[:, k, 0, :]
                places[f"Wctx{k}"] = C.ctxw[:, k, 1, :]
            for c in range(2 * HEADS):
                places["w", c] = C.score_w[:, c:c + 1]
                places["b", c] = C.score_b[:, c:c + 1]

            centred = [C.mean_b[:, :]] + [C.heads[:, h, :] for h in range(HEADS)]
            centred += [C.t[f"{n}{k}"][:, :] for n in ("Wa", "Wb", "Wlin") for k in range(2)]

            @block.scalar
            def _(act):
                for j, (n, _, _, width) in enumerate(jobs):
                    act.wait_ge(ready, j + 1)
                    to = places[n] if n in places else C.t[n][:, :]
                    nc.scalar.copy(to, tp[j % 2][:, 0:width]).then_inc(moved, 1)
                act.wait_ge(moved, len(jobs))
    with Phase(nc, "centre") as ph:
        chain = ph.sem("chain")
        with nc.Block() as block:
            @block.vector
            def _(dve):
                link = Chain(dve, chain)
                for m in centred:
                    link(nc.vector.tensor_reduce(C.row_mean[:, :], m, AX.X, ALU.add))
                    link(nc.vector.tensor_scalar(C.row_mean[:, :], C.row_mean[:, :], 1.0 / P, None, ALU.mult))
                    link(nc.vector.tensor_scalar(m, m, C.row_mean[:, :], None, ALU.subtract))
    return C


def load_edges(nc, A, keys, others, name):
    with Phase(nc, "edges_" + name) as ph:
        raw = [ph.sb("key", [P, TILES], I32), ph.sb("other", [P, TILES], I32)]
        loaded, padded, chain = ph.sem("loaded"), ph.sem("padded"), ph.sem("chain")
        with nc.Block() as block:
            @block.sync
            def _(sp):
                sp.wait_ge(padded, 1)
                for r, v in zip(raw, (keys, others)):
                    sp.dma_start(r[0:FULLP, :], v[0:FULLP * TILES].rearrange("(p t) -> p t", t=TILES)).then_inc(loaded, 16)
                    sp.dma_start(r[FULLP:FULLP + 1, 0:RESTT], v[FULLP * TILES:N].rearrange("(p t) -> p t", p=1)).then_inc(loaded, 16)
                sp.wait_ge(loaded, 64)

            @block.vector
            def _(dve):
                link = Chain(dve, chain)
                link(nc.vector.memset(raw[0][:, :], PAD_KEY))
                link(nc.vector.memset(raw[1][:, :], 0))
                link.tell(padded)
                dve.wait_ge(loaded, 64)
                link(nc.vector.tensor_copy(A[:, :, 0], raw[0][:, :]))
                link(nc.vector.tensor_copy(A[:, :, 1], raw[1][:, :]))


def sort_pass(nc, C, name, A, table, digit_rows, shift, zeroed=None):
    with Phase(nc, name) as ph:
        digit_i = ph.sb("digit_i", [P, TILES], I32)
        digit = ph.sb("digit", [P, TILES])
        rows = ph.sb("rows", [P, GT, P], BF16)
        onehot = ph.sb2("onehot", [P, GT, 256], BF16)
        running = ph.sb("running", [P, 2, TILES])
        counts = ph.sb("counts", [P, 2, TILES])
        base = ph.sb("base", [P, 2])
        start_i = ph.sb("start_i", [P, 2, TILES], I32)
        part_i = ph.sb("part_i", [P, 2, TILES], I32)
        start = ph.sb("start", [P, 2, TILES, 2], BF16)
        wide = ph.sb2("wide", [P, ROWS], BF16)
        member = ph.sb2("member", [P, 2, ROWS], BF16)
        before = ph.sb2("before", [P, GT, P], BF16)
        parts = ph.sb2("parts", [P, GT, 2])
        pos = ph.sb2("pos", [P, GT], I32)
        pos_lo = ph.sb2("pos_lo", [P, GT], I32)
        pos_hi = ph.sb2("pos_hi", [P, GT], I32)
        where = ph.sb2("where", [P, GT], I32)
        pairs = ph.sb2("pairs", [P, GT, 2], I32)
        tp = ph.ps("tp", [P, 4, P])
        count_ps = [ph.ps(f"count{h}", [P, 512]) for h in range(2)]
        base_ps = ph.ps("base_ps", [P, 2])
        pos_ps = ph.ps2("pos_ps", [P, GT, 2])
        digits_ready, turned, rows_ready, rows_out = (ph.sem(x) for x in ("digits_ready", "turned", "rows_ready", "rows_out"))
        chain = ph.sem("chain")
        hot, counted = ph.sems2("hot"), ph.sems2("counted")
        totals_ready, base_ready, start_ready = (ph.sem(x) for x in ("totals_ready", "base_ready", "start_ready"))
        wide_in, wide_used = ph.sems2("wide_in"), ph.sems2("wide_used")
        member_ready, placed, taken = ph.sems2("member_ready"), ph.sems2("placed"), ph.sems2("taken")
        where_ready, scattered = ph.sems2("where_ready"), ph.sems2("scattered")
        went_on = ph.sem("went_on")
        fill = ph.sb("fill", [P, 16 * SW]) if zeroed is not None else None
        filled, fill_ready = ph.sem("filled"), ph.sem("fill_ready")
        tail = TILES - 3 * P
        digit_tiles = digit_rows.rearrange("(t c) -> t c", c=P)
        with nc.Block() as block:
            @block.sync
            def _(sp):
                for b in range(2):
                    sp.sem_inc(wide_used[b], 1)
                sp.wait_ge(rows_ready, 1)
                sp.dma_start(digit_tiles[0:3 * P, :].rearrange("(j p) c -> p j c", p=P), rows[:, 0:3, :]).then_inc(rows_out, 16)
                sp.dma_start(digit_tiles[3 * P:TILES, :], rows[0:tail, 3, :]).then_inc(rows_out, 16)
                sp.wait_ge(rows_out, 32)
                with nc.sync.Fori(0, STEPS) as i:
                    for b in range(2):
                        sp.wait_ge(wide_used[b], i + 1)
                        sp.dma_start(wide[b][:, :], digit_rows[ds((i * 2 + b) * ROWS, ROWS)]
                                     .rearrange("(a n) -> a n", a=1).partition_broadcast(P)).then_inc(wide_in[b], 16)

            @block.tensor
            def _(pe):
                pe.wait_ge(digits_ready, 1)
                for j in range(4):
                    w = P if j < 3 else tail
                    last = nc.tensor.transpose(tp[0:w, j, :], digit[:, j * P:j * P + w], C.ident[:, :])
                last.then_inc(turned, 1)
                with nc.tensor.Fori(0, STEPS) as i:
                    for b in range(2):
                        pe.wait_ge(hot[b], i + 1)
                        for k in range(GT):
                            for h in range(2):
                                last = nc.tensor.matmul(count_ps[h][:, ds(i * 8 + b * 4 + k, 1)],
                                                        onehot[b][:, k, h * P:(h + 1) * P], C.ones_bf[:, :],
                                                        start=True, stop=True)
                        last.then_inc(counted[b], 1)
                pe.wait_ge(totals_ready, 1)
                nc.tensor.matmul(base_ps[:, 0:1], C.upper[:, :], running[:, 0, TILES - 1:TILES], start=True, stop=True)
                nc.tensor.matmul(base_ps[:, 1:2], C.upper[:, :], running[:, 1, TILES - 1:TILES], start=True, stop=False)
                nc.tensor.matmul(base_ps[:, 1:2], C.ones[:, :], running[:, 0, TILES - 1:TILES], start=False, stop=True).then_inc(base_ready, 1)
                pe.wait_ge(start_ready, 1)
                with nc.tensor.Fori(0, STEPS) as i:
                    for b in range(2):
                        pe.wait_ge(member_ready[b], i + 1)
                        pe.wait_ge(taken[b], i + 1)
                        for k in range(GT):
                            t = i * 8 + b * 4 + k
                            o = pos_ps[b][:, k, :]
                            nc.tensor.matmul(o, before[b][:, k, :], C.unit[:, :], start=True, stop=False)
                            for h in range(2):
                                last = nc.tensor.matmul(o, member[b][:, h, k * P:(k + 1) * P],
                                                        start[:, h, ds(t, 1), :].rearrange("p o c -> p (o c)"),
                                                        start=False, stop=(h == 1))
                        last.then_inc(placed[b], 1)

            @block.scalar
            def _(act):
                act.wait_ge(turned, 1)
                nc.scalar.copy(rows[:, 0:3, :], tp[:, 0:3, :]).then_inc(went_on, 1)
                act.wait_ge(went_on, 1)
                nc.scalar.copy(rows[0:tail, 3, :], tp[0:tail, 3, :]).then_inc(rows_ready, 1)
                if zeroed is not None:
                    chunks = zeroed.rearrange("(c p r) w -> c p (r w)", p=P, r=16)
                    act.wait_ge(fill_ready, 1)
                    for c in range(NODE_ROWS // (P * 16)):
                        nc.scalar.dma_start(chunks[c], fill[:, :]).then_inc(filled, 16)
                    act.wait_ge(filled, 16 * (NODE_ROWS // (P * 16)))

            @block.vector
            def _(dve):
                v = nc.vector
                link = Chain(dve, chain)
                if zeroed is not None:
                    v.memset(fill[:, :], 0.0).then_inc(fill_ready, 1)
                link(v.tensor_scalar(digit_i[:, :], A[:, :, 0], shift, 255, ALU.logical_shift_right, ALU.bitwise_and))
                link(v.tensor_copy(digit[:, :], digit_i[:, :]))
                link.tell(digits_ready)
                for b in range(2):
                    dve.sem_inc(counted[b], 1)
                    dve.sem_inc(taken[b], 1)
                link.restart()
                with v.Fori(0, STEPS) as i:
                    for b in range(2):
                        dve.wait_ge(counted[b], i + 1)
                        for k in range(GT):
                            last = v.tensor_scalar(onehot[b][:, k, :], C.digit_free[:, :],
                                                   digit[:, ds(i * 8 + b * 4 + k, 1)], None, ALU.is_equal)
                        last.then_inc(hot[b], 1)
                for b in range(2):
                    dve.wait_ge(counted[b], STEPS + 1)
                for h in range(2):
                    link(v.tensor_copy(counts[:, h, :], count_ps[h][:, 0:TILES]))
                    link(v.tensor_tensor_scan(running[:, h, :], counts[:, h, :], counts[:, h, :], 0.0,
                                              ALU.add, ALU.bypass))
                link.tell(totals_ready)
                dve.wait_ge(base_ready, 1)
                link(v.tensor_copy(base[:, :], base_ps[:, :]))
                for h in range(2):
                    link(v.tensor_sub(running[:, h, :], running[:, h, :], counts[:, h, :]))
                    link(v.tensor_scalar(start_i[:, h, :], running[:, h, :], base[:, h:h + 1], None, ALU.add))
                link(v.tensor_scalar(part_i[:, :, :], start_i[:, :, :], 255, None, ALU.bitwise_and))
                link(v.tensor_copy(start[:, :, :, 0], part_i[:, :, :]))
                link(v.tensor_scalar(part_i[:, :, :], start_i[:, :, :], 8, None, ALU.logical_shift_right))
                link(v.tensor_copy(start[:, :, :, 1], part_i[:, :, :]))
                link.tell(start_ready)
                link.restart()
                with v.Fori(0, STEPS) as i:
                    for b in range(2):
                        dve.wait_ge(wide_in[b], i * 16 + 16)
                        for h in range(2):
                            v.tensor_scalar(member[b][:, h, :], wide[b][:, :], C.digit_part[:, h:h + 1], None, ALU.is_equal)
                        for k in range(GT):
                            last = v.scalar_tensor_tensor(before[b][:, k, :], wide[b][:, k * P:(k + 1) * P],
                                                          digit[:, ds(i * 8 + b * 4 + k, 1)], C.lower[:, :],
                                                          ALU.is_equal, ALU.mult)
                        link(last)
                        link.tell(wide_used[b])
                        link.tell(member_ready[b])
                    for b in range(2):
                        dve.wait_ge(placed[b], i + 1)
                        link(v.tensor_copy(parts[b][:, :, :], pos_ps[b][:, :, :]))
                        link.tell(taken[b])
                        dve.wait_ge(scattered[b], i * 64 + 64)
                        link(v.scalar_tensor_tensor(pos[b][:, :], parts[b][:, :, 1], 256.0, parts[b][:, :, 0], ALU.mult, ALU.add))
                        v.tensor_scalar(pos_lo[b][:, :], pos[b][:, :], P - 1, None, ALU.bitwise_and)
                        v.tensor_copy(pairs[b][:, :, :], A[:, ds(i * 8 + b * 4, GT), :])
                        link(v.tensor_scalar(pos_hi[b][:, :], pos[b][:, :], 7, None, ALU.logical_shift_right))
                        link(v.scalar_tensor_tensor(where[b][:, :], pos_lo[b][:, :], float(TILES), pos_hi[b][:, :], ALU.mult, ALU.add))
                        link.tell(where_ready[b])
                    link.restart()

            @block.gpsimd
            def _(pool):
                for b in range(2):
                    first_credit(nc, C, b, scattered[b])
                with nc.gpsimd.Fori(0, STEPS) as i:
                    for b in range(2):
                        pool_wait(pool, where_ready[b], i + 1, went_on)
                        for k in range(GT):
                            nc.gpsimd.indirect_dma_start(
                                out=table, out_offset=bass.IndirectOffsetOnAxis(ap=where[b][:, k:k + 1], axis=0),
                                in_=pairs[b][:, k, :], in_offset=None, bounds_check=NP - 1,
                                oob_is_err=False).then_inc(scattered[b], 16)
                for b in range(2):
                    pool.wait_ge(scattered[b], 64 * (STEPS + 1))


def reload_pairs(nc, A, table, name):
    with Phase(nc, name) as ph:
        loaded = ph.sem("loaded")
        with nc.Block() as block:
            @block.sync
            def _(sp):
                sp.dma_start(A[:, :, :], table.rearrange("(p t) c -> p t c", t=TILES)).then_inc(loaded, 16)
                sp.wait_ge(loaded, 16)


class Order:

    KEY, OTHER, CLAMPED, TARGET = range(4)

    def __init__(self, nc, ctx, name):
        self.name = name
        self.index = nc.dram_tensor(f"{name}_index", (P, GROUPS * 4 * GT), I32, kind="Internal").ap()
        self.same = nc.dram_tensor(f"{name}_same", (NP,), BF16, kind="Internal").ap()
        self.pad_bias = ctx.enter_context(nc.sbuf_tensor(f"{name}_pad_bias", [P, TILES], FP32))

    def index_of(self, g, slot, slots=1):
        at = self.index.rearrange("p (g s) -> p g s", s=4 * GT)
        return at[:, ds(g, 1), slot * GT:(slot + slots) * GT].rearrange("p o s -> p (o s)")


def describe_order(nc, C, A, table, order, limit):
    with Phase(nc, "order_" + order.name) as ph:
        later = ph.sb("later", [P, TILES, 2], I32)
        earlier = ph.sb("earlier", [P, TILES, 2], I32)
        key, nxt, prv = ph.sb("key", [P, TILES]), ph.sb("nxt", [P, TILES]), ph.sb("prv", [P, TILES])
        same, more = ph.sb("same", [P, TILES]), ph.sb("more", [P, TILES])
        packed = ph.sb("packed", [P, GROUPS, 4, GT], I32)
        rows = ph.sb("rows", [P, 4, P], BF16)
        tp = ph.ps("tp", [P, 4, P])
        loaded, cleared, same_ready, turned, rows_ready, packed_ready, stored, chain, chain_act = (ph.sem(x) for x in (
            "loaded", "cleared", "same_ready", "turned", "rows_ready", "packed_ready", "stored", "chain", "chain_act"))
        tail = TILES - 3 * P
        tv = table.rearrange("(p t) c -> p t c", t=TILES)
        same_tiles = order.same.rearrange("(t c) -> t c", c=P)
        with nc.Block() as block:
            @block.sync
            def _(sp):
                sp.dma_start(A[:, :, :], tv).then_inc(loaded, 16)
                sp.wait_ge(cleared, 1)
                sp.dma_start(later[0:P - 1, :, :], tv[1:P, :, :]).then_inc(loaded, 16)
                sp.dma_start(later[P - 1:P, 0:TILES - 1, :], tv[0:1, 1:TILES, :]).then_inc(loaded, 16)
                sp.dma_start(earlier[1:P, :, :], tv[0:P - 1, :, :]).then_inc(loaded, 16)
                sp.dma_start(earlier[0:1, 1:TILES, :], tv[P - 1:P, 0:TILES - 1, :]).then_inc(loaded, 16)
                sp.wait_ge(rows_ready, 1)
                sp.dma_start(same_tiles[0:3 * P, :].rearrange("(j p) c -> p j c", p=P), rows[:, 0:3, :]).then_inc(stored, 16)
                sp.dma_start(same_tiles[3 * P:TILES, :], rows[0:tail, 3, :]).then_inc(stored, 16)
                sp.wait_ge(packed_ready, 1)
                sp.dma_start(order.index, packed[:, :, :, :].rearrange("p g s k -> p (g s k)")).then_inc(stored, 16)
                sp.wait_ge(stored, 48)

            @block.vector
            def _(dve):
                v = nc.vector
                link = Chain(dve, chain)
                v.memset(later[:, :, :], -1)
                link(v.memset(earlier[:, :, :], -1))
                link.tell(cleared)
                dve.wait_ge(loaded, 80)
                v.tensor_copy(key[:, :], A[:, :, 0])
                v.tensor_copy(nxt[:, :], later[:, :, 0])
                link(v.tensor_copy(prv[:, :], earlier[:, :, 0]))
                link(v.tensor_tensor(same[:, :], key[:, :], prv[:, :], ALU.is_equal))
                link.tell(same_ready)
                link(v.tensor_tensor(more[:, :], key[:, :], nxt[:, :], ALU.is_equal))
                link(v.scalar_tensor_tensor(more[:, :], more[:, :], float(PAD_KEY), key[:, :], ALU.mult, ALU.max))
                grouped = [x.rearrange("p (g k) -> p g k", k=GT) for x in (key[:, :], more[:, :])]
                other = A[:, :, 1].rearrange("p (g k) -> p g k", k=GT)
                v.tensor_scalar(packed[:, :, Order.KEY, :], grouped[0], float(NP - 1), None, ALU.min)
                v.tensor_copy(packed[:, :, Order.OTHER, :], other)
                v.tensor_scalar(packed[:, :, Order.CLAMPED, :], other, float(limit - 1), None, ALU.min)
                v.tensor_scalar(order.pad_bias[:, :], key[:, :], float(N), -1e30, ALU.is_ge, ALU.mult)
                link(v.tensor_copy(packed[:, :, Order.TARGET, :], grouped[1]))
                link.tell(packed_ready)

            @block.tensor
            def _(pe):
                pe.wait_ge(same_ready, 1)
                for j in range(4):
                    w = P if j < 3 else tail
                    last = nc.tensor.transpose(tp[0:w, j, :], same[:, j * P:j * P + w], C.ident[:, :])
                last.then_inc(turned, 1)

            @block.scalar
            def _(act):
                link = Chain(act, chain_act)
                act.wait_ge(turned, 1)
                link(nc.scalar.copy(rows[:, 0:3, :], tp[:, 0:3, :]))
                nc.scalar.copy(rows[0:tail, 3, :], tp[0:tail, 3, :]).then_inc(rows_ready, 1)


def gather(nc, to, table, index, sem, rows):
    nc.gpsimd.indirect_dma_start(out=to, out_offset=None, in_=table,
                                 in_offset=bass.IndirectOffsetOnAxis(ap=index, axis=0),
                                 bounds_check=rows - 1, oob_is_err=False).then_inc(sem, 16)


def load_targets(act, order, i, b, target, target_in, scattered):
    act.wait_ge(scattered[b], i * 64 + 64)
    act.dma_start(target[b][:, :], order.index_of(i * 2 + b, Order.TARGET)).then_inc(target_in[b], 16)


def edge_loaders(nc, order, block, slot, slots, gather_index, same, gather_index_in, same_in, gathered, same_used, unit):
    @block.sync
    def _(sp):
        for b in range(2):
            sp.sem_inc(same_used[b], 1)
        with nc.sync.Fori(0, STEPS) as i:
            for b in range(2):
                g = i * 2 + b
                sp.wait_ge(gathered[b], i * unit + unit)
                sp.dma_start(gather_index[b][:, :], order.index_of(g, slot, slots)).then_inc(gather_index_in[b], 16)
                sp.wait_ge(same_used[b], i + 1)
                sp.dma_start(same[b][:, :], order.same[ds(g * ROWS, ROWS)]
                             .rearrange("(a n) -> a n", a=1).partition_broadcast(P)).then_inc(same_in[b], 16)


def edge_pool(nc, C, block, gathers, sums, rows_out, target, target_in, rows_ready, gathered, scattered,
              gather_index_in, gathers_free, went_on, unit):
    @block.gpsimd
    def _(pool):
        for b in range(2):
            nc.gpsimd.dma_start(C.credit[b:b + 1, :], C.eps[0:1, :]).then_inc(gathered[b], unit)
            nc.gpsimd.dma_start(C.credit[2 + b:3 + b, :], C.eps[0:1, :]).then_inc(scattered[b], 64)

        def take(i, b):
            pool_wait(pool, gather_index_in[b], i * 16 + 16, went_on)
            pool_wait(pool, gathers_free[b], i + 1, went_on)
            gathers(b)

        def put(i, b):
            pool_wait(pool, target_in[b], i * 16 + 16, went_on)
            pool_wait(pool, rows_ready[b], i + 1, went_on)
            for k in range(GT):
                nc.gpsimd.indirect_dma_start(
                    out=sums, out_offset=bass.IndirectOffsetOnAxis(ap=target[b][:, k:k + 1], axis=0),
                    in_=rows_out[b][:, k, :], in_offset=None, bounds_check=NP - 1,
                    oob_is_err=False).then_inc(scattered[b], 16)

        take(0, 0)
        take(0, 1)
        with nc.gpsimd.Fori(0, STEPS - 1) as i:
            take(i + 1, 0)
            put(i, 0)
            take(i + 1, 1)
            put(i, 1)
        put(STEPS - 1, 0)
        put(STEPS - 1, 1)
        for b in range(2):
            pool.wait_ge(scattered[b], 64 * (STEPS + 1))


def plain_pass(nc, C, name, order, table, width, slot, weight, sums):
    counts = width == P
    with Phase(nc, name) as ph:
        rows = ph.sb2("rows", [P, GT, width])
        gather_index, target = ph.sb2("gather_index", [P, GT], I32), ph.sb2("target", [P, GT], I32)
        same = ph.sb2("same", [P, ROWS], BF16)
        total, scalar_total = ph.sb2("total", [P, ROWS]), ph.sb2("scalar_total", [1, ROWS])
        out_rows = ph.sb2("out_rows", [P, GT, SW])
        turned_ps, product = ph.ps2("turned_ps", [P, ROWS]), ph.ps2("product", [P, GT, P])
        scalar_ps, scalar_back = ph.ps2("scalar_ps", [1, ROWS]), ph.ps2("scalar_back", [P, GT])
        names = ("gather_index_in", "target_in", "same_in", "gathered", "scattered", "same_used",
                 "turned", "scanned", "projected", "copied", "rows_ready")
        (gather_index_in, target_in, same_in, gathered, scattered, same_used,
         turned, scanned, projected, copied, rows_ready) = (ph.sems2(x) for x in names)
        went_on, chain, chain_act = ph.sem("went_on"), ph.sem("chain"), ph.sem("chain_act")
        unit = 64
        with nc.Block() as block:
            edge_loaders(nc, order, block, slot, 1, gather_index, same, gather_index_in, same_in, gathered,
                         same_used, unit)

            def gathers(b):
                for k in range(GT):
                    gather(nc, rows[b][:, k, :], table, gather_index[b][:, k:k + 1], gathered[b], table.shape[0])

            edge_pool(nc, C, block, gathers, sums, out_rows, target, target_in, rows_ready, gathered, scattered,
                      gather_index_in, turned, went_on, unit)

            @block.tensor
            def _(pe):
                for b in range(2):
                    pe.sem_inc(turned[b], 1)
                    pe.sem_inc(projected[b], 1)
                with nc.tensor.Fori(0, STEPS) as i:
                    for b in range(2):
                        pe.wait_ge(gathered[b], i * unit + 2 * unit)
                        pe.wait_ge(scanned[b], i + 1)
                        for k in range(GT):
                            if not counts:
                                nc.tensor.transpose(scalar_ps[b][:, k * P:(k + 1) * P], rows[b][:, k, P:P + 1], C.ident[:, :])
                            last = nc.tensor.transpose(turned_ps[b][:, k * P:(k + 1) * P], rows[b][:, k, 0:P], C.ident[:, :])
                        last.then_inc(turned[b], 1)
                        pe.wait_ge(scanned[b], i + 2)
                        pe.wait_ge(copied[b], i + 1)
                        for k in range(GT):
                            nc.tensor.matmul(product[b][:, k, :], total[b][:, k * P:(k + 1) * P], weight,
                                             start=True, stop=True)
                            last = nc.tensor.matmul(scalar_back[b][:, k:k + 1], scalar_total[b][:, k * P:(k + 1) * P],
                                                    C.ones[0:1, 0:1], start=True, stop=True)
                        last.then_inc(projected[b], 1)

            @block.vector
            def _(dve):
                v = nc.vector
                link = Chain(dve, chain)
                v.memset(total[1][:, ROWS - 1:ROWS], 0.0)
                link(v.memset(scalar_total[1][:, ROWS - 1:ROWS], 0.0))
                for b in range(2):
                    dve.sem_inc(scanned[b], 1)
                link.restart()
                with v.Fori(0, STEPS) as i:
                    for b in range(2):
                        dve.wait_ge(turned[b], i + 2)
                        dve.wait_ge(same_in[b], i * 16 + 16)
                        dve.wait_ge(projected[b], i + 1)
                        source = C.ones_row[0:1, :] if counts else scalar_ps[b][:, :]
                        v.tensor_tensor_scan(scalar_total[b][:, :], same[b][0:1, :], source,
                                             scalar_total[1 - b][:, ROWS - 1:ROWS], ALU.mult, ALU.add)
                        link(v.tensor_tensor_scan(total[b][:, :], same[b][:, :], turned_ps[b][:, :],
                                                  total[1 - b][:, ROWS - 1:ROWS], ALU.mult, ALU.add))
                        link.tell(scanned[b])
                        link.tell(same_used[b])
                    link.restart()

            @block.scalar
            def _(act):
                link = Chain(act, chain_act)
                for b in range(2):
                    act.sem_inc(copied[b], 1)
                for b in range(2):
                    last = nc.scalar.copy(out_rows[b][:, :, P:SW], C.zeros[:, 0:GT * (SW - P)].rearrange("p (k c) -> p k c", k=GT))
                link(last)
                for b in range(2):
                    last = nc.scalar.activation(out_rows[b][:, :, P + 1], C.row_number[:, :], ACT.Copy, bias=float((b - 2) * ROWS + 1))
                link(last)
                link.restart()
                with nc.scalar.Fori(0, STEPS) as i:
                    for b in range(2):
                        load_targets(act, order, i, b, target, target_in, scattered)
                        nc.scalar.activation(out_rows[b][:, :, P + 1], out_rows[b][:, :, P + 1], ACT.Copy, bias=float(2 * ROWS))
                        act.wait_ge(projected[b], i + 2)
                        nc.scalar.copy(out_rows[b][:, :, P], scalar_back[b][:, :])
                        link(nc.scalar.copy(out_rows[b][:, :, 0:P], product[b][:, :, :]))
                        link.tell(copied[b])
                        link.tell(rows_ready[b])
                    link.restart()


def running_pass(nc, C, name, order, table, slot, row_sums):
    with Phase(nc, name) as ph:
        rows = ph.sb2("rows", [P, GT, P])
        gather_index = ph.sb2("gather_index", [P, GT], I32)
        same, total = ph.sb2("same", [P, ROWS], BF16), ph.sb2("total", [P, ROWS])
        out_rows = ph.sb2("out_rows", [P, GT, P])
        turned_ps, back_ps = ph.ps2("turned_ps", [P, ROWS]), ph.ps2("back_ps", [P, GT, P])
        (gather_index_in, same_in, gathered, same_used, turned, scanned, turned_back, copied, stored) = (
            ph.sems2(x) for x in ("gather_index_in", "same_in", "gathered", "same_used", "turned", "scanned",
                                  "turned_back", "copied", "stored"))
        went_on, chain, chain_act = ph.sem("went_on"), ph.sem("chain"), ph.sem("chain_act")
        unit = 16 * GT
        with nc.Block() as block:
            edge_loaders(nc, order, block, slot, 1, gather_index, same, gather_index_in, same_in, gathered,
                         same_used, unit)

            @block.gpsimd
            def _(pool):
                for b in range(2):
                    nc.gpsimd.dma_start(C.credit[b:b + 1, :], C.eps[0:1, :]).then_inc(gathered[b], unit)
                with nc.gpsimd.Fori(0, STEPS) as i:
                    for b in range(2):
                        pool_wait(pool, gather_index_in[b], i * 16 + 16, went_on)
                        pool_wait(pool, turned[b], i + 1, went_on)
                        for k in range(GT):
                            gather(nc, rows[b][:, k, :], table, gather_index[b][:, k:k + 1], gathered[b], table.shape[0])

            @block.tensor
            def _(pe):
                def turn_back(i, b):
                    pe.wait_ge(scanned[b], i + 2)
                    pe.wait_ge(copied[b], i + 1)
                    for k in range(GT):
                        last = nc.tensor.transpose(back_ps[b][:, k, :], total[b][:, k * P:(k + 1) * P], C.ident[:, :])
                    last.then_inc(turned_back[b], 1)

                for b in range(2):
                    pe.sem_inc(turned[b], 1)
                    pe.sem_inc(turned_back[b], 1)
                with nc.tensor.Fori(0, STEPS) as i:
                    for b in range(2):
                        pe.wait_ge(gathered[b], i * unit + 2 * unit)
                        pe.wait_ge(scanned[b], i + 1)
                        for k in range(GT):
                            last = nc.tensor.transpose(turned_ps[b][:, k * P:(k + 1) * P], rows[b][:, k, :], C.ident[:, :])
                        last.then_inc(turned[b], 1)
                        turn_back(i, b)

            @block.vector
            def _(dve):
                link = Chain(dve, chain)
                link(nc.vector.memset(total[1][:, ROWS - 1:ROWS], 0.0))
                for b in range(2):
                    dve.sem_inc(scanned[b], 1)
                link.restart()
                with nc.vector.Fori(0, STEPS) as i:
                    for b in range(2):
                        dve.wait_ge(turned[b], i + 2)
                        dve.wait_ge(same_in[b], i * 16 + 16)
                        dve.wait_ge(turned_back[b], i + 1)
                        link(nc.vector.tensor_tensor_scan(total[b][:, :], same[b][:, :], turned_ps[b][:, :],
                                                          total[1 - b][:, ROWS - 1:ROWS], ALU.mult, ALU.add))
                        link.tell(scanned[b])
                        link.tell(same_used[b])
                    link.restart()

            @block.scalar
            def _(act):
                link = Chain(act, chain_act)
                for b in range(2):
                    act.sem_inc(copied[b], 1)
                    act.sem_inc(stored[b], 16)
                with nc.scalar.Fori(0, STEPS) as i:
                    for b in range(2):
                        act.wait_ge(stored[b], i * 16 + 16)
                        act.wait_ge(turned_back[b], i + 2)
                        link(nc.scalar.copy(out_rows[b][:, :, :], back_ps[b][:, :, :]))
                        link.tell(copied[b])
                        act.dma_start(group_rows(row_sums, i * 2 + b), out_rows[b][:, :, :]).then_inc(stored[b], 16)
                    link.restart()
                for b in range(2):
                    act.wait_ge(stored[b], 16 * (STEPS + 1))


def attention_pass(nc, C, order, table, scores, sums):
    scale = float((P * HEADS) ** -0.5)
    with Phase(nc, "gat") as ph:
        rows, mine = ph.sb2("rows", [P, GT, P + HEADS]), ph.sb2("mine", [P, GT, HEADS])
        gather_index, target = ph.sb2("gather_index", [P, 2 * GT], I32), ph.sb2("target", [P, GT], I32)
        same = ph.sb2("same", [P, ROWS], BF16)
        e, ee, t1 = ph.sb2("e", [P, GT, HEADS]), ph.sb2("ee", [P, GT, HEADS]), ph.sb("t1", [P, GT, HEADS])
        weighted = ph.sb2("weighted", [P, HEADS, GT, P])
        total, scalar_total = ph.sb2("total", [P, HEADS, ROWS]), ph.sb2("scalar_total", [HEADS, ROWS])
        out_rows = ph.sb2("out_rows", [P, GT, SW])
        wsum, winv = ph.sb("wsum", [P, GT, HEADS]), ph.sb("winv", [P, GT, HEADS])
        turned_ps = [ph.ps(f"turned_ps{h}", [P, ROWS]) for h in range(HEADS)]
        product = ph.ps2("product", [P, HEADS, P])
        scalar_ps, scalar_back = ph.ps("scalar_ps", [HEADS, ROWS]), ph.ps("scalar_back", [P, GT, HEADS])
        names = ("gather_index_in", "target_in", "same_in", "gathered", "scattered", "same_used", "scores_ready",
                 "weighted_ready", "turned", "scanned", "product_ready", "product_used", "rows_ready")
        (gather_index_in, target_in, same_in, gathered, scattered, same_used, scores_ready,
         weighted_ready, turned, scanned, product_ready, product_used, rows_ready) = (ph.sems2(x) for x in names)
        sums_back, sums_used = ph.sem("sums_back"), ph.sem("sums_used")
        went_on, chain, chain_act = ph.sem("went_on"), ph.sem("chain"), ph.sem("chain_act")
        unit = 128
        with nc.Block() as block:
            edge_loaders(nc, order, block, Order.KEY, 2, gather_index, same, gather_index_in, same_in, gathered,
                         same_used, unit)

            def gathers(b):
                for k in range(GT):
                    gather(nc, rows[b][:, k, :], table, gather_index[b][:, GT + k:GT + k + 1], gathered[b], NP)
                    gather(nc, mine[b][:, k, :], scores, gather_index[b][:, k:k + 1], gathered[b], NP)

            edge_pool(nc, C, block, gathers, sums, out_rows, target, target_in, rows_ready, gathered, scattered,
                      gather_index_in, weighted_ready, went_on, unit)

            @block.scalar
            def _(act):
                link = Chain(act, chain_act)
                for b in range(2):
                    act.sem_inc(weighted_ready[b], 1)
                with nc.scalar.Fori(0, STEPS) as i:
                    for b in range(2):
                        act.wait_ge(scores_ready[b], i + 1)
                        act.wait_ge(turned[b], i + 1)
                        link(nc.scalar.activation(ee[b][:, :, :], e[b][:, :, :], ACT.Exp, scale=scale))
                        for h in range(HEADS):
                            for k in range(GT):
                                last = nc.scalar.activation(weighted[b][:, h, k, :], rows[b][:, k, 0:P], ACT.Copy,
                                                            scale=ee[b][:, k, h:h + 1])
                        link(last)
                        link.tell(weighted_ready[b])
                        load_targets(act, order, i, b, target, target_in, scattered)
                    link.restart()

            @block.tensor
            def _(pe):
                for b in range(2):
                    pe.sem_inc(turned[b], 1)
                pe.sem_inc(sums_back, 1)
                with nc.tensor.Fori(0, STEPS) as i:
                    for b in range(2):
                        pe.wait_ge(weighted_ready[b], i + 2)
                        pe.wait_ge(scanned[1 - b], i + 1 + b)
                        for k in range(GT):
                            nc.tensor.transpose(scalar_ps[:, k * P:(k + 1) * P], ee[b][:, k, :], C.ident[:, :])
                            for h in range(HEADS):
                                last = nc.tensor.transpose(turned_ps[h][:, k * P:(k + 1) * P], weighted[b][:, h, k, :], C.ident[:, :])
                        last.then_inc(turned[b], 1)
                        pe.wait_ge(scanned[b], i + 1 + 1)
                        pe.wait_ge(sums_used, i * 2 + b + 1)
                        for k in range(GT):
                            last = nc.tensor.matmul(scalar_back[:, k, :], scalar_total[b][:, k * P:(k + 1) * P],
                                                    C.ident[0:HEADS, 0:HEADS], start=True, stop=True)
                        last.then_inc(sums_back, 1)
                        for k in range(GT):
                            pe.wait_ge(product_used[k % 2], i * 4 + b * 2 + k // 2 + 1)
                            for h in range(HEADS):
                                last = nc.tensor.matmul(product[k % 2][:, h, :], total[b][:, h, k * P:(k + 1) * P],
                                                        C.heads[:, h, :], start=True, stop=True)
                            last.then_inc(product_ready[k % 2], 1)

            @block.vector
            def _(dve):
                v = nc.vector
                link = Chain(dve, chain)
                v.memset(total[1][:, :, ROWS - 1:ROWS], 0.0)
                link(v.memset(scalar_total[1][:, ROWS - 1:ROWS], 0.0))
                link.restart()
                for b in range(2):
                    dve.sem_inc(scanned[b], 1)
                    dve.sem_inc(product_used[b], 1)
                dve.sem_inc(sums_used, 1)

                def score(i, b):
                    dve.wait_ge(gathered[b], i * unit + 2 * unit)
                    dve.wait_ge(weighted_ready[b], i + 1)
                    link(v.tensor_add(t1[:, :, :], rows[b][:, :, P:P + HEADS], mine[b][:, :, :]))
                    link(v.scalar_tensor_tensor(e[b][:, :, :], t1[:, :, :], 0.2, t1[:, :, :], ALU.mult, ALU.max))
                    link.tell(scores_ready[b])

                def scan(i, b):
                    dve.wait_ge(turned[b], i + 2)
                    dve.wait_ge(same_in[b], i * 16 + 16)
                    v.tensor_tensor_scan(scalar_total[b][:, :], same[b][0:HEADS, :], scalar_ps[:, :],
                                         scalar_total[1 - b][:, ROWS - 1:ROWS], ALU.mult, ALU.add)
                    for h in range(HEADS):
                        last = v.tensor_tensor_scan(total[b][:, h, :], same[b][:, :], turned_ps[h][:, :],
                                                    total[1 - b][:, h, ROWS - 1:ROWS], ALU.mult, ALU.add)
                    link(last)
                    link.tell(scanned[b])
                    link.tell(same_used[b])

                def combine(i, b):
                    dve.wait_ge(sums_back, i * 2 + b + 2)
                    link(v.tensor_scalar(wsum[:, :, :], scalar_back[:, :, :], float(HEADS), None, ALU.mult))
                    link.tell(sums_used)
                    link(v.scalar_tensor_tensor(winv[:, :, :], wsum[:, :, :], 0.0, wsum[:, :, :], ALU.is_equal, ALU.add))
                    link(v.reciprocal(winv[:, :, :], winv[:, :, :]))
                    dve.wait_ge(scattered[b], i * 64 + 64)
                    v.tensor_scalar(out_rows[b][:, :, P:P + HEADS], wsum[:, :, :], 0.0, None, ALU.is_gt)
                    for k in range(GT):
                        dve.wait_ge(product_ready[k % 2], i * 4 + b * 2 + k // 2 + 1)
                        o = out_rows[b][:, k, 0:P]
                        link(v.tensor_scalar(o, product[k % 2][:, 0, :], winv[:, k, 0:1], None, ALU.mult))
                        for h in range(1, HEADS):
                            link(v.scalar_tensor_tensor(o, product[k % 2][:, h, :], winv[:, k, h:h + 1], o, ALU.mult, ALU.add))
                        link.tell(product_used[k % 2])
                    link.tell(rows_ready[b])

                score(0, 0)
                link.restart()
                with v.Fori(0, STEPS - 1) as i:
                    scan(i, 0)
                    score(i, 1)
                    combine(i, 0)
                    scan(i, 1)
                    score(i + 1, 0)
                    combine(i, 1)
                    link.restart()
                scan(STEPS - 1, 0)
                score(STEPS - 1, 1)
                combine(STEPS - 1, 0)
                scan(STEPS - 1, 1)
                combine(STEPS - 1, 1)


def context_pass(nc, C, block_no, order, ctx_table, agents, sums, last_max):
    with Phase(nc, f"ctx{block_no}") as ph:
        rows, mine = ph.sb2("rows", [P, GT, 2 * P]), ph.sb2("mine", [P, GT, P])
        gather_index, target = ph.sb2("gather_index", [P, 3 * GT], I32), ph.sb2("target", [P, GT], I32)
        same = ph.sb2("same", [P, ROWS], BF16)
        prod = ph.sb("prod", [P, GT, P])
        c, ee = ph.sb2("c", [P, GT]), ph.sb2("ee", [P, GT])
        part_max, all_max, running = ph.sb("part_max", [P, 1]), ph.sb("all_max", [1, 1]), ph.sb("running", [1, 1])
        shift, neg_shift, fade = ph.sb2("shift", [P, 1]), ph.sb2("neg_shift", [P, 1]), ph.sb2("fade", [P, 1])
        begin, scalar_begin = ph.sb("begin", [P, 1]), ph.sb("scalar_begin", [1, 1])
        weighted = ph.sb2("weighted", [P, GT, P])
        total, scalar_total = ph.sb2("total", [P, ROWS]), ph.sb2("scalar_total", [1, ROWS])
        out_rows = ph.sb2("out_rows", [P, GT, SW])
        turned_ps, product = ph.ps2("turned_ps", [P, ROWS]), ph.ps2("product", [P, GT, P])
        scalar_ps, scalar_back = ph.ps("scalar_ps", [1, ROWS]), ph.ps("scalar_back", [P, GT])
        max_row, max_wide = ph.ps("max_row", [1, P]), ph.ps("max_wide", [P, 1])
        names = ("gather_index_in", "target_in", "same_in", "gathered", "scattered", "same_used", "shift_ready",
                 "weighted_ready", "turned", "scanned", "projected", "copied", "rows_ready")
        (gather_index_in, target_in, same_in, gathered, scattered, same_used, shift_ready,
         weighted_ready, turned, scanned, projected, copied, rows_ready) = (ph.sems2(x) for x in names)
        parts_ready, row_ready, max_ready, wide_ready = (ph.sem(x) for x in ("parts_ready", "row_ready", "max_ready", "wide_ready"))
        went_on, chain, chain_act = ph.sem("went_on"), ph.sem("chain"), ph.sem("chain_act")
        unit = 128
        with nc.Block() as block:
            edge_loaders(nc, order, block, Order.KEY, 3, gather_index, same, gather_index_in, same_in, gathered,
                         same_used, unit)

            def gathers(b):
                for k in range(GT):
                    gather(nc, rows[b][:, k, :], ctx_table, gather_index[b][:, 2 * GT + k:2 * GT + k + 1], gathered[b], CTX)
                    gather(nc, mine[b][:, k, :], agents, gather_index[b][:, k:k + 1], gathered[b], NP)

            edge_pool(nc, C, block, gathers, sums, out_rows, target, target_in, rows_ready, gathered, scattered,
                      gather_index_in, weighted_ready, went_on, unit)

            @block.vector
            def _(dve):
                v = nc.vector
                link = Chain(dve, chain)
                v.memset(total[1][:, ROWS - 1:ROWS], 0.0)
                v.memset(scalar_total[1][:, ROWS - 1:ROWS], 0.0)
                v.memset(running[:, :], -1e30)
                link(v.memset(shift[1][:, :], -1e30))
                link.restart()
                for b in range(2):
                    dve.sem_inc(scanned[b], 1)

                def score(i, b):
                    g = i * 2 + b
                    dve.wait_ge(gathered[b], i * unit + 2 * unit)
                    dve.wait_ge(copied[b], i + 1)
                    link(v.tensor_mul(prod[:, :, :], rows[b][:, :, 0:P], mine[b][:, :, :]))
                    link(v.tensor_reduce(c[b][:, :], prod[:, :, :], AX.X, ALU.add))
                    link(v.scalar_tensor_tensor(c[b][:, :], c[b][:, :], 0.1, c[b][:, :], ALU.mult, ALU.max))
                    link(v.tensor_add(c[b][:, :], c[b][:, :], order.pad_bias[:, ds(g * GT, GT)]))
                    link(v.tensor_reduce(part_max[:, :], c[b][:, :], AX.X, ALU.max))
                    link.tell(parts_ready)
                    dve.wait_ge(row_ready, g + 1)
                    link(v.tensor_reduce(all_max[:, :], max_row[:, :], AX.X, ALU.max))
                    link(v.tensor_tensor(running[:, :], running[:, :], all_max[:, :], ALU.max))
                    link.tell(max_ready)
                    dve.wait_ge(wide_ready, g + 1)
                    link(v.tensor_copy(shift[b][:, :], max_wide[:, :]))
                    link(v.tensor_scalar(neg_shift[b][:, :], shift[b][:, :], -1.0, None, ALU.mult))
                    link.tell(shift_ready[b])

                def scan(i, b):
                    dve.wait_ge(turned[b], i + 2)
                    dve.wait_ge(same_in[b], i * 16 + 16)
                    dve.wait_ge(projected[b], i + 1)
                    v.tensor_tensor(scalar_begin[:, :], scalar_total[1 - b][:, ROWS - 1:ROWS], fade[b][0:1, :], ALU.mult)
                    link(v.tensor_tensor(begin[:, :], total[1 - b][:, ROWS - 1:ROWS], fade[b][:, :], ALU.mult))
                    v.tensor_tensor_scan(scalar_total[b][:, :], same[b][0:1, :], scalar_ps[:, :], scalar_begin[:, :],
                                         ALU.mult, ALU.add)
                    link(v.tensor_tensor_scan(total[b][:, :], same[b][:, :], turned_ps[b][:, :], begin[:, :],
                                              ALU.mult, ALU.add))
                    link.tell(scanned[b])
                    link.tell(same_used[b])

                score(0, 0)
                link.restart()
                with v.Fori(0, STEPS - 1) as i:
                    scan(i, 0)
                    score(i, 1)
                    scan(i, 1)
                    score(i + 1, 0)
                    link.restart()
                scan(STEPS - 1, 0)
                score(STEPS - 1, 1)
                scan(STEPS - 1, 1)
                link(v.tensor_copy(last_max[:, :], shift[1][:, :]))

            @block.scalar
            def _(act):
                link = Chain(act, chain_act)
                for b in range(2):
                    act.sem_inc(weighted_ready[b], 1)
                    act.sem_inc(copied[b], 1)
                for b in range(2):
                    last = nc.scalar.copy(out_rows[b][:, :, P:SW], C.zeros[:, 0:GT * (SW - P)].rearrange("p (k c) -> p k c", k=GT))
                link(last)
                link.restart()

                def weigh(i, b):
                    act.wait_ge(shift_ready[b], i + 1)
                    act.wait_ge(turned[b], i + 1)
                    act.wait_ge(scanned[b], i + 1)
                    nc.scalar.activation(fade[b][:, :], shift[1 - b][:, :], ACT.Exp, bias=neg_shift[b][:, :])
                    link(nc.scalar.activation(ee[b][:, :], c[b][:, :], ACT.Exp, bias=neg_shift[b][:, :]))
                    for k in range(GT):
                        last = nc.scalar.activation(weighted[b][:, k, :], rows[b][:, k, P:2 * P], ACT.Copy,
                                                    scale=ee[b][:, k:k + 1])
                    link(last)
                    link.tell(weighted_ready[b])

                def copy_out(i, b):
                    load_targets(act, order, i, b, target, target_in, scattered)
                    act.wait_ge(projected[b], i + 2)
                    nc.scalar.activation(out_rows[b][:, :, P + 1], C.zeros[:, 0:GT], ACT.Identity, bias=shift[b][:, :])
                    nc.scalar.copy(out_rows[b][:, :, P], scalar_back[:, :])
                    link(nc.scalar.copy(out_rows[b][:, :, 0:P], product[b][:, :, :]))
                    link.tell(copied[b])
                    link.tell(rows_ready[b])

                weigh(0, 0)
                link.restart()
                with nc.scalar.Fori(0, STEPS - 1) as i:
                    copy_out(i, 0)
                    weigh(i, 1)
                    copy_out(i, 1)
                    weigh(i + 1, 0)
                    link.restart()
                copy_out(STEPS - 1, 0)
                weigh(STEPS - 1, 1)
                copy_out(STEPS - 1, 1)

            @block.tensor
            def _(pe):
                for b in range(2):
                    pe.sem_inc(turned[b], 1)
                    pe.sem_inc(projected[b], 1)

                def maxima(i, b):
                    g = i * 2 + b
                    pe.wait_ge(parts_ready, g + 1)
                    nc.tensor.transpose(max_row[:, :], part_max[:, :], C.ident[:, :]).then_inc(row_ready, 1)
                    pe.wait_ge(max_ready, g + 1)
                    nc.tensor.matmul(max_wide[:, :], C.ones[0:1, :], running[:, :], start=True, stop=True).then_inc(wide_ready, 1)

                def turn(i, b):
                    pe.wait_ge(weighted_ready[b], i + 2)
                    pe.wait_ge(scanned[b], i + 1)
                    pe.wait_ge(scanned[1 - b], i + 1 + b)
                    for k in range(GT):
                        nc.tensor.transpose(scalar_ps[:, k * P:(k + 1) * P], ee[b][:, k:k + 1], C.ident[:, :])
                        last = nc.tensor.transpose(turned_ps[b][:, k * P:(k + 1) * P], weighted[b][:, k, :], C.ident[:, :])
                    last.then_inc(turned[b], 1)

                def project(i, b):
                    pe.wait_ge(scanned[b], i + 2)
                    pe.wait_ge(copied[b], i + 1)
                    pe.wait_ge(copied[1 - b], i + 1 + b)
                    for k in range(GT):
                        nc.tensor.matmul(product[b][:, k, :], total[b][:, k * P:(k + 1) * P], C.t[f"Wb{block_no}"][:, :],
                                         start=True, stop=True)
                        last = nc.tensor.matmul(scalar_back[:, k:k + 1], scalar_total[b][:, k * P:(k + 1) * P],
                                                C.ones[0:1, 0:1], start=True, stop=True)
                    last.then_inc(projected[b], 1)

                maxima(0, 0)
                with nc.tensor.Fori(0, STEPS - 1) as i:
                    turn(i, 0)
                    project(i, 0)
                    maxima(i, 1)
                    turn(i, 1)
                    project(i, 1)
                    maxima(i + 1, 0)
                turn(STEPS - 1, 0)
                project(STEPS - 1, 0)
                maxima(STEPS - 1, 1)
                turn(STEPS - 1, 1)
                project(STEPS - 1, 1)


def spread(vec):
    return vec[:, :].rearrange("p (o d) -> p o d", o=1).to_broadcast([P, GT, P])


class NodePhase(Phase):

    def __init__(self, nc, C, name, loads, stores):
        super().__init__(nc, name)
        self.C, self.loads, self.stores = C, loads, stores
        self.loaded, self.used, self.done, self.stored = self.ways_sem("loaded", "used", "done", "stored")
        self.chain, self.chain_act, self.chain_pool = self.sem("chain"), self.sem("chain_act"), self.sem("chain_pool")
        self.went_on = self.sem("went_on")

    def mover(self, block, load, store, peel_load=False, peel_store=False, late=None):
        nc = self.nc
        if late:
            self.late_loaded, = self.ways_sem("late_loaded")

        @block.sync
        def _(sp):
            def loads(i, b, last=False):
                pairs = load(i, b, last)
                for to, of in pairs:
                    sp.dma_start(to, of).then_inc(self.loaded[b], 16)
                if len(pairs) < self.loads:
                    sp.sem_inc(self.loaded[b], 16 * (self.loads - len(pairs)))

            def stores(i, b, last=False):
                for to, of in store(i, b, last):
                    sp.dma_start(to, of).then_inc(self.stored[b], 16)

            def late_loads(i, b):
                for to, of in late(i, b) if late else ():
                    sp.dma_start(to, of).then_inc(self.late_loaded[b], 16)

            def step(i, last_load=False):
                for b in range(WAYS):
                    sp.wait_ge(self.used[b], i + 1)
                    loads(i + 1, b, last_load)
                for b in range(WAYS):
                    sp.wait_ge(self.done[b], i + 1)
                    stores(i, b)
                    late_loads(i + 1, b)

            for b in range(WAYS):
                sp.sem_inc(self.stored[b], 16 * self.stores)
                loads(0, b)
                late_loads(0, b)
            with nc.sync.Fori(0, NODE_STEPS - 2) as i:
                step(i)
            step(NODE_STEPS - 2, peel_load)
            skipped = [0] * WAYS
            for b in range(WAYS):
                sp.wait_ge(self.done[b], NODE_STEPS)
                pairs = store(NODE_STEPS - 1, b, peel_store)
                skipped[b] = self.stores - len(pairs)
                for to, of in pairs:
                    sp.dma_start(to, of).then_inc(self.stored[b], 16)
            for b in range(WAYS):
                sp.wait_ge(self.stored[b], 16 * (self.stores * (NODE_STEPS + 1) - skipped[b]))

    def before_load(self, i):
        return i * 16 * self.loads + 16 * self.loads

    def before_store(self, i):
        return i * 16 * self.stores + 16 * self.stores


class Norm:

    def __init__(self, nc, C, ph, per_step):
        self.nc, self.C, self.per_step = nc, C, per_step
        self.stats, = ph.ways_sb([P, GT, 6], "stats")
        self.mean_var, = ph.ways_sb([P, GT, 2], "mean_var")
        self.squares, self.root, self.inv, self.bias = ph.ways_sb([P, GT], "squares", "root", "inv", "bias")
        self.junk = ph.sb("junk", [P, GT, P])
        self.var_ready, self.root_ready = ph.ways_sem("var_ready", "root_ready")

    def stats_dve(self, link, b, x):
        v = self.nc.vector
        for k in range(GT):
            last = v.bn_stats(self.stats[b][:, k, :], x[:, k, :])
        link(last)
        for k in range(GT):
            last = v.bn_aggr(self.mean_var[b][:, k, :], self.stats[b][:, k, :])
        link(last)
        link.tell(self.var_ready[b])

    def root_act(self, act, i, b):
        act.wait_ge(self.var_ready[b], i + 1)
        self.nc.scalar.activation(self.root[b][:, :], self.mean_var[b][:, :, 1], ACT.Sqrt,
                                  bias=self.C.eps[:, :]).then_inc(self.root_ready[b], 1)

    def squares_act(self, link, b, x, divisor, eps=True):
        s = self.nc.scalar
        for k in range(GT):
            last = s.activation(self.junk[:, k, :], x[:, k, :], ACT.Square, accum_out=self.squares[b][:, k:k + 1])
        link(last)
        kw = {"bias": self.C.eps[:, :]} if eps else {}
        link(s.activation(self.root[b][:, :], self.squares[b][:, :], ACT.Sqrt, scale=1.0 / divisor, **kw))
        link.tell(self.root_ready[b])

    def inverse_dve(self, dve, link, i, b, n, add=0.0, bias=False):
        v = self.nc.vector
        dve.wait_ge(self.root_ready[b], i * self.per_step + n + 1)
        if add:
            link(v.tensor_scalar(self.root[b][:, :], self.root[b][:, :], add, None, ALU.add))
        link(v.reciprocal(self.inv[b][:, :], self.root[b][:, :]))
        if bias:
            link(v.scalar_tensor_tensor(self.bias[b][:, :], self.mean_var[b][:, :, 0], -1.0, self.inv[b][:, :],
                                        ALU.mult, ALU.mult))

    def apply_act(self, b, x, y, func):
        for k in range(GT):
            last = self.nc.scalar.activation(y[:, k, :], x[:, k, :], func, scale=self.inv[b][:, k:k + 1],
                                             bias=self.bias[b][:, k:k + 1])
        return last


def scale_rows(v, link, out, x, scalars, other, op=ALU.add):
    for k in range(GT):
        last = v.scalar_tensor_tensor(out[:, k, :], x(k), scalars[:, k:k + 1], other(k), ALU.mult, op)
    link(last)


def input_rows(x, buf, i, b, last):
    if not last or b == 0:
        v = x[0:LASTG * ROWS, :].rearrange("(g p k) d -> p g k d", p=P, k=GT)
        return ((buf[:, :, :], v[:, ds(i * WAYS + b, 1), :, :].rearrange("p o k d -> p (o k) d")),)
    if b == 1:
        return ((buf[0:LASTP, :, :], x[LASTG * ROWS:N, :].rearrange("(p k) d -> p k d", k=GT)),)
    return ()


def norm_input(nc, C, x, h_out):
    with NodePhase(nc, C, "n0", 1, 1) as ph:
        X, H = ph.ways_sb([P, GT, P], "X", "H")
        norm = Norm(nc, C, ph, 1)
        ready, = ph.ways_sem("ready")
        with nc.Block() as block:
            ph.mover(block, lambda i, b, last: input_rows(x, X[b], i, b, last),
                     lambda i, b, last: ((group_rows(h_out, i * WAYS + b), H[b][:, :, :]),), peel_load=True)

            @block.vector
            def _(dve):
                link = Chain(dve, ph.chain)
                with nc.vector.Fori(0, NODE_STEPS) as i:
                    for b in range(WAYS):
                        dve.wait_ge(ph.loaded[b], ph.before_load(i))
                        norm.stats_dve(link, b, X[b])
                        if b >= 1:
                            norm.inverse_dve(dve, link, i, b - 1, 0, bias=True)
                            link.tell(ready[b - 1])
                    norm.inverse_dve(dve, link, i, WAYS - 1, 0, bias=True)
                    link.tell(ready[WAYS - 1])
                    link.restart()

            @block.scalar
            def _(act):
                link = Chain(act, ph.chain_act)
                with nc.scalar.Fori(0, NODE_STEPS) as i:
                    for b in range(WAYS + 1):
                        if b < WAYS:
                            norm.root_act(act, i, b)
                        if b >= 1:
                            act.wait_ge(ready[b - 1], i + 1)
                            act.wait_ge(ph.stored[b - 1], ph.before_store(i))
                            link(norm.apply_act(b - 1, X[b - 1], H[b - 1], ACT.Relu))
                            link.tell(ph.used[b - 1])
                            link.tell(ph.done[b - 1])
                    link.restart()


def sage_nodes(nc, C, x, h, sums, x_out, h_out):
    with NodePhase(nc, C, "n1", 3, 2) as ph:
        X, X1, H, HT, H1 = ph.ways_sb([P, GT, P], "X", "X1", "H", "HT", "H1")
        S, = ph.ways_sb([P, GT, SW], "S")
        inv, own = ph.sb("count_inv", [P, WAYS, GT]), ph.sb("own", [P, WAYS, GT])
        tp, po = ph.ps2("tp", [P, GT, P]), ph.ps2("po", [P, GT, 2, P])
        norm = Norm(nc, C, ph, 1)
        turned, moved, product, added, biased, ready = ph.ways_sem("turned", "moved", "product", "added", "biased", "ready")
        with nc.Block() as block:
            ph.mover(block, lambda i, b, last: input_rows(x, X[b], i, b, last) + (
                (S[b][:, :, :], group_rows(sums, i * WAYS + b)), (H[b][:, :, :], group_rows(h, i * WAYS + b))),
                lambda i, b, last: ((group_rows(x_out, i * WAYS + b), X1[b][:, :, :]),
                                    (group_rows(h_out, i * WAYS + b), H1[b][:, :, :])), peel_load=True)

            @block.gpsimd
            def _(pool):
                link = Chain(pool, ph.chain_pool)
                with nc.gpsimd.Fori(0, NODE_STEPS) as i:
                    for b in range(WAYS):
                        pool_wait(pool, ph.loaded[b], ph.before_load(i), ph.went_on)
                        link(nc.gpsimd.tensor_add(X[b][:, :, :], X[b][:, :, :], spread(C.v["bl"])))
                        link.tell(biased[b])
                    link.restart()

            @block.tensor
            def _(pe):
                for b in range(WAYS):
                    pe.sem_inc(added[b], 1)
                with nc.tensor.Fori(0, NODE_STEPS) as i:
                    for b in range(WAYS):
                        pe.wait_ge(ph.loaded[b], ph.before_load(i))
                        if b >= 2:
                            pe.wait_ge(moved[b - 2], i + 1)
                        for k in range(GT):
                            last = nc.tensor.transpose(tp[b % 2][:, k, :], H[b][:, k, :], C.ident[:, :])
                        last.then_inc(turned[b], 1)
                    for b in range(WAYS):
                        pe.wait_ge(moved[b], i + 1)
                        pe.wait_ge(added[(b + 2) % WAYS], i + 1 + (b >= 2))
                        for k in range(GT):
                            last = nc.tensor.matmul(po[b % 2][:, k, :, :].rearrange("p a d -> p (a d)"), HT[b][:, k, :],
                                                    C.wlr[:, :, :].rearrange("p a d -> p (a d)"), start=True, stop=True)
                        last.then_inc(product[b], 1)

            @block.vector
            def _(dve):
                v = nc.vector
                link = Chain(dve, ph.chain)
                with v.Fori(0, NODE_STEPS) as i:
                    for b in range(WAYS):
                        dve.wait_ge(ph.loaded[b], ph.before_load(i))
                        v.tensor_scalar(own[:, b, :], S[b][:, :, P], 0.0, -1.0, ALU.is_gt, ALU.mult)
                        last = v.tensor_scalar(inv[:, b, :], S[b][:, :, P], 1.0, None, ALU.max)
                    link(last)
                    link(v.reciprocal(inv[:, :, :], inv[:, :, :]))
                    for b in range(WAYS):
                        dve.wait_ge(ph.stored[b], ph.before_store(i))
                        dve.wait_ge(biased[b], i + 1)
                        scale_rows(v, link, X1[b], lambda k: S[b][:, k, 0:P], inv[:, b, :], lambda k: X[b][:, k, :])
                    for b in range(WAYS):
                        dve.wait_ge(product[b], i + 1)
                        link.tell(ph.used[b])
                        scale_rows(v, link, X1[b], lambda k: po[b % 2][:, k, 0, :], own[:, b, :], lambda k: X1[b][:, k, :])
                        link(v.tensor_add(X1[b][:, :, :], X1[b][:, :, :], po[b % 2][:, :, 1, :]))
                        link.tell(added[b])
                        norm.stats_dve(link, b, X1[b])
                        if b >= 1:
                            norm.inverse_dve(dve, link, i, b - 1, 0, bias=True)
                            link.tell(ready[b - 1])
                    norm.inverse_dve(dve, link, i, WAYS - 1, 0, bias=True)
                    link.tell(ready[WAYS - 1])
                    link.restart()

            @block.scalar
            def _(act):
                link = Chain(act, ph.chain_act)
                with nc.scalar.Fori(0, NODE_STEPS) as i:
                    for b in range(WAYS):
                        act.wait_ge(turned[b], i + 1)
                        link(nc.scalar.copy(HT[b][:, :, :], tp[b % 2][:, :, :]))
                        link.tell(moved[b])
                    for b in range(WAYS + 1):
                        if b < WAYS:
                            norm.root_act(act, i, b)
                        if b >= 1:
                            act.wait_ge(ready[b - 1], i + 1)
                            link(norm.apply_act(b - 1, X1[b - 1], H1[b - 1], ACT.Relu))
                            link.tell(ph.done[b - 1])
                    link.restart()


def hyper_rows(nc, C, name, sums, row_sums, e_out, affine):
    steps = HGROUPS // 2
    with Phase(nc, name) as ph:
        loaded, numbered, gathered, done, stored = (ph.sems2(n) for n in ("loaded", "numbered", "gathered", "done", "stored"))
        counts_read = ph.sems2("counts_read")
        chain, went_on = ph.sem("chain"), ph.sem("went_on")
        S, R, E = ph.sb2("S", [P, GT, SW]), ph.sb2("R", [P, GT, P]), ph.sb2("E", [P, GT, P + 1])
        number = ph.sb2("number", [P, GT], I32)
        inv, has = ph.sb2("inv", [P, GT]), ph.sb2("has", [P, GT])
        with nc.Block() as block:
            @block.sync
            def _(sp):
                for b in range(2):
                    sp.sem_inc(stored[b], 16)
                    sp.dma_start(S[b][:, :, :], group_rows(sums, b)).then_inc(loaded[b], 16)

                def store(i, b):
                    sp.wait_ge(done[b], i + 1)
                    sp.dma_start(group_rows(e_out, i * 2 + b), E[b][:, :, :]).then_inc(stored[b], 16)

                with nc.sync.Fori(0, steps - 1) as i:
                    for b in range(2):
                        sp.wait_ge(counts_read[b], i + 1)
                        sp.dma_start(S[b][:, :, :], group_rows(sums, i * 2 + 2 + b)).then_inc(loaded[b], 16)
                    for b in range(2):
                        store(i, b)
                for b in range(2):
                    store(steps - 1, b)
                for b in range(2):
                    sp.wait_ge(stored[b], 16 * (steps + 1))

            @block.vector
            def _(dve):
                v = nc.vector
                link = Chain(dve, chain)
                with v.Fori(0, steps) as i:
                    for b in range(2):
                        dve.wait_ge(loaded[b], i * 16 + 16)
                        v.tensor_scalar(number[b][:, :], S[b][:, :, P + 1], -1.0, 0.0, ALU.add, ALU.max)
                        v.tensor_scalar(has[b][:, :], S[b][:, :, P], 0.0, None, ALU.is_gt)
                        link(v.tensor_scalar(inv[b][:, :], S[b][:, :, P], 1.0, None, ALU.max))
                        link.tell(numbered[b])
                        link.tell(counts_read[b])
                        link(v.reciprocal(inv[b][:, :], inv[b][:, :]))
                        link(v.tensor_tensor(inv[b][:, :], inv[b][:, :], has[b][:, :], ALU.mult))
                    for b in range(2):
                        dve.wait_ge(gathered[b], i * 64 + 128)
                        dve.wait_ge(stored[b], i * 16 + 16)
                        v.tensor_copy(E[b][:, :, P], C.hw[:, ds(i * 2 + b, 1), :].rearrange("p o k -> p (o k)"))
                        for k in range(GT):
                            last = v.tensor_scalar(E[b][:, k, 0:P], R[b][:, k, :], inv[b][:, k:k + 1], None, ALU.mult)
                        link(last)
                        if affine:
                            link(v.tensor_mul(E[b][:, :, 0:P], E[b][:, :, 0:P], spread(C.bn_scale)))
                            for k in range(GT):
                                last = v.scalar_tensor_tensor(E[b][:, k, 0:P], C.bn_bias[:, :], has[b][:, k:k + 1],
                                                              E[b][:, k, 0:P], ALU.mult, ALU.add)
                            link(last)
                        link.tell(done[b])
                    link.restart()

            @block.gpsimd
            def _(pool):
                for b in range(2):
                    nc.gpsimd.dma_start(C.credit[b:b + 1, :], C.eps[0:1, :]).then_inc(gathered[b], 64)
                with nc.gpsimd.Fori(0, steps) as i:
                    for b in range(2):
                        pool_wait(pool, numbered[b], i + 1, went_on)
                        for k in range(GT):
                            gather(nc, R[b][:, k, :], row_sums, number[b][:, k:k + 1], gathered[b], NP)


def inverse_degree(link, v, d, one, inv):
    link(v.tensor_scalar(one, d, 0.0, None, ALU.is_gt))
    link(v.tensor_tensor(inv, d, one, ALU.mult))
    link(v.scalar_tensor_tensor(inv, one, -1.0, inv, ALU.mult, ALU.add))
    link(v.tensor_scalar(inv, inv, 1.0, None, ALU.add))
    link(v.reciprocal(inv, inv))
    link(v.tensor_tensor(inv, inv, one, ALU.mult))


def hyper_nodes1(nc, C, sums, g_out):
    with NodePhase(nc, C, "n3", 1, 1) as ph:
        S, = ph.ways_sb([P, GT, SW], "S")
        G, Q = ph.ways_sb([P, GT, P], "G", "Q")
        degree, one, inv = (ph.sb(n, [P, WAYS, GT]) for n in ("degree", "one", "inv_degree"))
        sum_ps, square_ps = ph.ps("sum_ps", [1, ROWS]), ph.ps("square_ps", [1, ROWS])
        wide_ps = ph.ps("wide_ps", [P, 2, P])
        part = ph.sb("part", [1, 2, ROWS])
        mean, second, var, row = ph.sb("mean", [1, P]), ph.sb("second", [1, P]), ph.sb("var", [1, P]), ph.sb("row", [1, 2, P])
        summed, squared = ph.ways_sem("summed", "squared")
        all_summed, var_ready, root_ready, row_ready, wide_ready = (ph.sem(n) for n in (
            "all_summed", "var_ready", "root_ready", "row_ready", "wide_ready"))
        with nc.Block() as block:
            ph.mover(block, lambda i, b, last: ((S[b][:, :, :], group_rows(sums, i * WAYS + b)),),
                     lambda i, b, last: ((group_rows(g_out, i * WAYS + b), G[b][:, :, :]),))

            @block.vector
            def _(dve):
                v = nc.vector
                link = Chain(dve, ph.chain)
                with v.Fori(0, NODE_STEPS) as i:
                    for b in range(WAYS):
                        dve.wait_ge(ph.loaded[b], ph.before_load(i))
                        last = v.tensor_copy(degree[:, b, :], S[b][:, :, P])
                    link(last)
                    inverse_degree(link, v, degree[:, :, :], one[:, :, :], inv[:, :, :])
                    for b in range(WAYS):
                        dve.wait_ge(ph.stored[b], ph.before_store(i))
                        dve.wait_ge(summed[b], i + 1)
                        for k in range(GT):
                            last = v.tensor_scalar(G[b][:, k, :], S[b][:, k, 0:P], inv[:, b, k:k + 1], None, ALU.mult)
                        link(last)
                        link.tell(ph.used[b])
                        link.tell(ph.done[b])
                    link.restart()
                dve.wait_ge(all_summed, 1)
                v.tensor_copy(part[:, 0, :], sum_ps[:, :])
                link(v.tensor_copy(part[:, 1, :], square_ps[:, :]))
                for j, to in enumerate((mean, second)):
                    link(v.tensor_add(part[:, j, 0:2 * P], part[:, j, 0:2 * P], part[:, j, 2 * P:4 * P]))
                    link(v.tensor_add(part[:, j, 0:P], part[:, j, 0:P], part[:, j, P:2 * P]))
                    link(v.tensor_scalar(to[:, :], part[:, j, 0:P], 1.0 / N, None, ALU.mult))
                link(v.tensor_mul(var[:, :], mean[:, :], mean[:, :]))
                link(v.tensor_sub(var[:, :], second[:, :], var[:, :]))
                link(v.tensor_scalar(var[:, :], var[:, :], 0.0, None, ALU.max))
                link.tell(var_ready)
                dve.wait_ge(root_ready, 1)
                link(v.reciprocal(var[:, :], var[:, :]))
                link(v.tensor_mul(row[:, 0, :], var[:, :], C.v["gamma"][0:1, :]))
                link(v.tensor_mul(mean[:, :], mean[:, :], row[:, 0, :]))
                link(v.tensor_sub(row[:, 1, :], C.v["beta"][0:1, :], mean[:, :]))
                link.tell(row_ready)
                dve.wait_ge(wide_ready, 1)
                v.tensor_copy(C.bn_scale[:, :], wide_ps[:, 0, :])
                link(v.tensor_copy(C.bn_bias[:, :], wide_ps[:, 1, :]))

            @block.scalar
            def _(act):
                with nc.scalar.Fori(0, NODE_STEPS) as i:
                    for b in range(WAYS):
                        act.wait_ge(ph.done[b], i + 1)
                        nc.scalar.activation(Q[b][:, :, :], G[b][:, :, :], ACT.Square).then_inc(squared[b], 1)
                act.wait_ge(var_ready, 1)
                nc.scalar.activation(var[:, :], var[:, :], ACT.Sqrt, bias=C.eps[0:1, :]).then_inc(root_ready, 1)

            @block.tensor
            def _(pe):
                for b in range(WAYS):
                    pe.sem_inc(summed[b], 1)
                z = C.zeros[:, 0:1]
                for o in (sum_ps, square_ps):
                    for k in range(GT):
                        nc.tensor.matmul(o[:, k * P:(k + 1) * P], z, C.zeros[:, :], start=(k == 0), stop=False,
                                         skip_group_check=True)
                with nc.tensor.Fori(0, NODE_STEPS) as i:
                    for b in range(WAYS):
                        pe.wait_ge(squared[b], i + 1)
                        nc.tensor.matmul(sum_ps[:, :], C.ones[:, 0:1], G[b][:, :, :].rearrange("p k d -> p (k d)"),
                                         start=False, stop=False, skip_group_check=True)
                        nc.tensor.matmul(square_ps[:, :], C.ones[:, 0:1], Q[b][:, :, :].rearrange("p k d -> p (k d)"),
                                         start=False, stop=False, skip_group_check=True).then_inc(summed[b], 1)
                for o in (sum_ps, square_ps):
                    last = nc.tensor.matmul(o[:, 0:P], z, C.zeros[:, :], start=False, stop=True, skip_group_check=True)
                last.then_inc(all_summed, 1)
                pe.wait_ge(row_ready, 1)
                nc.tensor.matmul(wide_ps[:, :, :].rearrange("p a d -> p (a d)"), C.ones[0:1, :],
                                 row[:, :, :].rearrange("p a d -> p (a d)"), start=True, stop=True).then_inc(wide_ready, 1)


def hyper_nodes2(nc, C, x, sums, x_out, h_out, score_out):
    with NodePhase(nc, C, "n4", 2, 3) as ph:
        X, X2, HT = ph.ways_sb([P, GT, P], "X", "X2", "HT")
        S, = ph.ways_sb([P, GT, SW], "S")
        H, = ph.ways_sb([P, GT, P + HEADS], "H")
        scores, = ph.ways_sb([P, GT, HEADS], "scores")
        degree, one, inv = (ph.sb(n, [P, WAYS, GT]) for n in ("degree", "one", "inv_degree"))
        tp, scores_ps = ph.ps2("tp", [P, GT, P]), [ph.ps(f"scores_ps{b}", [P, GT, 2 * HEADS]) for b in range(WAYS)]
        norm = Norm(nc, C, ph, 1)
        turned, moved, product, biased, ready, relued = ph.ways_sem("turned", "moved", "product", "biased", "ready", "relued")

        def score_bias(at):
            return C.score_b[:, at:at + HEADS].rearrange("p (o d) -> p o d", o=1).to_broadcast([P, GT, HEADS])

        with nc.Block() as block:
            ph.mover(block, lambda i, b, last: ((X[b][:, :, :], group_rows(x, i * WAYS + b)),
                                                (S[b][:, :, :], group_rows(sums, i * WAYS + b))),
                     lambda i, b, last: ((group_rows(x_out, i * WAYS + b), X2[b][:, :, :]),
                                         (group_rows(h_out, i * WAYS + b), H[b][:, :, :]),
                                         (group_rows(score_out, i * WAYS + b), scores[b][:, :, :])))

            @block.gpsimd
            def _(pool):
                link = Chain(pool, ph.chain_pool)
                with nc.gpsimd.Fori(0, NODE_STEPS) as i:
                    for b in range(WAYS):
                        pool_wait(pool, ph.loaded[b], ph.before_load(i), ph.went_on)
                        link(nc.gpsimd.tensor_add(X[b][:, :, :], X[b][:, :, :], spread(C.v["b2"])))
                        link.tell(biased[b])
                    link.restart()

            @block.vector
            def _(dve):
                v = nc.vector
                link = Chain(dve, ph.chain)
                with v.Fori(0, NODE_STEPS) as i:
                    for b in range(WAYS):
                        dve.wait_ge(ph.loaded[b], ph.before_load(i))
                        last = v.tensor_copy(degree[:, b, :], S[b][:, :, P])
                    link(last)
                    inverse_degree(link, v, degree[:, :, :], one[:, :, :], inv[:, :, :])
                    for b in range(WAYS):
                        dve.wait_ge(ph.stored[b], ph.before_store(i))
                        dve.wait_ge(biased[b], i + 1)
                        scale_rows(v, link, X2[b], lambda k: S[b][:, k, 0:P], inv[:, b, :], lambda k: X[b][:, k, :])
                        link.tell(ph.used[b])
                        norm.stats_dve(link, b, X2[b])
                        if b >= 1:
                            norm.inverse_dve(dve, link, i, b - 1, 0, bias=True)
                            link.tell(ready[b - 1])
                    norm.inverse_dve(dve, link, i, WAYS - 1, 0, bias=True)
                    link.tell(ready[WAYS - 1])
                    for b in range(WAYS):
                        dve.wait_ge(product[b], i + 1)
                        v.tensor_add(scores[b][:, :, :], scores_ps[b][:, :, 0:HEADS], score_bias(0))
                        link(v.tensor_add(H[b][:, :, P:P + HEADS], scores_ps[b][:, :, HEADS:2 * HEADS], score_bias(HEADS)))
                        link.tell(ph.done[b])
                    link.restart()

            @block.scalar
            def _(act):
                link = Chain(act, ph.chain_act)
                with nc.scalar.Fori(0, NODE_STEPS) as i:
                    for b in range(WAYS + 2):
                        if b < WAYS:
                            norm.root_act(act, i, b)
                        if 1 <= b <= WAYS:
                            act.wait_ge(ready[b - 1], i + 1)
                            link(norm.apply_act(b - 1, X2[b - 1], H[b - 1][:, :, 0:P], ACT.Relu))
                            link.tell(relued[b - 1])
                        if b >= 2:
                            act.wait_ge(turned[b - 2], i + 1)
                            link(nc.scalar.copy(HT[b - 2][:, :, :], tp[b % 2][:, :, :]))
                            link.tell(moved[b - 2])
                    link.restart()

            def score_rows(pe, i, b):
                pe.wait_ge(moved[b], i + 1)
                for k in range(GT):
                    last = nc.tensor.matmul(scores_ps[b][:, k, :], HT[b][:, k, :], C.score_w[:, :], start=True, stop=True)
                last.then_inc(product[b], 1)

            @block.tensor
            def _(pe):
                with nc.tensor.Fori(0, NODE_STEPS) as i:
                    for b in range(WAYS):
                        pe.wait_ge(relued[b], i + 1)
                        if b >= 2:
                            pe.wait_ge(moved[b - 2], i + 1)
                        for k in range(GT):
                            last = nc.tensor.transpose(tp[b % 2][:, k, :], H[b][:, k, 0:P], C.ident[:, :])
                        last.then_inc(turned[b], 1)
                        if b >= 1:
                            score_rows(pe, i, b - 1)
                    score_rows(pe, i, WAYS - 1)


def attention_nodes(nc, C, x, h, sums, x_out, h_out):
    with NodePhase(nc, C, "n5", 2, 2) as ph:
        X, X3, H, HT, A, T, Y, R, H3 = ph.ways_sb([P, GT, P], "X", "X3", "H", "HT", "A", "T", "Y", "R", "H3")
        S, = ph.ways_sb([P, GT, SW], "S")
        empty, = ph.ways_sb([P, GT, HEADS], "empty")
        tp, out_ps = ph.ps2("tp", [P, GT, P]), ph.ps2("out_ps", [P, GT, P])
        heads_ps = [ph.ps(f"heads_ps{k}", [P, HEADS, P]) for k in range(GT)]
        norm = Norm(nc, C, ph, 2)
        (turned, moved, product, empty_ready, based, summed, scaled, biased, relued, ready, xbiased, added) = ph.ways_sem(
            "turned", "moved", "product", "empty_ready", "based", "summed", "scaled", "biased", "relued", "ready", "xbiased", "added")
        fourth = ph.ways_sem("fourth")[0]
        heads_ready = [ph.sem(f"heads_ready{k}") for k in range(GT)]
        heads_used = [ph.sem(f"heads_used{k}") for k in range(GT)]
        heads_added = [ph.sem(f"heads_added{k}") for k in range(GT)]
        with nc.Block() as block:
            ph.mover(block, lambda i, b, last: ((S[b][:, :, :], group_rows(sums, i * WAYS + b)),
                                                (H[b][:, :, :], group_rows(h, i * WAYS + b, 0, P))),
                     lambda i, b, last: ((group_rows(x_out, i * WAYS + b), X3[b][:, :, :]),
                                         (group_rows(h_out, i * WAYS + b), H3[b][:, :, :])),
                     late=lambda i, b: ((X[b][:, :, :], group_rows(x, i * WAYS + b)),))

            def project_heads(pe, i, b):
                pe.wait_ge(moved[b], i * 2 + 1)
                for k in range(GT):
                    pe.wait_ge(heads_used[k], i * WAYS + b + 1)
                    nc.tensor.matmul(heads_ps[k][:, :, :].rearrange("p a d -> p (a d)"), HT[b][:, k, :],
                                     C.heads[:, :, :].rearrange("p a d -> p (a d)"), start=True,
                                     stop=True).then_inc(heads_ready[k], 1)

            def project_rows(pe, i, b):
                pe.wait_ge(moved[b], i * 2 + 2)
                if b >= 2:
                    pe.wait_ge(added[b - 2], i + 1)
                for k in range(GT):
                    last = nc.tensor.matmul(out_ps[b % 2][:, k, :], HT[b][:, k, :], C.t["V"][:, :], start=True, stop=True)
                last.then_inc(product[b], 1)

            @block.tensor
            def _(pe):
                for k in range(GT):
                    pe.sem_inc(heads_used[k], 1)
                with nc.tensor.Fori(0, NODE_STEPS) as i:
                    for b in range(WAYS):
                        pe.wait_ge(ph.loaded[b], ph.before_load(i))
                        if b >= 2:
                            pe.wait_ge(moved[b - 2], i * 2 + 1)
                        for k in range(GT):
                            last = nc.tensor.transpose(tp[b % 2][:, k, :], H[b][:, k, :], C.ident[:, :])
                        last.then_inc(turned[b], 1)
                    for b in range(WAYS):
                        project_heads(pe, i, b)
                    for b in range(WAYS):
                        pe.wait_ge(relued[b], i + 1)
                        if b >= 2:
                            pe.wait_ge(moved[b - 2], i * 2 + 2)
                        for k in range(GT):
                            last = nc.tensor.transpose(tp[b % 2][:, k, :], R[b][:, k, :], C.ident[:, :])
                        last.then_inc(turned[b], 1)
                        if b >= 1:
                            project_rows(pe, i, b - 1)
                    project_rows(pe, i, WAYS - 1)

            @block.gpsimd
            def _(pool):
                g = nc.gpsimd
                link = Chain(pool, ph.chain_pool)
                with g.Fori(0, NODE_STEPS) as i:
                    for b in range(WAYS):
                        pool_wait(pool, fourth[b], i + 1, ph.went_on)
                        link(g.tensor_add(T[b][:, :, :], T[b][:, :, :], spread(C.mean_b)))
                        link.tell(based[b])
                    for b in range(WAYS):
                        pool_wait(pool, scaled[b], i + 1, ph.went_on)
                        link(g.tensor_add(Y[b][:, :, :], Y[b][:, :, :], spread(C.v["ln_b"])))
                        link.tell(biased[b])
                    for b in range(WAYS):
                        pool_wait(pool, ph.late_loaded[b], i * 16 + 16, ph.went_on)
                        link(g.tensor_add(X[b][:, :, :], X[b][:, :, :], spread(C.v["Vb"])))
                        link.tell(xbiased[b])
                    link.restart()

            def add_fourth(dve, link, i, b):
                dve.wait_ge(based[b], i + 1)
                link(nc.vector.tensor_add(A[b][:, :, :], A[b][:, :, :], T[b][:, :, :]))
                link.tell(summed[b])

            @block.vector
            def _(dve):
                v = nc.vector
                link = Chain(dve, ph.chain)
                with v.Fori(0, NODE_STEPS) as i:
                    for b in range(WAYS):
                        dve.wait_ge(ph.loaded[b], ph.before_load(i))
                        link(v.tensor_scalar(empty[b][:, :, :], S[b][:, :, P:P + HEADS], -1.0 / HEADS, 1.0 / HEADS, ALU.mult, ALU.add))
                        link.tell(empty_ready[b])
                    for b in range(WAYS):
                        for pair in ((0, 1), (2, 3)):
                            for k in pair:
                                dve.wait_ge(heads_ready[k], i * WAYS + b + 1)
                            for a in range(HEADS - 1):
                                for k in pair:
                                    last = v.scalar_tensor_tensor(A[b][:, k, :], heads_ps[k][:, a, :], empty[b][:, k, a:a + 1],
                                                                  (A[b] if a else S[b])[:, k, 0:P], ALU.mult, ALU.add)
                                link(last)
                            for k in pair:
                                link.tell(heads_added[k])
                        link.tell(ph.used[b])
                        if b >= 1:
                            add_fourth(dve, link, i, b - 1)
                    add_fourth(dve, link, i, WAYS - 1)
                    for b in range(WAYS):
                        norm.inverse_dve(dve, link, i, b, 0, add=1e-6)
                        scale_rows(v, link, Y[b], lambda k: A[b][:, k, :], norm.inv[b], lambda k: C.v["ln_g"][:, :], ALU.mult)
                        link.tell(scaled[b])
                    for b in range(WAYS):
                        dve.wait_ge(product[b], i + 1)
                        dve.wait_ge(xbiased[b], i + 1)
                        dve.wait_ge(ph.stored[b], ph.before_store(i))
                        link(v.tensor_add(X3[b][:, :, :], X[b][:, :, :], out_ps[b % 2][:, :, :]))
                        link.tell(added[b])
                        norm.stats_dve(link, b, X3[b])
                        if b >= 1:
                            norm.inverse_dve(dve, link, i, b - 1, 1, bias=True)
                            link.tell(ready[b - 1])
                    norm.inverse_dve(dve, link, i, WAYS - 1, 1, bias=True)
                    link.tell(ready[WAYS - 1])
                    link.restart()

            def deviation(act, link, i, b):
                act.wait_ge(summed[b], i + 1)
                norm.squares_act(link, b, A[b], P - 1.0, eps=False)

            def move_back(act, link, i, b):
                act.wait_ge(turned[b], i * 2 + 2)
                link(nc.scalar.copy(HT[b][:, :, :], tp[b % 2][:, :, :]))
                link.tell(moved[b])

            def move_rows(act, link, i, ways):
                for b in ways:
                    act.wait_ge(turned[b], i * 2 + 1)
                    link(nc.scalar.copy(HT[b][:, :, :], tp[b % 2][:, :, :]))
                    link.tell(moved[b])

            def middle(act, link, i):
                for b in range(WAYS):
                    act.wait_ge(empty_ready[b], i + 1)
                    for k in range(GT):
                        act.wait_ge(heads_added[k], i * WAYS + b + 1)
                        link(nc.scalar.activation(T[b][:, k, :], heads_ps[k][:, HEADS - 1, :], ACT.Copy,
                                                  scale=empty[b][:, k, HEADS - 1:HEADS]))
                        link.tell(heads_used[k])
                    link.tell(fourth[b])
                    if b >= 2:
                        deviation(act, link, i, b - 2)
                for b in range(WAYS - 2, WAYS):
                    deviation(act, link, i, b)
                for b in range(WAYS):
                    act.wait_ge(biased[b], i + 1)
                    link(nc.scalar.activation(R[b][:, :, :], Y[b][:, :, :], ACT.Relu))
                    link.tell(relued[b])
                    if b >= 1:
                        move_back(act, link, i, b - 1)
                move_back(act, link, i, WAYS - 1)

            def finish(act, link, i):
                for b in range(WAYS + 1):
                    if b < WAYS:
                        norm.root_act(act, i, b)
                    if b >= 1:
                        act.wait_ge(ready[b - 1], i + 1)
                        link(norm.apply_act(b - 1, X3[b - 1], H3[b - 1], ACT.Relu))
                        link.tell(ph.done[b - 1])

            @block.scalar
            def _(act):
                link = Chain(act, ph.chain_act)
                move_rows(act, link, 0, range(WAYS))
                link.restart()
                with nc.scalar.Fori(0, NODE_STEPS - 1) as i:
                    middle(act, link, i)
                    move_rows(act, link, i + 1, (0, 1))
                    finish(act, link, i)
                    move_rows(act, link, i + 1, (2, 3))
                    link.restart()
                middle(act, link, NODE_STEPS - 1)
                finish(act, link, NODE_STEPS - 1)


def context_tables(nc, C, context, tables):
    full = CTX // P
    rest = CTX - full * P
    with Phase(nc, "ctxt") as ph:
        X = ph.sb("X", [P, CTILES, P])
        XC, XT = ph.sb("XC", [P, P]), ph.sb("XT", [P, P])
        T = ph.sb("T", [P, CTILES, 2, 2, P])
        stats, pair, work = ph.sb("stats", [P, 2, 6]), ph.sb("pair", [P, 2, 2]), ph.sb("work", [P, 2, P])
        mean_var, root = ph.sb("mean_var", [P, CTILES, 2, 2]), ph.sb("root", [P, CTILES, 2])
        tp, po = ph.ps("tp", [P, P]), ph.ps("po", [P, 2, 2, P])
        loaded, cleared, fetched, turned, moved, product, copied, var_ready, root_ready, done, stored, chain = (
            ph.sem(n) for n in ("loaded", "cleared", "fetched", "turned", "moved", "product", "copied", "var_ready",
                                "root_ready", "done", "stored", "chain"))
        with nc.Block() as block:
            @block.sync
            def _(sp):
                sp.wait_ge(cleared, 1)
                sp.dma_start(X[:, 0:full, :], context[0:full * P, :].rearrange("(t p) d -> p t d", p=P)).then_inc(loaded, 16)
                sp.dma_start(X[0:rest, full, :], context[full * P:CTX, :]).then_inc(loaded, 16)
                sp.wait_ge(done, 1)
                for k in range(2):
                    sp.dma_start(tables[k][0:full * P, :].rearrange("(t p) c -> p t c", p=P),
                                 T[:, 0:full, k, :, :].rearrange("p t a d -> p t (a d)")).then_inc(stored, 16)
                    sp.dma_start(tables[k][full * P:CTX, :], T[0:rest, full, k, :, :].rearrange("p a d -> p (a d)")).then_inc(stored, 16)
                sp.wait_ge(stored, 64)

            @block.tensor
            def _(pe):
                with nc.tensor.Fori(0, CTILES) as t:
                    pe.wait_ge(fetched, t + 1)
                    nc.tensor.transpose(tp[:, :], XC[:, :], C.ident[:, :]).then_inc(turned, 1)
                    pe.wait_ge(moved, t + 1)
                    nc.tensor.matmul(po[:, :, :, :].rearrange("p k a d -> p (k a d)"), XT[:, :],
                                     C.ctxw[:, :, :, :].rearrange("p k a d -> p (k a d)"), start=True, stop=True).then_inc(product, 1)

            @block.scalar
            def _(act):
                act.wait_ge(loaded, 32)
                with nc.scalar.Fori(0, CTILES) as t:
                    nc.scalar.copy(XC[:, :], X[:, ds(t, 1), :].rearrange("p o d -> p (o d)")).then_inc(fetched, 1)
                    act.wait_ge(turned, t + 1)
                    nc.scalar.copy(XT[:, :], tp[:, :]).then_inc(moved, 1)
                    act.wait_ge(product, t + 1)
                    nc.scalar.copy(T[:, ds(t, 1), :, :, :].rearrange("p o k a d -> p (o k a d)"),
                                   po[:, :, :, :].rearrange("p k a d -> p (k a d)")).then_inc(copied, 1)
                    act.wait_ge(copied, t + 1)
                act.wait_ge(var_ready, 1)
                nc.scalar.activation(root[:, :, :], mean_var[:, :, :, 1], ACT.Sqrt, bias=C.eps[:, :]).then_inc(root_ready, 1)

            @block.vector
            def _(dve):
                v = nc.vector
                link = Chain(dve, chain)
                link(v.memset(X[:, :, :], 0.0))
                link.tell(cleared)
                link.restart()

                def projected(t, k):
                    return T[:, ds(t, 1), k, 1, :].rearrange("p o d -> p (o d)")

                with v.Fori(0, CTILES) as t:
                    dve.wait_ge(copied, t + 1)
                    for k in range(2):
                        last = v.bn_stats(stats[:, k, :], projected(t, k))
                    link(last)
                    for k in range(2):
                        last = v.bn_aggr(pair[:, k, :], stats[:, k, :])
                    link(last)
                    link(v.tensor_copy(mean_var[:, ds(t, 1), :, :].rearrange("p o k c -> p (o k) c"), pair[:, :, :]))
                    link.restart()
                link.tell(var_ready)
                dve.wait_ge(root_ready, 1)
                link(v.reciprocal(root[:, :, :], root[:, :, :]))
                link.restart()
                with v.Fori(0, CTILES) as t:
                    link(v.tensor_copy(pair[:, :, 0], mean_var[:, ds(t, 1), :, 0].rearrange("p o k -> p (o k)")))
                    link(v.tensor_copy(pair[:, :, 1], root[:, ds(t, 1), :].rearrange("p o k -> p (o k)")))
                    for k in range(2):
                        link(v.tensor_scalar(work[:, k, :], projected(t, k), pair[:, k, 0:1], pair[:, k, 1:2],
                                             ALU.subtract, ALU.mult))
                        link(v.tensor_mul(work[:, k, :], work[:, k, :], C.v[f"gnc_w{k}"][:, :]))
                        link(v.tensor_add(projected(t, k), work[:, k, :], C.v[f"gnc_b{k}"][:, :]))
                    link.restart()
                link.tell(done)


def agent_nodes(nc, C, block_no, agents, sums, last_max, agents_out, x, out):
    final = out is not None
    with NodePhase(nc, C, f"n6{block_no}", 2, 1) as ph:
        A, AT, B, Y, Z, R, O = ph.ways_sb([P, GT, P], "A", "AT", "B", "Y", "Z", "R", "O")
        S, = ph.ways_sb([P, GT, SW], "S")
        X = ph.ways_sb([P, GT, P], "X")[0] if final else None
        low, fade, share = (ph.sb(n, [P, WAYS, GT]) for n in ("low", "fade", "share"))
        neg_max = ph.sb("neg_max", [P, 1])
        tp, out_ps = ph.ps2("tp", [P, GT, P]), [ph.ps(f"out_ps{b}", [P, GT, P]) for b in range(WAYS)]
        norm = Norm(nc, C, ph, 3)
        (turned, moved, product, faded, low_ready, summed, scaled, biased, ready, relued, abiased, b_used, whole) = ph.ways_sem(
            "turned", "moved", "product", "faded", "low_ready", "summed", "scaled", "biased", "ready", "relued", "abiased",
            "b_used", "whole")
        y_used, = ph.ways_sem("y_used")

        def w(name):
            return C.v[f"{name}{block_no}"]

        def loads(i, b, last):
            g = i * WAYS + b
            return (A[b][:, :, :], group_rows(agents, g)), (S[b][:, :, :], group_rows(sums, g))

        def stores(i, b, last):
            g = i * WAYS + b
            if not final:
                return ((group_rows(agents_out, g), O[b][:, :, :]),)
            if not last or b == 0:
                o = out[0:LASTG * ROWS, :].rearrange("(g p k) d -> p g k d", p=P, k=GT)
                return ((o[:, ds(g, 1), :, :].rearrange("p o k d -> p (o k) d"), O[b][:, :, :]),)
            if b == 1:
                return ((out[LASTG * ROWS:N, :].rearrange("(p k) d -> p k d", k=GT), O[b][0:LASTP, :, :]),)
            return ()

        with nc.Block() as block:
            ph.mover(block, loads, stores, peel_store=final,
                     late=(lambda i, b: ((X[b][:, :, :], group_rows(x, i * WAYS + b)),)) if final else None)

            @block.tensor
            def _(pe):
                def project(i, b, n, weight):
                    pe.wait_ge(moved[b], i * 2 + n + 1)
                    for k in range(GT):
                        last = nc.tensor.matmul(out_ps[b][:, k, :], AT[b][:, k, :], weight[:, :], start=True, stop=True)
                    last.then_inc(product[b], 1)

                for b in range(WAYS):
                    pe.sem_inc(whole[b], 1)
                with nc.tensor.Fori(0, NODE_STEPS) as i:
                    for b in range(WAYS):
                        pe.wait_ge(ph.loaded[b], ph.before_load(i))
                        if b >= 2:
                            pe.wait_ge(moved[b - 2], i * 2 + 1)
                        for k in range(GT):
                            last = nc.tensor.transpose(tp[b % 2][:, k, :], A[b][:, k, :], C.ident[:, :])
                        last.then_inc(turned[b], 1)
                        if b >= 1:
                            pe.wait_ge(whole[b - 1], i + 1)
                            project(i, b - 1, 0, C.t[f"Wa{block_no}"])
                    pe.wait_ge(whole[WAYS - 1], i + 1)
                    project(i, WAYS - 1, 0, C.t[f"Wa{block_no}"])
                    for b in range(WAYS):
                        pe.wait_ge(relued[b], i + 1)
                        if b >= 2:
                            pe.wait_ge(moved[b - 2], i * 2 + 2)
                        for k in range(GT):
                            last = nc.tensor.transpose(tp[b % 2][:, k, :], R[b][:, k, :], C.ident[:, :])
                        last.then_inc(turned[b], 1)
                        if b >= 1:
                            project(i, b - 1, 1, C.t[f"Wlin{block_no}"])
                    project(i, WAYS - 1, 1, C.t[f"Wlin{block_no}"])

            @block.gpsimd
            def _(pool):
                g = nc.gpsimd
                link = Chain(pool, ph.chain_pool)
                for b in range(WAYS):
                    pool.sem_inc(b_used[b], 1)
                with g.Fori(0, NODE_STEPS) as i:
                    for b in range(WAYS):
                        pool_wait(pool, ph.loaded[b], ph.before_load(i), ph.went_on)
                        pool_wait(pool, b_used[b], i + 1, ph.went_on)
                        link(g.tensor_add(B[b][:, :, :], A[b][:, :, :], spread(w("gnl_b"))))
                        link.tell(abiased[b])
                    for n, name in enumerate(("gna_b", "norm_b")):
                        for b in range(WAYS):
                            pool_wait(pool, scaled[b], i * 2 + n + 1, ph.went_on)
                            link(g.tensor_add(Z[b][:, :, :], Z[b][:, :, :], spread(w(name))))
                            link.tell(biased[b])
                    link.restart()

            def read_maxima(dve, link, i):
                v = nc.vector
                for b in range(WAYS):
                    dve.wait_ge(ph.loaded[b], ph.before_load(i))
                    link(v.tensor_scalar(low[:, b, :], S[b][:, :, P + 1], neg_max[:, :], 0.0, ALU.add, ALU.min))
                    link.tell(low_ready[b])

            def main_dve(dve, link, i):
                v = nc.vector
                for b in range(WAYS):
                    dve.wait_ge(faded[b], i + 1)
                    last = v.tensor_tensor(share[:, b, :], fade[:, b, :], S[b][:, :, P], ALU.mult)
                link(last)
                link(v.tensor_scalar(share[:, :, :], share[:, :, :], 1e-16, None, ALU.add))
                link(v.reciprocal(share[:, :, :], share[:, :, :]))
                link(v.tensor_tensor(share[:, :, :], share[:, :, :], fade[:, :, :], ALU.mult))
                for b in range(WAYS):
                    dve.wait_ge(product[b], i * 2 + 1)
                    if not final:
                        dve.wait_ge(y_used[b], i + 1)
                    scale_rows(v, link, Y[b], lambda k: S[b][:, k, 0:P], share[:, b, :], lambda k: out_ps[b][:, k, :])
                    link.tell(summed[b])
                    dve.wait_ge(abiased[b], i + 1)
                    link.tell(ph.used[b])
                for b in range(WAYS):
                    norm.inverse_dve(dve, link, i, b, 0)
                    scale_rows(v, link, Z[b], lambda k: Y[b][:, k, :], norm.inv[b], lambda k: w("gna_w")[:, :], ALU.mult)
                    link.tell(scaled[b])
                for b in range(WAYS):
                    dve.wait_ge(biased[b], i * 2 + 1)
                    norm.stats_dve(link, b, Z[b])
                for b in range(WAYS):
                    dve.wait_ge(norm.root_ready[b], i * 3 + 2)
                    link(v.reciprocal(norm.inv[b][:, :], norm.root[b][:, :]))
                    for k in range(GT):
                        last = v.tensor_scalar(Y[b][:, k, :], Z[b][:, k, :], norm.mean_var[b][:, k, 0:1],
                                               norm.inv[b][:, k:k + 1], ALU.subtract, ALU.mult)
                    link(last)
                    link(v.tensor_mul(Z[b][:, :, :], Y[b][:, :, :], spread(w("norm_w"))))
                    link.tell(scaled[b])

            def finish_dve(dve, link, i):
                v = nc.vector
                for b in range(WAYS):
                    norm.inverse_dve(dve, link, i, b, 2)
                    scale_rows(v, link, Y[b], lambda k: out_ps[b][:, k, :], norm.inv[b], lambda k: w("gnl_w")[:, :], ALU.mult)
                    link.tell(whole[b])
                    if final:
                        dve.wait_ge(ph.stored[b], ph.before_store(i))
                        dve.wait_ge(ph.late_loaded[b], i * 16 + 16)
                        link(v.tensor_add(Y[b][:, :, :], Y[b][:, :, :], B[b][:, :, :]))
                        link.tell(b_used[b])
                        link(v.scalar_tensor_tensor(O[b][:, :, :], Y[b][:, :, :], 0.0, X[b][:, :, :], ALU.max, ALU.add))
                        link.tell(ph.done[b])
                    else:
                        link(v.tensor_add(Y[b][:, :, :], Y[b][:, :, :], B[b][:, :, :]))
                        link.tell(b_used[b])
                        link.tell(ready[b])

            @block.vector
            def _(dve):
                link = Chain(dve, ph.chain)
                for b in range(WAYS):
                    dve.sem_inc(y_used[b], 1)
                link(nc.vector.tensor_scalar(neg_max[:, :], last_max[:, :], -1.0, None, ALU.mult))
                read_maxima(dve, link, 0)
                link.restart()
                with nc.vector.Fori(0, NODE_STEPS - 1) as i:
                    main_dve(dve, link, i)
                    read_maxima(dve, link, i + 1)
                    finish_dve(dve, link, i)
                    link.restart()
                main_dve(dve, link, NODE_STEPS - 1)
                finish_dve(dve, link, NODE_STEPS - 1)

            def move(act, link, i, b, n):
                act.wait_ge(turned[b], i * 2 + n + 1)
                link(nc.scalar.copy(AT[b][:, :, :], tp[b % 2][:, :, :]))
                link.tell(moved[b])

            def deviation(act, link, i, b):
                act.wait_ge(product[b], i * 2 + 2)
                norm.squares_act(link, b, out_ps[b], float(P))

            def start_act(act, link, i):
                for b in range(WAYS):
                    act.wait_ge(low_ready[b], i + 1)
                    link(nc.scalar.activation(fade[:, b, :], low[:, b, :], ACT.Exp))
                    link.tell(faded[b])
                for b in (0, 1):
                    move(act, link, i, b, 0)

            def start_rest_act(act, link, i):
                for b in (2, 3):
                    move(act, link, i, b, 0)

            def main_act(act, link, i):
                for b in range(WAYS):
                    act.wait_ge(summed[b], i + 1)
                    norm.squares_act(link, b, Y[b], float(P))
                for b in range(WAYS):
                    norm.root_act(act, i, b)
                for b in range(WAYS):
                    act.wait_ge(biased[b], i * 2 + 2)
                    link(nc.scalar.activation(R[b][:, :, :], Z[b][:, :, :], ACT.Relu))
                    link.tell(relued[b])
                    if b >= 1:
                        move(act, link, i, b - 1, 1)
                    if b >= 2:
                        deviation(act, link, i, b - 2)
                move(act, link, i, WAYS - 1, 1)
                for b in range(WAYS - 2, WAYS):
                    deviation(act, link, i, b)

            def finish_act(act, link, i):
                if final:
                    return
                for b in range(WAYS):
                    act.wait_ge(ready[b], i + 1)
                    act.wait_ge(ph.stored[b], ph.before_store(i))
                    link(nc.scalar.activation(O[b][:, :, :], Y[b][:, :, :], ACT.Relu))
                    link.tell(y_used[b])
                    link.tell(ph.done[b])

            @block.scalar
            def _(act):
                link = Chain(act, ph.chain_act)
                start_act(act, link, 0)
                start_rest_act(act, link, 0)
                link.restart()
                with nc.scalar.Fori(0, NODE_STEPS - 1) as i:
                    main_act(act, link, i)
                    start_act(act, link, i + 1)
                    finish_act(act, link, i)
                    start_rest_act(act, link, i + 1)
                    link.restart()
                main_act(act, link, NODE_STEPS - 1)
                finish_act(act, link, NODE_STEPS - 1)


def gnn_layers(nc, w, out):
    with ExitStack() as ctx:
        def dram(name, shape, dt=FP32):
            return nc.dram_tensor(name, shape, dt, kind="Internal").ap()

        C = make_consts(nc, ctx, w)
        C.bn_scale = ctx.enter_context(nc.sbuf_tensor("bn_scale", [P, P], FP32))
        C.bn_bias = ctx.enter_context(nc.sbuf_tensor("bn_bias", [P, P], FP32))
        last_max = ctx.enter_context(nc.sbuf_tensor("last_max", [P, 1], FP32))
        by_dst_sums, by_src_sums = dram("by_dst_sums", (NODE_ROWS, SW)), dram("by_src_sums", (NODE_ROWS, SW))
        digit_rows = dram("digit_rows", (NP,), BF16)
        h0, h1, g, x1, x2, x3, a0, a1 = (dram(n, (NODE_ROWS, P)) for n in ("h0", "h1", "g", "x1", "x2", "x3", "a0", "a1"))
        h2, src_scores = dram("h2", (NODE_ROWS, P + HEADS)), dram("src_scores", (NODE_ROWS, HEADS))
        hyper = dram("hyper", (HGROUPS * ROWS, P + 1))
        row_sums = dram("row_sums", (NP, P))
        ctx_tables = [dram(f"ctx_table{k}", (CTX, 2 * P)) for k in range(2)]

        orders = {name: Order(nc, ctx, name) for name in ("by_src", "by_dst")}
        with ExitStack() as sorting:
            A = sorting.enter_context(nc.sbuf_tensor("pairs", [P, TILES, 2], I32))
            for name, key, other, limit, sums in (("by_src", "src", "dst", HYPER, by_src_sums),
                                                  ("by_dst", "dst", "src", CTX, by_dst_sums)):
                once, twice = dram(f"{name}_once", (NP, 2), I32), dram(f"{name}_twice", (NP, 2), I32)
                load_edges(nc, A, w[key], w[other], name)
                sort_pass(nc, C, name + "_low", A, once, digit_rows, 0, zeroed=sums)
                reload_pairs(nc, A, once, name + "_reload")
                sort_pass(nc, C, name + "_high", A, twice, digit_rows, 8)
                describe_order(nc, C, A, twice, orders[name], limit)
        by_src, by_dst = orders["by_src"], orders["by_dst"]
        norm_input(nc, C, w["x"], h0)
        plain_pass(nc, C, "sage", by_dst, h0, P, Order.OTHER, C.wlr[:, 0, :], by_dst_sums)
        sage_nodes(nc, C, w["x"], h0, by_dst_sums, x1, h1)
        for step, (rows, weight) in enumerate(((h1, "W1"), (g, "W2"))):
            running_pass(nc, C, f"hyper_in{step}", by_dst, rows, Order.OTHER, row_sums)
            hyper_rows(nc, C, f"hyper_rows{step}", by_dst_sums, row_sums, hyper, affine=step == 1)
            plain_pass(nc, C, f"hyper_out{step}", by_src, hyper, P + 1, Order.CLAMPED, C.t[weight][:, :], by_src_sums)
            if step == 0:
                hyper_nodes1(nc, C, by_src_sums, g)
        hyper_nodes2(nc, C, x1, by_src_sums, x2, h2, src_scores)
        attention_pass(nc, C, by_src, h2, src_scores, by_src_sums)
        attention_nodes(nc, C, x2, h2, by_src_sums, x3, a0)
        context_tables(nc, C, w["L3_gnn_ctx"], ctx_tables)
        for k in range(2):
            agents = (a0, a1)[k]
            context_pass(nc, C, k, by_dst, ctx_tables[k], agents, by_dst_sums, last_max)
            agent_nodes(nc, C, k, agents, by_dst_sums, last_max, a1, x3, out if k == 1 else None)


_OUTS = [((50000, 128), "float32")]


def kernel(**inputs):
    import numpy as _np
    import concourse.bacc as _bacc
    from concourse import mybir as _mybir
    from concourse.bass_utils import run_bass_kernel_spmd as _run

    nc = _bacc.Bacc("TRN2", target_bir_lowering=False, num_devices=1)
    arrays, args = {}, {}
    for name, value in inputs.items():
        a = _np.ascontiguousarray(value)
        arrays[f"in_{name}_dram"] = a
        args[name] = nc.dram_tensor(f"in_{name}_dram", a.shape, _mybir.dt.from_np(a.dtype), kind="ExternalInput").ap()
    out = nc.dram_tensor("out_0_dram", _OUTS[0][0], _mybir.dt.float32, kind="ExternalOutput").ap()
    gnn_layers(nc, args, out)
    r = _run(nc, [arrays], core_ids=[0])
    return r.results[0]["out_0_dram"]
```
